# Optimizing a Trainium2 kernel written in Bass

```python
import numpy as np
import jax
import jax.numpy as jnp

def _softmax(x, axis=-1):
    return jax.nn.softmax(x, axis=axis)

def _gelu(x):
    return jax.nn.gelu(x, approximate=True)

def _silu(x):
    return jax.nn.silu(x)

def _sigmoid(x):
    return jax.nn.sigmoid(x)

def _layernorm(x, axis=-1, eps=1e-05):
    m = jnp.mean(x, axis=axis, keepdims=True)
    v = jnp.var(x, axis=axis, keepdims=True)
    return (x - m) / jnp.sqrt(v + eps)

def _scatter_add(tgt, idx, src, axis=0):
    return tgt.at[idx].add(src)

def _segment_sum(src, seg, n):
    return jax.ops.segment_sum(src, seg, n)
kernel_name = 'mk_decoder_preln_d1_seqx_r2_374a48'

def setup_inputs(seed: int=0):
    np.random.seed(seed)
    _w = jnp.asarray

    def _rec_inputs():
        import jax
        import jax.numpy as jnp
        _rk = jax.random.key(seed)
        x = -0.0003929 + 0.9999 * jax.random.normal(jax.random.fold_in(_rk, 1), (2, 2048, 512), jnp.float32)
        _lenS = 2048 - jax.random.randint(jax.random.fold_in(_rk, 7), (2,), 0, max(1, 2048 // 4) + 1, jnp.int32)
        _lenS2 = 77 - jax.random.randint(jax.random.fold_in(_rk, 8), (2,), 0, max(1, 77 // 4) + 1, jnp.int32)
        _ctx_768P = jax.random.normal(jax.random.fold_in(_rk, 11), (2, 16, 384), jnp.float32)
        _ctx_768c = jax.random.dirichlet(jax.random.fold_in(_rk, 511), 0.3 * jnp.ones((16,), jnp.float32), (2, 77))
        _ctx_768t = jnp.einsum('bsk,bkd->bsd', _ctx_768c, _ctx_768P)
        _ctx_768t = _ctx_768t * jax.lax.rsqrt(jnp.mean(jnp.square(_ctx_768t)) + 1e-12) * 0.953939
        ctx_768 = 2.09791e-05 + 1.00001 * (_ctx_768t + 0.3 * jax.random.normal(jax.random.fold_in(_rk, 611), (2, 77, 384), jnp.float32))
        return (x, ctx_768)
    x, ctx_768 = _rec_inputs()

    def _L0_attn_setup():
        import jax, jax.numpy as jnp
        import numpy as np
        DIM = 512
        HID = 768
        K = 4
        N, T = (4, 2048)

        def _mk_forget_base(h, a=0.001, b=0.1, lo=-4.323, hi=-9.0):
            x = np.log(np.expm1(np.linspace(a, b, h, dtype=np.float64)))
            x = (x - x.min()) / (x.max() - x.min())
            x = x * abs(hi - lo) + hi
            return jnp.asarray(x, dtype=jnp.float32)
        key = jax.random.key(seed)
        ks = jax.random.split(key, 6)
        x = jax.random.normal(ks[0], (N, T, DIM), jnp.float32)
        Wi = jax.random.normal(ks[1], (2 * HID, DIM), jnp.float32) * DIM ** (-0.5)
        conv_w = jax.random.normal(ks[2], (HID, 1, K), jnp.float32) * K ** (-0.5)
        conv_b = jax.random.normal(ks[3], (HID,), jnp.float32) * 0.01
        Wg = jax.random.normal(ks[4], (2 * HID, HID), jnp.float32) * HID ** (-0.5)
        bg = jnp.zeros((2 * HID,), jnp.float32)
        forget_base = _mk_forget_base(HID)
        Wo = jax.random.normal(ks[5], (DIM, HID), jnp.float32) * HID ** (-0.5)
        return {'x': x, 'Wi': Wi, 'conv_w': conv_w, 'conv_b': conv_b, 'Wg': Wg, 'bg': bg, 'forget_base': forget_base, 'Wo': Wo}
    _L0_attn_all = _L0_attn_setup()
    _L0_attn_in = {k: v for k, v in _L0_attn_all.items() if k in ('Wi', 'conv_w', 'conv_b', 'Wg', 'bg', 'forget_base', 'Wo')}
    del _L0_attn_all

    def _L0_xattn_setup():
        import jax, jax.numpy as jnp
        import numpy as np
        HEADS = 8
        DIM_HEAD = 64
        QUERY_DIM = 512
        CONTEXT_DIM = 384
        INNER = HEADS * DIM_HEAD
        key = jax.random.key(seed)
        ks = jax.random.split(key, 7)
        B, Sq, Skv = (4, 2048, 512)
        x = jax.random.normal(ks[0], (B, Sq, QUERY_DIM), dtype=jnp.float32)
        context = jax.random.normal(ks[1], (B, Skv, CONTEXT_DIM), dtype=jnp.float32)
        Wq = jax.random.normal(ks[2], (QUERY_DIM, INNER), dtype=jnp.float32) * QUERY_DIM ** (-0.5)
        Wk = jax.random.normal(ks[3], (CONTEXT_DIM, INNER), dtype=jnp.float32) * CONTEXT_DIM ** (-0.5)
        Wv = jax.random.normal(ks[4], (CONTEXT_DIM, INNER), dtype=jnp.float32) * CONTEXT_DIM ** (-0.5)
        Wo = jax.random.normal(ks[5], (INNER, QUERY_DIM), dtype=jnp.float32) * INNER ** (-0.5)
        bo = jax.random.normal(ks[6], (QUERY_DIM,), dtype=jnp.float32) * 0.01
        return {'x': x, 'context': context, 'Wq': Wq, 'Wk': Wk, 'Wv': Wv, 'Wo': Wo, 'bo': bo}
    _L0_xattn_all = _L0_xattn_setup()
    _L0_xattn_in = {k: v for k, v in _L0_xattn_all.items() if k in ('Wq', 'Wk', 'Wv', 'Wo', 'bo')}
    del _L0_xattn_all

    def _L0_ffn_setup():
        import jax, jax.numpy as jnp
        import numpy as np
        B, S, D, H, E = (8, 1024, 512, 2048, 16)
        key = jax.random.key(seed)
        ks = jax.random.split(key, 4)
        sd = 1.0 / np.sqrt(D).astype(np.float32)
        sh = 1.0 / np.sqrt(H).astype(np.float32)
        return {'x': jax.random.normal(ks[0], (B, S, D), jnp.float32), 'Wg': jax.random.normal(ks[1], (D, E), jnp.float32) * sd, 'bg': jnp.zeros((E,), jnp.float32), 'W1': jax.random.normal(ks[2], (E, D, H), jnp.float32) * sd, 'b1': jnp.zeros((E, H), jnp.float32), 'W2': jax.random.normal(ks[3], (E, H, D), jnp.float32) * sh, 'b2': jnp.zeros((E, D), jnp.float32)}
    _L0_ffn_all = _L0_ffn_setup()
    _L0_ffn_in = {k: v for k, v in _L0_ffn_all.items() if k in ('Wg', 'bg', 'W1', 'b1', 'W2', 'b2')}
    del _L0_ffn_all
    return {'x': x, 'ctx_768': ctx_768, 'L0_attn_Wi': _L0_attn_in['Wi'], 'L0_attn_conv_w': _L0_attn_in['conv_w'], 'L0_attn_conv_b': _L0_attn_in['conv_b'], 'L0_attn_Wg': _L0_attn_in['Wg'], 'L0_attn_bg': _L0_attn_in['bg'], 'L0_attn_forget_base': _L0_attn_in['forget_base'], 'L0_attn_Wo': _L0_attn_in['Wo'], 'L0_xattn_Wq': _L0_xattn_in['Wq'], 'L0_xattn_Wk': _L0_xattn_in['Wk'], 'L0_xattn_Wv': _L0_xattn_in['Wv'], 'L0_xattn_Wo': _L0_xattn_in['Wo'], 'L0_xattn_bo': _L0_xattn_in['bo'], 'L0_ffn_Wg': _L0_ffn_in['Wg'], 'L0_ffn_bg': _L0_ffn_in['bg'], 'L0_ffn_W1': _L0_ffn_in['W1'], 'L0_ffn_b1': _L0_ffn_in['b1'], 'L0_ffn_W2': _L0_ffn_in['W2'], 'L0_ffn_b2': _L0_ffn_in['b2']}

def reference(x, ctx_768, L0_attn_Wi, L0_attn_conv_w, L0_attn_conv_b, L0_attn_Wg, L0_attn_bg, L0_attn_forget_base, L0_attn_Wo, L0_xattn_Wq, L0_xattn_Wk, L0_xattn_Wv, L0_xattn_Wo, L0_xattn_bo, L0_ffn_Wg, L0_ffn_bg, L0_ffn_W1, L0_ffn_b1, L0_ffn_W2, L0_ffn_b2):
    import jax
    import jax.numpy as jnp

    def _L0_attn_ref(x, Wi, conv_w, conv_b, Wg, bg, forget_base, Wo):
        import jax, jax.numpy as jnp
        import numpy as np
        DIM = 512
        HID = 768
        K = 4
        N, T = (4, 2048)

        def _mk_forget_base(h, a=0.001, b=0.1, lo=-4.323, hi=-9.0):
            x = np.log(np.expm1(np.linspace(a, b, h, dtype=np.float64)))
            x = (x - x.min()) / (x.max() - x.min())
            x = x * abs(hi - lo) + hi
            return jnp.asarray(x, dtype=jnp.float32)
        gi = jnp.einsum('ntc,hc->nth', x, Wi)
        gate, u = jnp.split(gi, 2, axis=-1)
        u = jax.lax.conv_general_dilated(u.transpose(0, 2, 1), conv_w, window_strides=(1,), padding=[(K - 1, 0)], dimension_numbers=('NCH', 'OIH', 'NCH'), feature_group_count=HID) + conv_b[None, :, None]
        u = u.transpose(0, 2, 1)
        fg = jnp.einsum('nth,gh->ntg', u, Wg) + bg
        forget, inp = jnp.split(fg, 2, axis=-1)
        alpha = jnp.exp(-8.0 * jax.nn.softplus(forget_base) * jax.nn.sigmoid(forget))
        beta = jnp.sqrt(1.0 - alpha ** 2 + 1e-06)
        xt = beta * jax.nn.sigmoid(inp) * u

        def step(h, ax):
            a, xx = ax
            h = a * h + xx
            return (h, h)
        _, h = jax.lax.scan(step, jnp.zeros((x.shape[0], HID), x.dtype), (alpha.transpose(1, 0, 2), xt.transpose(1, 0, 2)))
        h = h.transpose(1, 0, 2)
        return jnp.einsum('nth,ch->ntc', jax.nn.gelu(gate, approximate=False) * h, Wo)

    def _L0_xattn_ref(x, context, Wq, Wk, Wv, Wo, bo):
        import jax, jax.numpy as jnp
        import numpy as np
        HEADS = 8
        DIM_HEAD = 64
        QUERY_DIM = 512
        CONTEXT_DIM = 384
        INNER = HEADS * DIM_HEAD
        B, Sq, _ = x.shape
        h, d = (HEADS, DIM_HEAD)
        scale = d ** (-0.5)
        q = (x @ Wq).reshape(B, Sq, h, d).transpose(0, 2, 1, 3)
        k = (context @ Wk).reshape(B, -1, h, d).transpose(0, 2, 1, 3)
        v = (context @ Wv).reshape(B, -1, h, d).transpose(0, 2, 1, 3)
        scores = jnp.einsum('bhid,bhjd->bhij', q, k) * scale
        attn = jax.nn.softmax(scores, axis=-1)
        out = jnp.einsum('bhij,bhjd->bhid', attn, v)
        out = out.transpose(0, 2, 1, 3).reshape(B, Sq, h * d)
        return out @ Wo + bo

    def _L0_ffn_ref(x, Wg, bg, W1, b1, W2, b2):
        import jax, jax.numpy as jnp
        import numpy as np
        B, S, D, H, E = (8, 1024, 512, 2048, 16)
        d = x.shape[-1]
        xf = x.reshape(-1, d)
        n_tok = xf.shape[0]
        n_exp = Wg.shape[1]
        cap = -(-n_tok // n_exp)
        score = jax.nn.softmax(xf @ Wg + bg, axis=-1)
        gate = jnp.max(score, axis=-1)
        idx = jnp.argmax(score, axis=-1)
        onehot = jax.nn.one_hot(idx, n_exp, dtype=jnp.int32)
        pos = jnp.sum((jnp.cumsum(onehot, axis=0) - 1) * onehot, axis=-1)
        keep = pos < cap
        safe_pos = jnp.where(keep, pos, cap - 1)
        buf = jnp.zeros((n_exp, cap, d), x.dtype).at[idx, safe_pos].add(jnp.where(keep[:, None], xf, 0.0))
        h = jax.nn.relu(jnp.einsum('ecd,edh->ech', buf, W1) + b1[:, None, :])
        y = jnp.einsum('ech,ehd->ecd', h, W2) + b2[:, None, :]
        out = y[idx, safe_pos] * gate[:, None]
        out = jnp.where(keep[:, None], out, 0.0)
        return out.reshape(x.shape)
    x = x + _L0_attn_ref(_layernorm(x, axis=-1), L0_attn_Wi, L0_attn_conv_w, L0_attn_conv_b, L0_attn_Wg, L0_attn_bg, L0_attn_forget_base, L0_attn_Wo)
    x = x + _L0_xattn_ref(_layernorm(x, axis=-1), ctx_768, L0_xattn_Wq, L0_xattn_Wk, L0_xattn_Wv, L0_xattn_Wo, L0_xattn_bo)
    x = x + _L0_ffn_ref(_layernorm(x, axis=-1), L0_ffn_Wg, L0_ffn_bg, L0_ffn_W1, L0_ffn_b1, L0_ffn_W2, L0_ffn_b2)
    return x

_drawn_inputs = setup_inputs


def setup_inputs(seed=0):
    import zlib

    import numpy as np

    out = dict(_drawn_inputs(seed))
    spreads = {'L0_attn_bg': (0.0, 0.361),
     'L0_ffn_bg': (0.0, 0.1),
     'L0_ffn_b1': (0.0, 0.657),
     'L0_ffn_b2': (0.0, 0.457)}
    factors = {'L0_xattn_bo': 3.633}
    for name, (base, spread) in spreads.items():
        noise = np.random.default_rng([zlib.crc32(name.encode()), seed]).standard_normal(out[name].shape)
        drawn = base * np.exp(spread * noise) if base else spread * noise
        out[name] = jnp.asarray(drawn.astype(out[name].dtype))
    for name, factor in factors.items():
        out[name] = (out[name] * factor).astype(out[name].dtype)
    return out
```

```python
from contextlib import ExitStack

import concourse.bass as bass
from concourse import mybir

F32 = mybir.dt.float32
F32R = mybir.dt.float32r
BF16 = mybir.dt.bfloat16
I32 = mybir.dt.int32
U32 = mybir.dt.uint32
ALU = mybir.AluOpType
ACT = mybir.ActivationFunctionType
AX = mybir.AxisListType

P = 128
BATCH, SEQ, D = 2, 2048, 512
TOK = BATCH * SEQ
HID, TAPS = 768, 4
DC, HC = D // P, HID // P
EPS = 1e-5

TB = 256
NBLK = TOK // TB
BLK_SEQ = SEQ // TB
TT = TB // P
RING = 4
USES = 4 * HC
GRP = 2

HEADS, DH, CTX, NKV = 8, 64, 384, 77
CC = CTX // P
HG = HEADS // 2
SC = HEADS * NKV
SCC = -(-(SC + 1) // P)
SCP = SCC * P
NTILE = TOK // P
TILE_SEQ = SEQ // P
SCALE = DH ** -0.5

NE, HE = 16, 2048
CAP = -(-TOK // NE)
SLOTS = NE * CAP
NQ = 4
QH = HE // NQ
QC = QH // P
ST = CAP // P


def split(mm, out, pairs, start=True, stop=True):
    n = len(pairs)
    for k, ((ah, al), (bh, bl)) in enumerate(pairs):
        mm(out, ah, bh, start=start and k == 0, stop=False)
        mm(out, ah, bl, start=False, stop=False)
        last = mm(out, al, bh, start=False, stop=stop and k == n - 1)
    return last


def wait_apart(eng, sem, value, passed):
    eng.wait_ge(sem, value)
    eng.sem_inc(passed, 1)


def constants(nc, sb, sem):
    c = {
        "ident": sb("ident", [P, P], F32), "tri": sb("tri", [P, P], BF16), "ones": sb("ones", [P, P], BF16),
        "iota16": sb("iota16", [P, NE], F32), "iotap": sb("iotap", [P, 1], F32),
        "mhalf": sb("mhalf", [P, TT], F32),
    }
    made = sem("constants_made")
    with nc.Block() as block:
        @block.gpsimd
        def _(pool):
            pool.memset(c["ident"][:, :], 0.0).then_inc(made, 1)
            pool.memset(c["tri"][:, :], 1.0).then_inc(made, 1)
            pool.memset(c["ones"][:, :], 1.0).then_inc(made, 1)
            pool.memset(c["mhalf"][:, :], -0.5).then_inc(made, 1)
            pool.wait_ge(made, 4)
            pool.affine_select(out=c["ident"][:, :], in_=c["ident"][:, :], compare_op=ALU.not_equal, fill=1.0,
                               base=0, pattern=[[-1, P]], channel_multiplier=1).then_inc(made, 1)
            pool.affine_select(out=c["tri"][:, :], in_=c["tri"][:, :], compare_op=ALU.is_gt, fill=0.0,
                               base=0, pattern=[[1, P]], channel_multiplier=-1).then_inc(made, 1)
            pool.iota(c["iota16"][:, :], pattern=[[1, NE]], base=0, channel_multiplier=0,
                      allow_small_or_imprecise_dtypes=True).then_inc(made, 1)
            pool.iota(c["iotap"][:, :], pattern=[[0, 1]], base=0, channel_multiplier=1,
                      allow_small_or_imprecise_dtypes=True).then_inc(made, 1)
            pool.wait_ge(made, 8)
    return c


def prepare_recurrence(nc, sem, stage, w, dram, small):
    landed = [sem("w_landed0"), sem("w_landed1")]
    hi_done, lo_done, small_landed = sem("w_hi_done"), sem("w_lo_done"), sem("small_landed")
    wo_landed = sem("wo_landed")
    sp_step, sp_exp = sem("softplus_step"), sem("softplus_exp")
    jobs = [(dram["Wi"], w["Wih"], w["Wil"], k) for k in range(DC)] + \
           [(dram["Wg"], w["Wgh"], w["Wgl"], k) for k in range(HC)]
    fb, cw = small["fb"], small["work"]
    with nc.Block() as block:
        @block.sync
        def _(sp):
            for name in ("fb", "conv_w", "conv_b", "bg"):
                sp.dma_start(small[name][:, :], dram[name]).then_inc(small_landed, 16)
            for n, (src, hi, lo, k) in enumerate(jobs):
                if n >= 2:
                    sp.wait_ge(lo_done, n - 1)
                sp.dma_start(stage[:, n % 2, :], src[:, k, :]).then_inc(landed[n % 2], 16)
            sp.dma_start(w["Wo"][:, :, :], dram["Wo"]).then_inc(wo_landed, 16)
            sp.wait_ge(wo_landed, 16)

        @block.scalar
        def _(act):
            act.wait_ge(small_landed, 64)
            act.activation(cw[:, 0, :], fb[:, :], ACT.Abs).then_inc(sp_exp, 1)
            act.wait_ge(sp_exp, 1)
            act.activation(cw[:, 1, :], cw[:, 0, :], ACT.Exp, scale=-1.0).then_inc(sp_exp, 1)
            for n, (src, hi, lo, k) in enumerate(jobs):
                act.wait_ge(landed[n % 2], 16 * (n // 2 + 1))
                act.activation(hi[:, k, :], stage[:, n % 2, :], ACT.Copy).then_inc(hi_done, 1)

        @block.vector
        def _(dve):
            for n, (src, hi, lo, k) in enumerate(jobs):
                dve.wait_ge(hi_done, n + 1)
                dve.tensor_tensor(lo[:, k, :], stage[:, n % 2, :], hi[:, k, :].bitcast(F32),
                                  ALU.subtract).then_inc(lo_done, 1)
            step = [0]

            def then(ins):
                step[0] += 1
                ins.then_inc(sp_step, 1)
                dve.wait_ge(sp_step, step[0])

            dve.wait_ge(sp_exp, 2)
            dve.wait_ge(small_landed, 64)
            e, s, s2, acc = cw[:, 1, :], cw[:, 2, :], cw[:, 3, :], cw[:, 4, :]
            then(dve.tensor_scalar(s, e, 2.0, None, ALU.add))
            then(dve.reciprocal(s, s))
            then(dve.tensor_tensor(s, s, e, ALU.mult))
            then(dve.tensor_tensor(s2, s, s, ALU.mult))
            then(dve.tensor_scalar(acc, s2, 1.0 / 19, 1.0 / 17, ALU.mult, ALU.add))
            for m in (15, 13, 11, 9, 7, 5, 3, 1):
                then(dve.tensor_tensor(acc, acc, s2, ALU.mult))
                then(dve.tensor_scalar(acc, acc, 1.0 / m, None, ALU.add))
            then(dve.tensor_tensor(acc, acc, s, ALU.mult))
            then(dve.tensor_scalar(s, fb[:, :], 0.0, None, ALU.max))
            then(dve.scalar_tensor_tensor(out=acc, in0=acc, scalar=2.0, in1=s, op0=ALU.mult, op1=ALU.add))
            then(dve.tensor_scalar(small["decay"][:, :], acc, -4.0, None, ALU.mult))
            then(dve.tensor_scalar(small["hbg"][:, :], small["bg"][:, :], 0.5, None, ALU.mult))
            then(dve.memset(small["one_eps"][:, :], 1.0 + 1e-6))


def recurrence(nc, sb, ps, sem, c, w, dram, small):
    ident = c["ident"]
    SLOT = 2 * GRP
    X, R, XN = (sb(n, [P, TT, D], F32) for n in ("X", "R", "XN"))
    XTh, XTl = sb("XTh", [P, DC, TB], F32R), sb("XTl", [P, DC, TB], F32R)
    HALO = TAPS - 1
    UR = sb("UR", [P, HC, TB + HALO], F32)
    U = sb("U", [P, HC, TB], F32)
    Uh, Ul = sb("Uh", [P, HC, TB], F32R), sb("Ul", [P, HC, TB], F32R)
    G, GH = sb("G", [P, HC, TB], F32), sb("GH", [P, HC, TB], F32)
    H = sb("H", [P, GRP, TB], F32)
    TI, AL, BE = (sb(n, [P, SLOT, TB], F32) for n in ("TI", "AL", "BE"))
    carry = sb("carry", [P, HC], F32)
    stats, mv = sb("stats", [P, TT, 6], F32), sb("mv", [P, TT, 2], F32)
    rstd = sb("rstd", [P, TT], F32)
    pT = ps("pT", [P, DC, TB])
    pM = ps("pM", [P, RING, 512])
    pO = ps("pO", [P, TT, 512])

    x_landed, r_landed, x1_stored = sem("x_landed"), sem("r_landed"), sem("x1_stored")
    ln_step, ln_pow, ln_done = sem("ln_step"), sem("ln_pow"), sem("ln_done")
    xT_done, xhi_done, xlo_done = sem("xT_done"), sem("xhi_done"), sem("xlo_done")
    mm_done, mm_free = sem("mm_done"), sem("mm_free")
    conv_step, u_done, halo_done = sem("conv_step"), sem("u_done"), sem("halo_done")
    act_gate, gate_step, h_done = sem("act_gate"), sem("gate_step"), sem("h_done")
    gh_done, wo_done, resid_done = sem("gh_done"), sem("wo_done"), sem("resid_done")
    reset, passed = sem("reset"), sem("passed")

    x_v = dram["x"].rearrange("(n t p) d -> n p t d", t=TT, p=P)
    x1_v = dram["x1"].rearrange("(n t p) d -> n p t d", t=TT, p=P)
    CW, CB, DEC, HBG = small["conv_w"], small["conv_b"], small["decay"], small["hbg"]
    NG = HC // GRP
    AG = 5 * GRP

    def segments(eng, body):
        body(0, True, False)
        with eng.Fori(1, BLK_SEQ) as i:
            body(i, False, False)
        for b in range(1, BATCH):
            if b > 1:
                with eng.Fori(b * BLK_SEQ, (b + 1) * BLK_SEQ - (b == BATCH - 1)) as i:
                    body(i, False, False)
        with eng.Fori(BLK_SEQ, NBLK - 1) as i:
            body(i, False, False)
        body(NBLK - 1, False, True)

    with nc.Block() as block:
        @block.sync
        def _(sp):
            sp.dma_start(X[:, :, :], x_v[0]).then_inc(x_landed, 16)

            def body(i, first, last):
                if not last:
                    sp.wait_ge(ln_done, i + 1)
                    sp.dma_start(X[:, :, :], x_v[bass.ds(i + 1, 1)].rearrange("o p t d -> p (o t) d")
                                 if not isinstance(i, int) else x_v[i + 1]).then_inc(x_landed, 16)
                if not first:
                    sp.wait_ge(resid_done, i)
                    sp.dma_start(x1_v[bass.ds(i - 1, 1)].rearrange("o p t d -> p (o t) d")
                                 if not isinstance(i, int) else x1_v[i - 1], R[:, :, :]).then_inc(x1_stored, 16)
                    sp.wait_ge(x1_stored, 16 * i)
                sp.dma_start(R[:, :, :], x_v[bass.ds(i, 1)].rearrange("o p t d -> p (o t) d")
                             if not isinstance(i, int) else x_v[i]).then_inc(r_landed, 16)

            segments(sp, body)
            sp.wait_ge(resid_done, NBLK)
            sp.dma_start(x1_v[NBLK - 1], R[:, :, :]).then_inc(x1_stored, 16)
            sp.wait_ge(x1_stored, 16 * NBLK)

        @block.gpsimd
        def _(pool):
            def inverse_deviation(i):
                pool.wait_ge(ln_step, 6 * i + 5)
                pool.tensor_tensor(rstd[:, :], mv[:, :, 1], c["mhalf"][:, :], ALU.pow).then_inc(ln_pow, 1)

            def body(i, first, last):
                if not last:
                    inverse_deviation(i + 1)
                for k in range(HC):
                    pool.wait_ge(h_done, HC * i + k + 1)
                    if k == 0 and not first:
                        pool.wait_ge(wo_done, i)
                    pool.tensor_tensor(GH[:, k, :], G[:, k, :], H[:, k % GRP, :], ALU.mult).then_inc(gh_done, 1)

            inverse_deviation(0)
            segments(pool, body)

        @block.scalar
        def _(act):
            def x_hi(i):
                act.wait_ge(xT_done, i + 1)
                act.activation(XTh[:, 0:2, :], pT[:, 0:2, :], ACT.Copy).then_inc(xhi_done, 1)
                act.activation(XTh[:, 2:4, :], pT[:, 2:4, :], ACT.Copy).then_inc(xhi_done, 1)

            def body(i, first, last):
                use = 0
                if not first:
                    act.wait_ge(halo_done, i)
                for k in range(HC):
                    act.wait_ge(mm_done, USES * i + use + 1)
                    act.activation(UR[:, k, HALO:], pM[:, use % RING, 0:TB], ACT.Copy).then_inc(mm_free, 1)
                    use += 1
                if not first:
                    act.wait_ge(gh_done, HC * i)
                for k in range(HC):
                    act.wait_ge(mm_done, USES * i + use + 1)
                    act.activation(G[:, k, :], pM[:, use % RING, 0:TB], ACT.Gelu).then_inc(mm_free, 1)
                    use += 1
                if not last:
                    x_hi(i + 1)
                for g in range(NG):
                    for k in range(g * GRP, (g + 1) * GRP):
                        if k >= SLOT:
                            act.wait_ge(h_done, HC * i + k - SLOT + 1)
                        elif k == 0 and not first:
                            act.wait_ge(h_done, HC * i)
                        act.wait_ge(mm_done, USES * i + use + 1)
                        act.activation(AL[:, k % SLOT, :], pM[:, use % RING, 0:TB], ACT.Tanh, bias=HBG[:, k:k + 1],
                                       scale=0.5).then_inc(mm_free, 1)
                        use += 1
                        act.wait_ge(mm_done, USES * i + use + 1)
                        act.activation(TI[:, k % SLOT, :], pM[:, use % RING, 0:TB], ACT.Tanh, bias=HBG[:, HC + k:HC + k + 1],
                                       scale=0.5).then_inc(mm_free, 1)
                        use += 1
                    for k in range(g * GRP, (g + 1) * GRP):
                        act.wait_ge(mm_free, USES * i + use - 1 - 2 * ((g + 1) * GRP - 1 - k))
                        act.activation(AL[:, k % SLOT, :], AL[:, k % SLOT, :], ACT.Exp, bias=DEC[:, k:k + 1],
                                       scale=DEC[:, k:k + 1]).then_inc(act_gate, 1)
                    for k in range(GRP):
                        act.wait_ge(act_gate, 3 * HC * i + 3 * GRP * g + k + 1)
                        act.activation(BE[:, (g * GRP + k) % SLOT, :], AL[:, (g * GRP + k) % SLOT, :], ACT.Square).then_inc(act_gate, 1)
                    for k in range(GRP):
                        act.wait_ge(act_gate, 3 * HC * i + 3 * GRP * g + GRP + k + 1)
                        act.activation(BE[:, (g * GRP + k) % SLOT, :], BE[:, (g * GRP + k) % SLOT, :], ACT.Sqrt,
                                       bias=small["one_eps"][:, 0:1], scale=-1.0).then_inc(act_gate, 1)

            x_hi(0)
            segments(act, body)

        @block.vector
        def _(dve):
            def norm(i):
                dve.wait_ge(x_landed, 16 * i + 16)
                for t in range(TT):
                    dve.bn_stats(stats[:, t, :], X[:, t, :]).then_inc(ln_step, 1)
                for t in range(TT):
                    wait_apart(dve, ln_step, 6 * i + t + 1, passed)
                    dve.bn_aggr(mv[:, t, :], stats[:, t, :]).then_inc(ln_step, 1)
                dve.wait_ge(ln_step, 6 * i + 2 * TT)
                dve.tensor_scalar(mv[:, :, 1], mv[:, :, 1], EPS, None, ALU.add).then_inc(ln_step, 2)
                dve.wait_ge(ln_pow, i + 1)
                if not (isinstance(i, int) and i == 0):
                    dve.wait_ge(xT_done, i)
                for t in range(TT):
                    ins = dve.tensor_scalar(XN[:, t, :], X[:, t, :], mv[:, t, 0:1], rstd[:, t:t + 1],
                                            ALU.subtract, ALU.mult)
                ins.then_inc(ln_done, 1)

            def x_lo(i):
                for b in range(2):
                    dve.wait_ge(xhi_done, 2 * i + b + 1)
                    dve.tensor_tensor(XTl[:, 2 * b:2 * b + 2, :], pT[:, 2 * b:2 * b + 2, :],
                                      XTh[:, 2 * b:2 * b + 2, :].bitcast(F32), ALU.subtract).then_inc(xlo_done, 1)

            def convolve(i, first):
                for k in range(HC):
                    dve.wait_ge(mm_free, USES * i + k + 1)
                    base = HC * (TAPS + 1) * i + (TAPS + 1) * k
                    dve.tensor_scalar(U[:, k, :], UR[:, k, 0:TB], CW[:, TAPS * k:TAPS * k + 1], CB[:, k:k + 1],
                                      ALU.mult, ALU.add).then_inc(conv_step, 1)
                    for j in range(1, TAPS):
                        dve.wait_ge(conv_step, base + j)
                        dve.scalar_tensor_tensor(out=U[:, k, :], in0=UR[:, k, j:j + TB],
                                                 scalar=CW[:, TAPS * k + j:TAPS * k + j + 1], in1=U[:, k, :],
                                                 op0=ALU.mult, op1=ALU.add).then_inc(conv_step, 1)
                    dve.wait_ge(conv_step, base + TAPS)
                    dve.tensor_copy(Uh[:, k, :], U[:, k, :]).then_inc(conv_step, 1)
                    dve.wait_ge(conv_step, base + TAPS + 1)
                    dve.tensor_tensor(Ul[:, k, :], U[:, k, :], Uh[:, k, :].bitcast(F32),
                                      ALU.subtract).then_inc(u_done, 1)
                dve.tensor_copy(UR[:, :, 0:HALO], UR[:, :, TB:TB + HALO]).then_inc(halo_done, 1)

            def gates(i):
                for k in range(HC):
                    g, r, q = k // GRP, k % GRP, k % SLOT
                    dve.wait_ge(act_gate, 3 * HC * i + 3 * GRP * g + 2 * GRP + r + 1)
                    base = 4 * HC * i + 4 * k
                    dve.scalar_tensor_tensor(out=TI[:, q, :], in0=TI[:, q, :], scalar=1.0, in1=U[:, k, :],
                                             op0=ALU.add, op1=ALU.mult).then_inc(gate_step, 1)
                    dve.wait_ge(gate_step, base + 1)
                    dve.scalar_tensor_tensor(out=TI[:, q, :], in0=TI[:, q, :], scalar=0.5, in1=BE[:, q, :],
                                             op0=ALU.mult, op1=ALU.mult).then_inc(gate_step, 1)
                    dve.wait_ge(gate_step, base + 2)
                    if k >= GRP:
                        dve.wait_ge(gh_done, HC * i + k - GRP + 1)
                    else:
                        dve.wait_ge(gh_done, HC * i)
                    dve.tensor_tensor_scan(H[:, r, :], AL[:, q, :], TI[:, q, :], carry[:, k:k + 1],
                                           ALU.mult, ALU.add).then_inc(h_done, 1)
                    dve.wait_ge(h_done, HC * i + k + 1)
                    dve.tensor_copy(carry[:, k:k + 1], H[:, r, TB - 1:TB]).then_inc(gate_step, 2)

            def residual(i):
                dve.wait_ge(wo_done, i + 1)
                dve.wait_ge(r_landed, 16 * i + 16)
                for t in range(TT):
                    ins = dve.tensor_tensor(R[:, t, :], pO[:, t, :], R[:, t, :], ALU.add)
                ins.then_inc(resid_done, 1)

            def fresh_sequence(n):
                dve.memset(UR[:, :, 0:HALO], 0.0).then_inc(reset, 1)
                dve.memset(carry[:, :], 0.0).then_inc(reset, 1)
                dve.wait_ge(reset, 2 * n)

            def body(i, first, last):
                convolve(i, first)
                if not first:
                    residual(i - 1)
                if not last:
                    norm(i + 1)
                    x_lo(i + 1)
                gates(i)

            fresh_sequence(1)
            norm(0)
            x_lo(0)
            body(0, True, False)
            with dve.Fori(1, BLK_SEQ) as i:
                body(i, False, False)
            dve.wait_ge(halo_done, BLK_SEQ)
            dve.wait_ge(gate_step, 4 * HC * BLK_SEQ)
            fresh_sequence(2)
            with dve.Fori(BLK_SEQ, NBLK - 1) as i:
                body(i, False, False)
            body(NBLK - 1, False, True)
            residual(NBLK - 1)

        @block.tensor
        def _(pe):
            def transposes(i):
                pe.wait_ge(ln_done, i + 1)
                if not (isinstance(i, int) and i == 0):
                    pe.wait_ge(xlo_done, 2 * i)
                for k in range(DC):
                    for t in range(TT):
                        mm = pe.transpose(pT[:, k, t * P:(t + 1) * P], XN[:, t, k * P:(k + 1) * P], ident[:, :])
                mm.then_inc(xT_done, 1)

            def product(out_use, i, pairs, offset=0, skip_free=False):
                if not skip_free:
                    pe.wait_ge(mm_free, USES * i + out_use + offset - RING + 1)
                split(pe.matmul, pM[:, out_use % RING, 0:TB], pairs).then_inc(mm_done, 1)

            def in_product(i, chunk, use, **kw):
                s = slice(chunk * P, (chunk + 1) * P)
                product(use, i, [((w["Wih"][:, k, s], w["Wil"][:, k, s]), (XTh[:, k, :], XTl[:, k, :]))
                                 for k in range(DC)], **kw)

            def u_products(i, first=False, offset=0):
                pe.wait_ge(xlo_done, 2 * (i + (1 if offset else 0)) + 2)
                for k in range(HC):
                    in_product(i, HC + k, k, offset=offset, skip_free=first and k < RING)

            def body(i, first, last):
                for k in range(HC):
                    in_product(i, k, HC + k)
                if not last:
                    transposes(i + 1)
                pe.wait_ge(u_done, HC * (i + 1))
                for k in range(HC):
                    for half in range(2):
                        s = slice((half * HC + k) * P, (half * HC + k + 1) * P)
                        product(2 * HC + 2 * k + half, i, [((w["Wgh"][:, m, s], w["Wgl"][:, m, s]),
                                                            (Uh[:, m, :], Ul[:, m, :])) for m in range(HC)])
                if not last:
                    u_products(i, offset=USES)
                pe.wait_ge(gh_done, HC * (i + 1))
                if not first:
                    pe.wait_ge(resid_done, i)
                for t in range(TT):
                    for k in range(HC):
                        mm = pe.matmul(pO[:, t, :], GH[:, k, t * P:(t + 1) * P], w["Wo"][:, k, :],
                                       start=(k == 0), stop=(k == HC - 1))
                mm.then_inc(wo_done, 1)

            transposes(0)
            u_products(0, first=True)
            segments(pe, body)


def prepare_attention(nc, sb, ps, sem, aw, dram):
    NJ = BATCH * NKV
    ctxT, Wk, Wv = sb("ctxT", [P, CC, NJ], F32), sb("Wk", [P, CC, D], F32), sb("Wv", [P, CC, D], F32)
    WqT, Wo = sb("WqT", [DH, HEADS, D], F32), sb("Wo2", [DH, HEADS, D], F32)
    KT, VT = sb("KT", [DH, HEADS, NJ], F32), sb("VT", [DH, HEADS, NJ], F32)
    VWs = sb("VWs", [NKV, 4, D], F32)
    stage = sb("VW_stage", [P, BATCH, SCC, D], F32)
    zero = sb("zero", [P, 4 * D], F32)
    pR = ps("pR", [P, 4, 512])
    in_landed, zeroed, pads_stored, slots_zeroed = (sem(n) for n in ("in_landed", "zeroed", "pads_stored", "slots_zeroed"))
    pe_done, evac, wk_hi, vw_stored = sem("pe_done"), sem("evac"), sem("wk_hi"), [sem(f"vw_stored{n}") for n in range(4)]
    back, vw_hi, vw_lo = [sem(f"vw_back{b}") for b in range(BATCH)], sem("vw_hi"), sem("vw_lo")
    NK, NS = 2 * HEADS, DC * HEADS
    NV = BATCH * HEADS
    vw = dram["vw"]

    with nc.Block() as block:
        @block.sync
        def _(sp):
            for t, n in ((ctxT, "ctxT"), (Wk, "Wk"), (Wv, "Wv"), (WqT, "WqT"), (Wo, "xWo")):
                sp.dma_start(t[:, :, :], dram[n]).then_inc(in_landed, 16)
            sp.wait_ge(zeroed, 1)
            pad = vw[:, SC + 1:SCP, :].rearrange("b r d -> r b d")
            sp.dma_start(pad, zero[0:SCP - SC - 1, 0:BATCH * D].rearrange("r (b d) -> r b d", b=BATCH)).then_inc(pads_stored, 16)
            for b in range(BATCH):
                sp.dma_start(vw[b, SC:SC + 1, :], dram["bo"]).then_inc(pads_stored, 16)
            for n in range(NV):
                b, h = n // HEADS, n % HEADS
                sp.wait_ge(evac, NK + NS + n + 1)
                sp.dma_start(vw[b, h * NKV:(h + 1) * NKV, :], VWs[:, n % 4, :]).then_inc(vw_stored[n % 4], 16)
                if h == HEADS - 1:
                    for r in range(4):
                        sp.wait_ge(vw_stored[r], 16 * ((n + 4 - r) // 4))
                    sp.wait_ge(pads_stored, 16 * (1 + BATCH))
                    sp.dma_start(stage[:, b, :, :], vw[b].rearrange("(c p) d -> p c d", p=P)).then_inc(back[b], 16)

        @block.gpsimd
        def _(pool):
            pool.memset(zero[:, :], 0.0).then_inc(zeroed, 1)
            pool.wait_ge(zeroed, 1)
            xs = dram["xs"][0:SLOTS, :].rearrange("(n p r) d -> n p (r d)", p=P, r=4)
            for n in range(SLOTS // P // 4):
                pool.dma_start(xs[n], zero[:, :]).then_inc(slots_zeroed, 16)
            pool.dma_start(dram["ys"][SLOTS:SLOTS + 1, :], zero[0:1, 0:D]).then_inc(slots_zeroed, 16)
            pool.wait_ge(slots_zeroed, 16 * (SLOTS // P // 4 + 1))

        @block.tensor
        def _(pe):
            pe.wait_ge(in_landed, 80)
            use = 0

            def begin():
                if use >= 4:
                    pe.wait_ge(evac, use - 3)

            for src in (Wk, Wv):
                for h in range(HEADS):
                    begin()
                    for k in range(CC):
                        mm = pe.matmul(pR[0:DH, use % 4, 0:NJ], src[:, k, h * DH:(h + 1) * DH], ctxT[:, k, :],
                                       start=(k == 0), stop=(k == CC - 1))
                    mm.then_inc(pe_done, 1)
                    use += 1
            for k in range(DC):
                for h in range(HEADS):
                    begin()
                    if k == 0:
                        pe.wait_ge(evac, h + 1)
                    pe.matmul(pR[:, use % 4, 0:NJ], WqT[:, h, k * P:(k + 1) * P], KT[:, h, :],
                              start=True, stop=True).then_inc(pe_done, 1)
                    use += 1
            for b in range(BATCH):
                for h in range(HEADS):
                    begin()
                    pe.matmul(pR[0:NKV, use % 4, :], VT[:, h, b * NKV:(b + 1) * NKV], Wo[:, h, :],
                              start=True, stop=True).then_inc(pe_done, 1)
                    use += 1

        @block.scalar
        def _(act):
            for n in range(NS):
                k, h = n // HEADS, n % HEADS
                act.wait_ge(pe_done, NK + n + 1)
                act.activation(aw["WKh"][:, :, k, h * NKV:(h + 1) * NKV],
                               pR[:, (NK + n) % 4, 0:NJ].rearrange("p (b j) -> p b j", b=BATCH), ACT.Copy).then_inc(wk_hi, 1)
            for b in range(BATCH):
                act.wait_ge(back[b], 16)
                act.activation(aw["VWh"][:, b, :, :], stage[:, b, :, :], ACT.Copy).then_inc(vw_hi, 1)

        @block.vector
        def _(dve):
            for n in range(NK):
                dve.wait_ge(pe_done, n + 1)
                dve.tensor_copy((KT if n < HEADS else VT)[:, n % HEADS, :], pR[0:DH, n % 4, 0:NJ]).then_inc(evac, 1)
            for n in range(NS):
                k, h = n // HEADS, n % HEADS
                js = slice(h * NKV, (h + 1) * NKV)
                dve.wait_ge(wk_hi, n + 1)
                dve.tensor_tensor(aw["WKl"][:, :, k, js], pR[:, (NK + n) % 4, 0:NJ].rearrange("p (b j) -> p b j", b=BATCH),
                                  aw["WKh"][:, :, k, js].bitcast(F32), ALU.subtract).then_inc(evac, 1)
            for n in range(NV):
                dve.wait_ge(pe_done, NK + NS + n + 1)
                if n >= 4:
                    dve.wait_ge(vw_stored[n % 4], 16 * (n // 4))
                dve.tensor_copy(VWs[:, n % 4, :], pR[0:NKV, (NK + NS + n) % 4, :]).then_inc(evac, 1)
            for b in range(BATCH):
                dve.wait_ge(vw_hi, b + 1)
                dve.tensor_tensor(aw["VWl"][:, b, :, :], stage[:, b, :, :], aw["VWh"][:, b, :, :].bitcast(F32),
                                  ALU.subtract).then_inc(vw_lo, 1)


def attention(nc, sb, ps, sem, c, aw, dram, route):
    ident = c["ident"]
    XA, XN, R, X2, X3 = (sb(n, [P, D], F32) for n in ("XA", "XN1", "R1", "X2", "X3"))
    XTh, XTl = sb("X1Th", [P, DC, P], F32R), sb("X1Tl", [P, DC, P], F32R)
    X3T = sb("X3T", [P, DC, P], F32)
    E = sb("E", [P, SCP], F32)
    PTh, PTl = sb("PTh", [P, SCC, P], F32R), sb("PTl", [P, SCC, P], F32R)
    mx, den = sb("mx", [P, HEADS], F32), sb("den", [P, HEADS], F32)
    st1, mv1, rs1 = sb("st1", [P, 6], F32), sb("mv1", [P, 2], F32), sb("rs1", [P, 1], F32)
    st3, mv3, rs3 = sb("st3", [P, 6], F32), sb("mv3", [P, 2], F32), sb("rs3", [P, 1], F32)
    Wg, bg = sb("Wgate", [P, DC, NE], F32), sb("bgate", [P, NE], F32)
    lg, sco, ohp = sb("lg", [P, NE], F32), sb("sco", [P, NE], F32), sb("ohp", [P, NE], F32)
    oh, seen = sb("oh", [P, NE], BF16), sb("seen", [P, NE], BF16)
    mx8, ix8 = sb("mx8", [P, 8], F32), sb("ix8", [P, 8], U32)
    col = {n: sb("col_" + n, [P, 1], F32) for n in
           ("lmax", "sum", "rsum", "expert", "pos", "keep", "slot", "away", "spill", "far", "sidx")}
    SI = sb("SI", [P, 1], U32)
    pT, pS = ps("pT1", [P, DC, P]), ps("pS", [P, 2, 512])
    pP, pY = ps("pP", [P, 2, 4, P]), ps("pY", [P, D])
    pT3, pL = ps("pT3", [P, DC, P]), ps("pL", [P, 512])

    xa_landed, r_landed, x2_stored, g_landed = (sem(n) for n in ("xa_landed", "r1_landed", "x2_stored", "g_landed"))
    ln1_step, ln1_pow, ln1_done = sem("ln1_step"), sem("ln1_pow"), sem("ln1_done")
    ln3_step, ln3_pow, ln3_done = sem("ln3_step"), sem("ln3_pow"), sem("ln3_done")
    xT_done, xhi_done, xlo_done, score_done = (sem(n) for n in ("x1T_done", "x1hi_done", "x1lo_done", "score_done"))
    max_done, sub_done, exp_done, soft_step, prob_done = (sem(n) for n in ("max_done", "sub_done", "exp_done", "soft_step", "prob_done"))
    pt_done, phi_done, plo_done, y_done, x2_done = (sem(n) for n in ("pt_done", "phi_done", "plo_done", "y_done", "x2_done"))
    x3T_done, x3T_copied, logit_done, rexp_done, count_done = (sem(n) for n in ("x3T_done", "x3T_copied", "logit_done", "rexp_done", "count_done"))
    passed, pool_passed = sem("passed"), sem("pool_passed")
    rt, scattered, init = sem("route_step"), sem("scattered"), sem("init")
    RT1, RT = 9, 20

    x1_v = dram["x1"].rearrange("(n p) d -> n p d", p=P)
    x2_v = dram["x2"].rearrange("(n p) d -> n p d", p=P)

    def tile(v, t):
        return v[t] if isinstance(t, int) else v[bass.ds(t, 1)].rearrange("o p d -> p (o d)")

    def is0(t):
        return isinstance(t, int) and t == 0

    def segments(eng, body):
        body(0, 0, 0)
        for b in range(BATCH):
            with eng.Fori(max(b * TILE_SEQ, 1), (b + 1) * TILE_SEQ - 1) as t:
                body(t, b, b)
            t = (b + 1) * TILE_SEQ - 1
            body(t, b, b + 1 if b + 1 < BATCH else None)

    with nc.Block() as block:
        @block.sync
        def _(sp):
            sp.dma_start(Wg[:, :, :], dram["Wgate"]).then_inc(g_landed, 16)
            sp.dma_start(bg[:, :], dram["bgate"].partition_broadcast(P)).then_inc(g_landed, 16)
            sp.dma_start(XA[:, :], x1_v[0]).then_inc(xa_landed, 16)

            def body(t, b, nb):
                if nb is not None:
                    sp.wait_ge(ln1_done, t + 1)
                    sp.dma_start(XA[:, :], tile(x1_v, t + 1)).then_inc(xa_landed, 16)
                if not is0(t):
                    sp.wait_ge(x2_done, t)
                sp.dma_start(R[:, :], tile(x1_v, t)).then_inc(r_landed, 16)
                if not is0(t):
                    sp.dma_start(tile(x2_v, t - 1), X2[:, :]).then_inc(x2_stored, 16)

            segments(sp, body)
            sp.wait_ge(x2_done, NTILE)
            sp.dma_start(x2_v[NTILE - 1], X2[:, :]).then_inc(x2_stored, 16)
            sp.wait_ge(x2_stored, 16 * NTILE)

        @block.gpsimd
        def _(pool):
            half = c["mhalf"][:, 0:1]

            def pow1(t):
                pool.wait_ge(ln1_step, 3 * t + 3)
                pool.tensor_tensor(rs1[:, :], mv1[:, 1:2], half, ALU.pow).then_inc(ln1_pow, 1)

            def pow3(t):
                pool.wait_ge(ln3_step, 3 * t + 3)
                pool.tensor_tensor(rs3[:, :], mv3[:, 1:2], half, ALU.pow).then_inc(ln3_pow, 1)

            def scatter(t):
                pool.wait_ge(rt, RT * t + RT)
                wait_apart(pool, ln3_done, t + 1, pool_passed)
                pool.indirect_dma_start(out=dram["xs"], out_offset=bass.IndirectOffsetOnAxis(SI[:, 0:1], 0),
                                        in_=X3[:, :], in_offset=None).then_inc(scattered, 16)

            def body(t, b, nb):
                if nb is not None:
                    pow1(t + 1)
                if not is0(t):
                    pow3(t - 1)
                    scatter(t - 1)

            pool.memset(seen[:, :], 0.0).then_inc(init, 1)
            pool.memset(E[:, SC:SC + 1], 1.0).then_inc(init, 1)
            pool.memset(E[:, SC + 1:SCP], 0.0).then_inc(init, 1)
            pool.tensor_scalar(col["spill"][:, :], c["iotap"][:, :], 1.0, float(SLOTS + 1), ALU.mult, ALU.add).then_inc(init, 1)
            pow1(0)
            segments(pool, body)
            pow3(NTILE - 1)
            scatter(NTILE - 1)
            pool.wait_ge(scattered, 16 * NTILE)

        @block.scalar
        def _(act):
            def x_hi(t):
                act.wait_ge(xT_done, t + 1)
                act.activation(XTh[:, :, :], pT[:, :, :], ACT.Copy).then_inc(xhi_done, 1)

            def x3_copy(t):
                act.wait_ge(x3T_done, t + 1)
                if not is0(t):
                    act.wait_ge(logit_done, t)
                act.activation(X3T[:, :, :], pT3[:, :, :], ACT.Copy).then_inc(x3T_copied, 1)

            def route_exp(t):
                act.wait_ge(rt, RT * t + 3)
                act.activation(sco[:, :], lg[:, :], ACT.Exp, accum_out=col["sum"][:, :]).then_inc(rexp_done, 1)

            def body(t, b, nb):
                act.wait_ge(sub_done, t + 1)
                act.activation(E[:, 0:SC], E[:, 0:SC], ACT.Exp, scale=SCALE).then_inc(exp_done, 1)
                act.wait_ge(pt_done, t + 1)
                if not is0(t):
                    act.wait_ge(y_done, t)
                act.activation(PTh[:, 0:4, :], pP[:, 0, :, :], ACT.Copy).then_inc(phi_done, 1)
                act.activation(PTh[:, 4:SCC, :], pP[:, 1, 0:SCC - 4, :], ACT.Copy).then_inc(phi_done, 1)
                if not is0(t):
                    x3_copy(t - 1)
                if nb is not None:
                    x_hi(t + 1)
                if not is0(t):
                    route_exp(t - 1)

            x_hi(0)
            segments(act, body)
            x3_copy(NTILE - 1)
            route_exp(NTILE - 1)

        @block.vector
        def _(dve):
            s_v = pS[:, :, 0:HG * NKV].rearrange("p g (h j) -> p g h j", h=HG)
            e_v = E[:, 0:SC].rearrange("p (g h j) -> p g h j", g=2, h=HG)
            e_h = E[:, 0:SC].rearrange("p (h j) -> p h j", h=HEADS)
            mx_v = mx[:, :].rearrange("p (g h) -> p g h", g=2)

            def stats(src, landed, lv, st, mv, step, t):
                dve.wait_ge(landed, lv)
                dve.bn_stats(st[:, :], src[:, :]).then_inc(step, 1)
                wait_apart(dve, step, 3 * t + 1, passed)
                dve.bn_aggr(mv[:, :], st[:, :]).then_inc(step, 1)
                dve.wait_ge(step, 3 * t + 2)
                dve.tensor_scalar(mv[:, 1:2], mv[:, 1:2], EPS, None, ALU.add).then_inc(step, 1)

            def norm1(t):
                dve.wait_ge(ln1_pow, t + 1)
                if not is0(t):
                    dve.wait_ge(xT_done, t)
                dve.tensor_scalar(XN[:, :], XA[:, :], mv1[:, 0:1], rs1[:, 0:1], ALU.subtract, ALU.mult).then_inc(ln1_done, 1)

            def norm3(t):
                dve.wait_ge(ln3_pow, t + 1)
                if not is0(t):
                    dve.wait_ge(scattered, 16 * t)
                dve.tensor_scalar(X3[:, :], X2[:, :], mv3[:, 0:1], rs3[:, 0:1], ALU.subtract, ALU.mult).then_inc(ln3_done, 1)

            def x_lo(t):
                dve.wait_ge(xhi_done, t + 1)
                dve.tensor_tensor(XTl[:, :, :], pT[:, :, :], XTh[:, :, :].bitcast(F32), ALU.subtract).then_inc(xlo_done, 1)

            def soft_begin(t):
                dve.wait_ge(score_done, t + 1)
                dve.tensor_reduce(mx_v, s_v, AX.X, ALU.max).then_inc(max_done, 1)
                dve.wait_ge(max_done, t + 1)
                if not is0(t):
                    dve.wait_ge(pt_done, t)
                dve.tensor_tensor(e_v, s_v, mx_v.unsqueeze(3).to_broadcast([P, 2, HG, NKV]), ALU.subtract).then_inc(sub_done, 1)

            def soft_end(t):
                dve.wait_ge(exp_done, t + 1)
                dve.tensor_reduce(den[:, :], e_h, AX.X, ALU.add).then_inc(soft_step, 1)
                dve.wait_ge(soft_step, 2 * t + 1)
                dve.reciprocal(den[:, :], den[:, :]).then_inc(soft_step, 1)
                dve.wait_ge(soft_step, 2 * t + 2)
                dve.tensor_tensor(e_h, e_h, den[:, :].unsqueeze(2).to_broadcast([P, HEADS, NKV]), ALU.mult).then_inc(prob_done, 1)

            def p_lo(t):
                dve.wait_ge(phi_done, 2 * t + 1)
                dve.tensor_tensor(PTl[:, 0:4, :], pP[:, 0, :, :], PTh[:, 0:4, :].bitcast(F32), ALU.subtract).then_inc(plo_done, 1)
                dve.wait_ge(phi_done, 2 * t + 2)
                dve.tensor_tensor(PTl[:, 4:SCC, :], pP[:, 1, 0:SCC - 4, :], PTh[:, 4:SCC, :].bitcast(F32), ALU.subtract).then_inc(plo_done, 1)

            def output(t):
                dve.wait_ge(y_done, t + 1)
                dve.wait_ge(r_landed, 16 * t + 16)
                if not is0(t):
                    dve.wait_ge(x2_stored, 16 * t)
                dve.tensor_tensor(X2[:, :], pY[:, :], R[:, :], ALU.add).then_inc(x2_done, 1)

            def route_expert(t):
                def step(k, ins, apart=False):
                    ins.then_inc(rt, 1)
                    if apart:
                        wait_apart(dve, rt, RT * t + k, passed)
                    else:
                        dve.wait_ge(rt, RT * t + k)
                dve.wait_ge(logit_done, t + 1)
                step(1, dve.tensor_tensor(lg[:, :], pL[:, 0:NE], bg[:, :], ALU.add))
                step(2, dve.tensor_reduce(col["lmax"][:, :], lg[:, :], AX.X, ALU.max))
                step(3, dve.tensor_scalar(lg[:, :], lg[:, :], col["lmax"][:, 0:1], None, ALU.subtract))
                dve.wait_ge(rexp_done, t + 1)
                step(4, dve.reciprocal(col["rsum"][:, :], col["sum"][:, :]))
                step(5, dve.tensor_scalar(sco[:, :], sco[:, :], col["rsum"][:, 0:1], None, ALU.mult), apart=True)
                step(6, dve.max(mx8[:, :], sco[:, :]), apart=True)
                step(7, dve.max_index(ix8[:, :], mx8[:, :], sco[:, :]))
                step(8, dve.tensor_copy(col["expert"][:, :], ix8[:, 0:1]))
                step(9, dve.tensor_scalar(oh[:, :], c["iota16"][:, :], col["expert"][:, 0:1], None, ALU.is_equal))

            def route_slot(t):
                def step(k, ins):
                    ins.then_inc(rt, 1)
                    dve.wait_ge(rt, RT * t + k)
                x = {n: v[:, :] for n, v in col.items()}
                dve.wait_ge(count_done, t + 1)
                step(10, dve.tensor_tensor_reduce(ohp[:, :], pL[:, 64:64 + NE], oh[:, :], 1.0, 0.0, ALU.mult, ALU.add, x["pos"]))
                step(11, dve.tensor_tensor(seen[:, :], seen[:, :], oh[:, :], ALU.add))
                step(12, dve.tensor_scalar(x["keep"], x["pos"], float(CAP), None, ALU.is_lt))
                step(13, dve.scalar_tensor_tensor(out=x["slot"], in0=x["expert"], scalar=float(CAP), in1=x["pos"],
                                                  op0=ALU.mult, op1=ALU.add))
                step(14, dve.tensor_tensor(x["away"], x["slot"], x["spill"], ALU.subtract))
                step(15, dve.scalar_tensor_tensor(out=x["sidx"], in0=x["away"], scalar=x["keep"], in1=x["spill"],
                                                  op0=ALU.mult, op1=ALU.add))
                step(16, dve.tensor_scalar(x["far"], x["slot"], float(SLOTS), x["keep"], ALU.subtract, ALU.mult))
                step(17, dve.tensor_scalar(route["place"][:, bass.ds(t, 1)], x["far"], float(SLOTS), None, ALU.add))
                step(18, dve.tensor_tensor(route["gate"][:, bass.ds(t, 1)], mx8[:, 0:1], x["keep"], ALU.mult))
                if not is0(t):
                    dve.wait_ge(scattered, 16 * t)
                step(19, dve.tensor_scalar(x["spill"], x["spill"], float(P), None, ALU.add))
                step(20, dve.tensor_copy(SI[:, :], x["sidx"]))

            def body(t, b, nb):
                soft_begin(t)
                if nb is not None:
                    stats(XA, xa_landed, 16 * (t + 1) + 16, st1, mv1, ln1_step, t + 1)
                if not is0(t):
                    stats(X2, x2_done, t, st3, mv3, ln3_step, t - 1)
                soft_end(t)
                if not is0(t):
                    norm3(t - 1)
                if nb is not None:
                    norm1(t + 1)
                p_lo(t)
                if nb is not None:
                    x_lo(t + 1)
                if not is0(t):
                    route_expert(t - 1)
                output(t)
                if not is0(t):
                    route_slot(t - 1)

            dve.wait_ge(init, 4)
            dve.wait_ge(g_landed, 32)
            stats(XA, xa_landed, 16, st1, mv1, ln1_step, 0)
            norm1(0)
            x_lo(0)
            segments(dve, body)
            stats(X2, x2_done, NTILE, st3, mv3, ln3_step, NTILE - 1)
            norm3(NTILE - 1)
            route_expert(NTILE - 1)
            route_slot(NTILE - 1)

        @block.tensor
        def _(pe):
            def transpose_x(t):
                pe.wait_ge(ln1_done, t + 1)
                if not is0(t):
                    pe.wait_ge(xlo_done, t)
                for k in range(DC):
                    mm = pe.transpose(pT[:, k, :], XN[:, k * P:(k + 1) * P], ident[:, :])
                mm.then_inc(xT_done, 1)

            def scores(t, b):
                pe.wait_ge(xlo_done, t + 1)
                if not is0(t):
                    pe.wait_ge(sub_done, t)
                for g in range(2):
                    s = slice(g * HG * NKV, (g + 1) * HG * NKV)
                    mm = split(pe.matmul, pS[:, g, 0:HG * NKV],
                               [((XTh[:, k, :], XTl[:, k, :]), (aw["WKh"][:, b, k, s], aw["WKl"][:, b, k, s]))
                                for k in range(DC)])
                mm.then_inc(score_done, 1)

            def transpose_x3(t):
                pe.wait_ge(ln3_done, t + 1)
                if not is0(t):
                    pe.wait_ge(x3T_copied, t)
                for k in range(DC):
                    mm = pe.transpose(pT3[:, k, :], X3[:, k * P:(k + 1) * P], ident[:, :])
                mm.then_inc(x3T_done, 1)

            def logits(t):
                pe.wait_ge(x3T_copied, t + 1)
                if not is0(t):
                    pe.wait_ge(rt, RT * t)
                for k in range(DC):
                    mm = pe.matmul(pL[:, 0:NE], X3T[:, k, :], Wg[:, k, :], start=(k == 0), stop=(k == DC - 1))
                mm.then_inc(logit_done, 1)

            def count(t):
                pe.wait_ge(rt, RT * t + RT1)
                pe.matmul(pL[:, 64:64 + NE], c["tri"][:, :], oh[:, :], start=True, stop=False)
                pe.matmul(pL[:, 64:64 + NE], c["ones"][:, :], seen[:, :], start=False, stop=True).then_inc(count_done, 1)

            def body(t, b, nb):
                pe.wait_ge(prob_done, t + 1)
                if not is0(t):
                    pe.wait_ge(plo_done, 2 * t)
                for k in range(SCC):
                    mm = pe.transpose(pP[:, k // 4, k % 4, :], E[:, k * P:(k + 1) * P], ident[:, :])
                mm.then_inc(pt_done, 1)
                if not is0(t):
                    transpose_x3(t - 1)
                if nb is not None:
                    transpose_x(t + 1)
                    scores(t + 1, nb)
                if not is0(t):
                    logits(t - 1)
                pe.wait_ge(plo_done, 2 * t + 2)
                if not is0(t):
                    pe.wait_ge(x2_done, t)
                split(pe.matmul, pY[:, :], [((PTh[:, k, :], PTl[:, k, :]), (aw["VWh"][:, b, k, :], aw["VWl"][:, b, k, :]))
                                            for k in range(SCC)]).then_inc(y_done, 1)
                if not is0(t):
                    count(t - 1)

            transpose_x(0)
            scores(0, 0)
            segments(pe, body)
            transpose_x3(NTILE - 1)
            logits(NTILE - 1)
            count(NTILE - 1)


def experts(nc, sb, ps, sem, c, dram):
    ident = c["ident"]
    raw = [sb(f"raw{n}", [P, 4, 512], F32) for n in range(4)]
    Wh = [sb(f"Wh{n}", [P, 4, 512], F32R) for n in range(4)]
    Wl = [sb(f"Wl{n}", [P, 4, 512], F32R) for n in range(4)]
    XE = sb("XE", [P, ST, D], F32)
    XTh, XTl = sb("XEh", [P, DC, CAP], F32R), sb("XEl", [P, DC, CAP], F32R)
    HR = [sb(f"HR{n}", [P, QC, CAP], F32) for n in range(2)]
    Hh = [sb(f"Hh{n}", [P, QC, CAP], F32R) for n in range(2)]
    Hl = [sb(f"Hl{n}", [P, QC, CAP], F32R) for n in range(2)]
    B1 = sb("B1", [P, HE // P], F32)
    B2 = sb("B2", [P, D], F32)
    Y = sb("Y", [P, ST, D], F32)
    pX = ps("pX", [P, DC, CAP])
    pH = [ps(f"pH{n}", [P, QC, CAP]) for n in range(2)]
    pY = ps("pYE", [P, ST, D])

    w_landed = [sem(f"w_landed_{n}") for n in range(4)]
    xe_landed, b_landed, y_stored = sem("xe_landed"), sem("b_landed"), sem("y_stored")
    whi, wlo = sem("whi_done"), sem("wlo_done")
    xT_done, xhi, xlo = sem("xeT_done"), sem("xehi_done"), sem("xelo_done")
    h_done, relu, hhi, hlo = sem("h1_done"), sem("relu_done"), sem("hhi_done"), sem("hlo_done")
    w2_done, y_done = sem("w2_done"), sem("ye_done")

    xs_v = dram["xs"][0:SLOTS, :].rearrange("(e t p) d -> e p t d", t=ST, p=P)
    ys_v = dram["ys"][0:SLOTS, :].rearrange("(e t p) d -> e p t d", t=ST, p=P)
    w1_v = dram["W1"].rearrange("e (k p) (q h) -> e q p k h", p=P, q=NQ)
    w2_v = dram["W2"].rearrange("e (q k p) d -> e q p k d", p=P, q=NQ)
    b1_v, b2_v = dram["b1"], dram["b2"]

    def at(v, e):
        return v[e] if isinstance(e, int) else v[bass.ds(e, 1)]

    def at3(v, e):
        return v[e] if isinstance(e, int) else v[bass.ds(e, 1)].rearrange("o p t d -> p (o t) d")

    def segments(eng, body):
        body(0, True, False)
        with eng.Fori(1, NE - 1) as e:
            body(e, False, False)
        body(NE - 1, False, True)

    with nc.Block() as block:
        @block.sync
        def _(sp):
            def body(e, first, last):
                for j in range(2 * NQ):
                    v = (w1_v, w2_v)[j % 2]
                    src = v[e, j // 2] if isinstance(e, int) else v[bass.ds(e, 1), j // 2].rearrange("o p k h -> p (o k) h")
                    if not (first and j < 4):
                        sp.wait_ge(wlo, 2 * NQ * e + j - 3)
                    sp.dma_start(raw[j % 4][:, :, :], src).then_inc(w_landed[j % 4], 16)
                    if j == 0:
                        if not first:
                            sp.wait_ge(xT_done, e)
                        sp.dma_start(XE[:, :, :], at3(xs_v, e)).then_inc(xe_landed, 16)
                    if j == 1:
                        if not first:
                            sp.wait_ge(y_done, e)
                        sp.dma_start(B1[:, :], b1_v[e] if isinstance(e, int) else
                                     b1_v[bass.ds(e, 1)].rearrange("o p k -> p (o k)")).then_inc(b_landed, 16)
                        sp.dma_start(B2[:, :], (b2_v[e:e + 1, :] if isinstance(e, int) else b2_v[bass.ds(e, 1), :])
                                     .to_broadcast([P, D])).then_inc(b_landed, 16)

            segments(sp, body)

        @block.gpsimd
        def _(pool):
            def body(e, first, last):
                pool.wait_ge(y_done, e + 1)
                dst = ys_v[e] if isinstance(e, int) else ys_v[bass.ds(e, 1)].rearrange("o p t d -> p (o t) d")
                pool.dma_start(dst, Y[:, :, :]).then_inc(y_stored, 16)

            segments(pool, body)
            pool.wait_ge(y_stored, 16 * NE)

        def w_free(eng, e, j, first):
            if j < 4 and first:
                return
            q = (j // 2) - 2
            if j % 2 == 0:
                eng.wait_ge(h_done, NQ * e + q + 1)
            else:
                eng.wait_ge(w2_done, NQ * e + q + 1)

        @block.scalar
        def _(act):
            def w_hi(e, j, first):
                act.wait_ge(w_landed[j % 4], 32 * e + 16 * (j // 4) + 16)
                w_free(act, e, j, first)
                act.activation(Wh[j % 4][:, :, :], raw[j % 4][:, :, :], ACT.Copy).then_inc(whi, 1)

            def body(e, first, last):
                act.wait_ge(xT_done, e + 1)
                for b in range(2):
                    act.activation(XTh[:, 2 * b:2 * b + 2, :], pX[:, 2 * b:2 * b + 2, :], ACT.Copy).then_inc(xhi, 1)
                for q in range(NQ):
                    w_hi(e, 2 * q, first)
                    w_hi(e, 2 * q + 1, first)
                    act.wait_ge(h_done, NQ * e + q + 1)
                    act.wait_ge(b_landed, 32 * e + 32)
                    if not (first and q < 2):
                        act.wait_ge(hlo, NQ * e + q - 1)
                    for k in range(QC):
                        act.activation(HR[q % 2][:, k, :], pH[q % 2][:, k, :], ACT.Relu,
                                       bias=B1[:, q * QC + k:q * QC + k + 1]).then_inc(relu, 1)
                    act.wait_ge(relu, QC * (NQ * e + q + 1))
                    if not (first and q < 2):
                        act.wait_ge(w2_done, NQ * e + q - 1)
                    act.activation(Hh[q % 2][:, :, :], HR[q % 2][:, :, :], ACT.Copy).then_inc(hhi, 1)

            segments(act, body)

        @block.vector
        def _(dve):
            def w_lo(e, j):
                dve.wait_ge(whi, 2 * NQ * e + j + 1)
                dve.tensor_tensor(Wl[j % 4][:, :, :], raw[j % 4][:, :, :], Wh[j % 4][:, :, :].bitcast(F32),
                                  ALU.subtract).then_inc(wlo, 1)

            def body(e, first, last):
                for b in range(2):
                    dve.wait_ge(xhi, 2 * e + b + 1)
                    dve.tensor_tensor(XTl[:, 2 * b:2 * b + 2, :], pX[:, 2 * b:2 * b + 2, :],
                                      XTh[:, 2 * b:2 * b + 2, :].bitcast(F32), ALU.subtract).then_inc(xlo, 1)
                for q in range(NQ):
                    w_lo(e, 2 * q)
                    if q == 0 and not first:
                        finish(e - 1, False)
                    w_lo(e, 2 * q + 1)
                    dve.wait_ge(hhi, NQ * e + q + 1)
                    dve.tensor_tensor(Hl[q % 2][:, :, :], HR[q % 2][:, :, :], Hh[q % 2][:, :, :].bitcast(F32),
                                      ALU.subtract).then_inc(hlo, 1)

            def finish(e, last):
                dve.wait_ge(w2_done, NQ * e + NQ)
                dve.wait_ge(b_landed, 32 * e + 32)
                if not (isinstance(e, int) and e == 0):
                    dve.wait_ge(y_stored, 16 * e)
                for t in range(ST):
                    ins = dve.tensor_tensor(Y[:, t, :], pY[:, t, :], B2[:, :], ALU.add)
                ins.then_inc(y_done, 1)

            segments(dve, body)
            finish(NE - 1, True)

        @block.tensor
        def _(pe):
            def transposes(e, first=False):
                pe.wait_ge(xe_landed, 16 * e + 16)
                if not first:
                    pe.wait_ge(xlo, 2 * e)
                for k in range(DC):
                    for t in range(ST):
                        mm = pe.transpose(pX[:, k, t * P:(t + 1) * P], XE[:, t, k * P:(k + 1) * P], ident[:, :])
                mm.then_inc(xT_done, 1)

            def first_product(e, q, first):
                j = (2 * q) % 4
                pe.wait_ge(wlo, 2 * NQ * e + 2 * q + 1)
                pe.wait_ge(xlo, 2 * e + 2)
                if not (first and q < 2):
                    pe.wait_ge(relu, QC * (NQ * e + q - 1))
                for m in range(QC):
                    s = slice(m * P, (m + 1) * P)
                    mm = split(pe.matmul, pH[q % 2][:, m, :], [((Wh[j][:, k, s], Wl[j][:, k, s]), (XTh[:, k, :], XTl[:, k, :]))
                                                               for k in range(DC)])
                mm.then_inc(h_done, 1)

            def second_product(e, q, first):
                j = (2 * q + 1) % 4
                pe.wait_ge(wlo, 2 * NQ * e + 2 * q + 2)
                pe.wait_ge(hlo, NQ * e + q + 1)
                if q == 0 and not first:
                    pe.wait_ge(y_done, e)
                for t in range(ST):
                    s = slice(t * P, (t + 1) * P)
                    mm = split(pe.matmul, pY[:, t, :], [((Hh[q % 2][:, k, s], Hl[q % 2][:, k, s]), (Wh[j][:, k, :], Wl[j][:, k, :]))
                                                        for k in range(QC)], start=(q == 0), stop=(q == NQ - 1))
                mm.then_inc(w2_done, 1)

            def body(e, first, last):
                for q in range(NQ):
                    first_product(e, q, first)
                    if q:
                        second_product(e, q - 1, first)
                if not last:
                    transposes(e + 1)
                second_product(e, NQ - 1, first)

            transposes(0, first=True)
            segments(pe, body)


def combine(nc, sb, ps, sem, dram, route):
    N = 4
    X, Yg = [sb(f"XC{n}", [P, D], F32) for n in range(N)], [sb(f"YG{n}", [P, D], F32) for n in range(N)]
    IDX = [sb(f"IDX{n}", [P, 1], U32) for n in range(N)]
    x_landed, y_landed, o_stored = ([sem(f"{s}{n}") for n in range(N)] for s in ("xc_landed", "yg_landed", "o_stored"))
    idx_done, sum_done, passed = sem("idx_done"), sem("sum_done"), sem("passed")
    x2_v = dram["x2"].rearrange("(n p) d -> n p d", p=P)
    out_v = dram["out"].rearrange("(n p) d -> n p d", p=P)

    def tile(v, t):
        return v[bass.ds(t, 1)].rearrange("o p d -> p (o d)")

    def first_then_loop(eng, body):
        for n in range(N):
            body(0, n, True)
        with eng.Fori(1, NTILE // N) as g:
            for n in range(N):
                body(g, n, False)

    with nc.Block() as block:
        @block.sync
        def _(sp):
            def body(g, n, first):
                if not first:
                    sp.wait_ge(sum_done, N * (g - 1) + n + 1)
                    sp.dma_start(tile(out_v, N * (g - 1) + n), X[n][:, :]).then_inc(o_stored[n], 16)
                    sp.wait_ge(o_stored[n], 16 * g)
                sp.dma_start(X[n][:, :], tile(x2_v, N * g + n)).then_inc(x_landed[n], 16)

            first_then_loop(sp, body)
            for n in range(N):
                sp.wait_ge(sum_done, NTILE - N + n + 1)
                sp.dma_start(out_v[NTILE - N + n], X[n][:, :]).then_inc(o_stored[n], 16)
            for n in range(N):
                sp.wait_ge(o_stored[n], 16 * (NTILE // N))

        @block.gpsimd
        def _(pool):
            def body(g, n, first):
                if not first:
                    pool.wait_ge(sum_done, N * (g - 1) + n + 1)
                wait_apart(pool, idx_done, N * g + n + 1, passed)
                pool.indirect_dma_start(out=Yg[n][:, :], out_offset=None, in_=dram["ys"],
                                        in_offset=bass.IndirectOffsetOnAxis(IDX[n][:, 0:1], 0)).then_inc(y_landed[n], 16)

            first_then_loop(pool, body)

        @block.vector
        def _(dve):
            def index(g, n):
                dve.tensor_copy(IDX[n][:, :], route["place"][:, bass.ds(N * g + n, 1)]).then_inc(idx_done, 1)

            def total(g, n):
                dve.wait_ge(y_landed[n], 16 * g + 16)
                dve.wait_ge(x_landed[n], 16 * g + 16)
                dve.scalar_tensor_tensor(out=X[n][:, :], in0=Yg[n][:, :], scalar=route["gate"][:, bass.ds(N * g + n, 1)],
                                         in1=X[n][:, :], op0=ALU.mult, op1=ALU.add).then_inc(sum_done, 1)

            for n in range(N):
                index(0, n)
            with dve.Fori(1, NTILE // N) as g:
                for n in range(N):
                    total(g - 1, n)
                    index(g, n)
            for n in range(N):
                total(NTILE // N - 1, n)



def build(nc, dram):
    with ExitStack() as top:
        def alloc(stack):
            def sb(name, shape, dt):
                return stack.enter_context(nc.sbuf_tensor(name, shape, dt))

            def ps(name, shape, dt=F32):
                return stack.enter_context(nc.psum_tensor(name, shape, dt))

            def sem(name):
                return stack.enter_context(nc.semaphore(name))
            return sb, ps, sem

        sb, ps, sem = alloc(top)
        c = constants(nc, sb, sem)
        with ExitStack() as part:
            sb, ps, sem = alloc(part)
            w = {n: sb(n, [P, k, 2 * HID], F32R) for n, k in (("Wih", DC), ("Wil", DC), ("Wgh", HC), ("Wgl", HC))}
            w["Wo"] = sb("Wo_sb", [P, HC, D], F32)
            small = {"fb": sb("fb", [P, HC], F32), "conv_w": sb("conv_w", [P, HC * TAPS], F32),
                     "conv_b": sb("conv_b", [P, HC], F32), "bg": sb("bg", [P, 2 * HC], F32),
                     "hbg": sb("hbg", [P, 2 * HC], F32), "decay": sb("decay", [P, HC], F32),
                     "one_eps": sb("one_eps", [P, 1], F32), "work": sb("work", [P, 5, HC], F32)}
            with ExitStack() as staging:
                sb2, _, sem2 = alloc(staging)
                prepare_recurrence(nc, sem2, sb2("w_stage", [P, 2, 2 * HID], F32), w, dram, small)
            recurrence(nc, sb, ps, sem, c, w, dram, small)
        sb, ps, sem = alloc(top)
        route = {"place": sb("place", [P, NTILE], F32), "gate": sb("gate", [P, NTILE], F32)}
        with ExitStack() as part:
            sb, ps, sem = alloc(part)
            aw = {n: sb(n, [P, BATCH, DC, SC], F32R) for n in ("WKh", "WKl")}
            aw |= {n: sb(n, [P, BATCH, SCC, D], F32R) for n in ("VWh", "VWl")}
            with ExitStack() as sub:
                prepare_attention(nc, *alloc(sub), aw, dram)
            attention(nc, sb, ps, sem, c, aw, dram, route)
        with ExitStack() as part:
            experts(nc, *alloc(part), c, dram)
        with ExitStack() as part:
            combine(nc, *alloc(part), dram, route)


SCRATCH = {"x1": [TOK, D], "x2": [TOK, D], "vw": [BATCH, SCP, D],
           "xs": [SLOTS + 1 + TOK, D],
           "ys": [SLOTS + 1, D]}


def layout(i):
    import numpy as np

    def chunks(a):
        return np.ascontiguousarray(a.reshape(a.shape[0] // P, P, a.shape[1]).transpose(1, 0, 2))

    def columns(a):
        return np.ascontiguousarray(a.reshape(-1, P).T)

    return {
        "x": i["x"].reshape(TOK, D),
        "Wi": chunks(i["L0_attn_Wi"].T), "Wg": chunks(i["L0_attn_Wg"].T), "Wo": chunks(i["L0_attn_Wo"].T),
        "conv_w": np.ascontiguousarray(i["L0_attn_conv_w"].reshape(HC, P, TAPS).transpose(1, 0, 2).reshape(P, HC * TAPS)),
        "conv_b": columns(i["L0_attn_conv_b"]), "bg": columns(i["L0_attn_bg"]), "fb": columns(i["L0_attn_forget_base"]),
        "ctxT": np.ascontiguousarray(i["ctx_768"].reshape(BATCH * NKV, CC, P).transpose(2, 1, 0)),
        "Wk": chunks(i["L0_xattn_Wk"]), "Wv": chunks(i["L0_xattn_Wv"]),
        "WqT": np.ascontiguousarray(i["L0_xattn_Wq"].T.reshape(HEADS, DH, D).transpose(1, 0, 2)),
        "xWo": np.ascontiguousarray(i["L0_xattn_Wo"].reshape(HEADS, DH, D).transpose(1, 0, 2)),
        "bo": i["L0_xattn_bo"].reshape(1, D),
        "Wgate": chunks(i["L0_ffn_Wg"]), "bgate": i["L0_ffn_bg"],
        "W1": i["L0_ffn_W1"], "W2": i["L0_ffn_W2"],
        "b1": np.ascontiguousarray(i["L0_ffn_b1"].reshape(NE, HE // P, P).transpose(0, 2, 1)), "b2": i["L0_ffn_b2"],
    }


def kernel(**inputs):
    import numpy as _np
    import concourse.bacc as _bacc
    from concourse import mybir as _mybir
    from concourse.bass_utils import run_bass_kernel_spmd as _run

    nc = _bacc.Bacc("TRN2", target_bir_lowering=False, num_devices=1)
    arrays, dram = {}, {}
    for name, a in layout({k: _np.asarray(v) for k, v in inputs.items()}).items():
        a = _np.ascontiguousarray(a)
        arrays[f"in_{name}"] = a
        dram[name] = nc.dram_tensor(f"in_{name}", a.shape, _mybir.dt.from_np(a.dtype), kind="ExternalInput").ap()
    for name, shape in SCRATCH.items():
        dram[name] = nc.dram_tensor(name, shape, F32, kind="Internal").ap()
    dram["out"] = nc.dram_tensor("out_dram", (TOK, D), F32, kind="ExternalOutput").ap()
    build(nc, dram)
    r = _run(nc, [arrays], core_ids=[0])
    return r.results[0]["out_dram"].reshape(BATCH, SEQ, D)
```

```python
from contextlib import ExitStack

import concourse.bass as bass
from concourse import mybir

F32 = mybir.dt.float32
F32R = mybir.dt.float32r
BF16 = mybir.dt.bfloat16
I32 = mybir.dt.int32
U32 = mybir.dt.uint32
ALU = mybir.AluOpType
ACT = mybir.ActivationFunctionType
AX = mybir.AxisListType

P = 128
BATCH, SEQ, D = 2, 2048, 512
TOK = BATCH * SEQ
HID, TAPS = 768, 4
DC, HC = D // P, HID // P
EPS = 1e-5

TB = 256
NBLK = TOK // TB
BLK_SEQ = SEQ // TB
TT = TB // P
RING = 4
USES = 4 * HC
GRP = 2

HEADS, DH, CTX, NKV = 8, 64, 384, 77
CC = CTX // P
HG = HEADS // 2
SC = HEADS * NKV
SCC = -(-(SC + 1) // P)
SCP = SCC * P
NTILE = TOK // P
TILE_SEQ = SEQ // P
SCALE = DH ** -0.5

NE, HE = 16, 2048
CAP = -(-TOK // NE)
SLOTS = NE * CAP
NQ = 4
QH = HE // NQ
QC = QH // P
ST = CAP // P


def split(mm, out, pairs, start=True, stop=True):
    n = len(pairs)
    for k, ((ah, al), (bh, bl)) in enumerate(pairs):
        mm(out, ah, bh, start=start and k == 0, stop=False)
        mm(out, ah, bl, start=False, stop=False)
        last = mm(out, al, bh, start=False, stop=stop and k == n - 1)
    return last


def wait_apart(eng, sem, value, passed):
    eng.wait_ge(sem, value)
    eng.sem_inc(passed, 1)


def constants(nc, sb, sem):
    c = {
        "ident": sb("ident", [P, P], F32), "tri": sb("tri", [P, P], BF16), "ones": sb("ones", [P, P], BF16),
        "iota16": sb("iota16", [P, NE], F32), "iotap": sb("iotap", [P, 1], F32),
        "mhalf": sb("mhalf", [P, TT], F32),
    }
    made = sem("constants_made")
    with nc.Block() as block:
        @block.gpsimd
        def _(pool):
            pool.memset(c["ident"][:, :], 0.0).then_inc(made, 1)
            pool.memset(c["tri"][:, :], 1.0).then_inc(made, 1)
            pool.memset(c["ones"][:, :], 1.0).then_inc(made, 1)
            pool.memset(c["mhalf"][:, :], -0.5).then_inc(made, 1)
            pool.wait_ge(made, 4)
            pool.affine_select(out=c["ident"][:, :], in_=c["ident"][:, :], compare_op=ALU.not_equal, fill=1.0,
                               base=0, pattern=[[-1, P]], channel_multiplier=1).then_inc(made, 1)
            pool.affine_select(out=c["tri"][:, :], in_=c["tri"][:, :], compare_op=ALU.is_gt, fill=0.0,
                               base=0, pattern=[[1, P]], channel_multiplier=-1).then_inc(made, 1)
            pool.iota(c["iota16"][:, :], pattern=[[1, NE]], base=-NE, channel_multiplier=0,
                      allow_small_or_imprecise_dtypes=True).then_inc(made, 1)
            pool.iota(c["iotap"][:, :], pattern=[[0, 1]], base=0, channel_multiplier=1,
                      allow_small_or_imprecise_dtypes=True).then_inc(made, 1)
            pool.wait_ge(made, 8)
    return c


def prepare(nc, sb, ps, sem, w, dram, small):
    stage = sb("w_stage", [P, 2, 2 * HID], F32)
    landed = [sem("w_landed0"), sem("w_landed1")]
    hi_done, lo_done, small_landed, wo_landed = (sem(n) for n in ("w_hi_done", "w_lo_done", "small_landed", "wo_landed"))
    sp_step, sp_exp = sem("softplus_step"), sem("softplus_exp")
    jobs = [(dram["Wi"], w["Wih"], w["Wil"], k) for k in range(DC)] + \
           [(dram["Wg"], w["Wgh"], w["Wgl"], k) for k in range(HC)]
    fb, cw = small["fb"], small["work"]

    NJ = BATCH * NKV
    NP = HEADS // 2
    ctxT, Wk, Wv = sb("ctxT", [P, CC, NJ], F32), sb("Wk", [P, CC, D], F32), sb("Wv", [P, CC, D], F32)
    WqT, Wo = sb("WqT", [P, NP, D], F32), sb("Wo2", [P, NP, D], F32)
    KT, VT = sb("KT", [P, NP, NJ], F32), sb("VT", [P, NP, NJ], F32)
    WKs, VWs = sb("WKs", [P, 2, BATCH, SC], F32), sb("VWs", [NKV, 2, D], F32)
    zero = sb("zero", [SCP - SC - 1, D], F32)
    none = sb("none", [P, 2 * SLOTS // P], F32)
    pR = ps("pR", [P, 4, 512])
    in_landed, zeroed, pads_stored, map_cleared = (sem(n) for n in ("in_landed", "zeroed", "pads_stored", "map_cleared"))
    pe_done, evac = sem("pe_done"), sem("evac")
    wk_stored, vw_stored = [[sem(f"{n}_stored{b}") for b in range(2)] for n in ("wk", "vw")]
    NK, NS, NV = 2 * NP, DC * HEADS, BATCH * HEADS
    vw = dram["vw"]

    with nc.Block() as block:
        @block.sync
        def _(sp):
            for t, n in ((ctxT, "ctxT"), (Wk, "Wk"), (Wv, "Wv")):
                sp.dma_start(t[:, :, :], dram[n]).then_inc(in_landed, 16)
            for n, (src, hi, lo, k) in enumerate(jobs):
                if n >= 2:
                    sp.wait_ge(lo_done, n - 1)
                sp.dma_start(stage[:, n % 2, :], src[:, k, :]).then_inc(landed[n % 2], 16)
                if n == 0:
                    for name in ("fb", "conv_w", "conv_b", "bg"):
                        sp.dma_start(small[name][:, :], dram[name]).then_inc(small_landed, 16)
                    for t, nm in ((WqT, "WqT"), (Wo, "xWo")):
                        sp.dma_start(t[:, :, :], dram[nm]).then_inc(in_landed, 16)
            sp.dma_start(w["Wo"][:, :, :], dram["Wo"]).then_inc(wo_landed, 16)
            sp.wait_ge(wo_landed, 16)

        @block.gpsimd
        def _(pool):
            pool.memset(zero[:, :], 0.0).then_inc(zeroed, 1)
            pool.memset(none[:, :], 2.0 * TOK).then_inc(zeroed, 1)
            pool.wait_ge(zeroed, 2)
            pool.dma_start(dram["slotmap"][0:SLOTS, :].rearrange("(p r) c -> p (r c)", p=P), none[:, :]).then_inc(map_cleared, 16)
            for b in range(BATCH):
                pool.dma_start(vw[b, SC + 1:SCP, :], zero[:, :]).then_inc(pads_stored, 16)
                pool.dma_start(vw[b, SC:SC + 1, :], dram["bo"]).then_inc(pads_stored, 16)
            for k in range(DC):
                pool.wait_ge(evac, NK + HEADS * (k + 1))
                pool.dma_start(dram["wk"][:, :, k, :], WKs[:, k % 2, :, :]).then_inc(wk_stored[k % 2], 16)
            for n in range(NV):
                b, h = n // HEADS, n % HEADS
                pool.wait_ge(evac, NK + NS + n + 1)
                pool.dma_start(vw[b, h * NKV:(h + 1) * NKV, :], VWs[:, n % 2, :]).then_inc(vw_stored[n % 2], 16)
            pool.wait_ge(map_cleared, 16)
            pool.wait_ge(pads_stored, 32 * BATCH)
            for r in range(2):
                pool.wait_ge(wk_stored[r], 16 * DC // 2)
                pool.wait_ge(vw_stored[r], 16 * NV // 2)

        @block.tensor
        def _(pe):
            pe.wait_ge(in_landed, 80)
            use = 0

            def begin():
                if use >= 4:
                    pe.wait_ge(evac, use - 3)

            for src in (Wk, Wv):
                for h in range(NP):
                    begin()
                    for k in range(CC):
                        mm = pe.matmul(pR[:, use % 4, 0:NJ], src[:, k, h * P:(h + 1) * P], ctxT[:, k, :],
                                       start=(k == 0), stop=(k == CC - 1))
                    mm.then_inc(pe_done, 1)
                    use += 1
            pe.wait_ge(evac, NK)
            for k in range(DC):
                for h in range(HEADS):
                    begin()
                    r = slice(h % 2 * DH, h % 2 * DH + DH)
                    pe.matmul(pR[:, use % 4, 0:NJ], WqT[r, h // 2, k * P:(k + 1) * P], KT[r, h // 2, :],
                              start=True, stop=True).then_inc(pe_done, 1)
                    use += 1
            for b in range(BATCH):
                for h in range(HEADS):
                    begin()
                    r = slice(h % 2 * DH, h % 2 * DH + DH)
                    pe.matmul(pR[0:NKV, use % 4, :], VT[r, h // 2, b * NKV:(b + 1) * NKV], Wo[r, h // 2, :],
                              start=True, stop=True).then_inc(pe_done, 1)
                    use += 1

        @block.scalar
        def _(act):
            act.wait_ge(small_landed, 64)
            act.activation(cw[:, 0, :], fb[:, :], ACT.Abs).then_inc(sp_exp, 1)
            act.wait_ge(sp_exp, 1)
            act.activation(cw[:, 1, :], cw[:, 0, :], ACT.Exp, scale=-1.0).then_inc(sp_exp, 1)
            for n, (src, hi, lo, k) in enumerate(jobs):
                act.wait_ge(landed[n % 2], 16 * (n // 2 + 1))
                act.activation(hi[:, k, :], stage[:, n % 2, :], ACT.Copy).then_inc(hi_done, 1)

        @block.vector
        def _(dve):
            def projections():
                for n in range(NK):
                    dve.wait_ge(pe_done, n + 1)
                    dve.tensor_copy((KT if n < NP else VT)[:, n % NP, :], pR[:, n % 4, 0:NJ]).then_inc(evac, 1)

            def wk(k):
                for h in range(HEADS):
                    n = HEADS * k + h
                    dve.wait_ge(pe_done, NK + n + 1)
                    if h == 0 and k >= 2:
                        dve.wait_ge(wk_stored[k % 2], 16 * (k // 2))
                    dve.tensor_copy(WKs[:, k % 2, :, h * NKV:(h + 1) * NKV],
                                    pR[:, (NK + n) % 4, 0:NJ].rearrange("p (b j) -> p b j", b=BATCH)).then_inc(evac, 1)

            def vwo(b):
                for n in range(b * HEADS, (b + 1) * HEADS):
                    dve.wait_ge(pe_done, NK + NS + n + 1)
                    if n >= 2:
                        dve.wait_ge(vw_stored[n % 2], 16 * (n // 2))
                    dve.tensor_copy(VWs[:, n % 2, :], pR[0:NKV, (NK + NS + n) % 4, :]).then_inc(evac, 1)

            between = {0: lambda: projections(), 2: lambda: wk(0), 3: lambda: wk(1), 4: lambda: wk(2),
                       5: lambda: wk(3), 7: lambda: vwo(0), 9: lambda: vwo(1)}
            for n, (src, hi, lo, k) in enumerate(jobs):
                dve.wait_ge(hi_done, n + 1)
                dve.tensor_tensor(lo[:, k, :], stage[:, n % 2, :], hi[:, k, :].bitcast(F32),
                                  ALU.subtract).then_inc(lo_done, 1)
                if n in between:
                    between[n]()
            step = [0]

            def then(ins):
                step[0] += 1
                ins.then_inc(sp_step, 1)
                dve.wait_ge(sp_step, step[0])

            dve.wait_ge(sp_exp, 2)
            dve.wait_ge(small_landed, 64)
            e, s, s2, acc = cw[:, 1, :], cw[:, 2, :], cw[:, 3, :], cw[:, 4, :]
            then(dve.tensor_scalar(s, e, 2.0, None, ALU.add))
            then(dve.reciprocal(s, s))
            then(dve.tensor_tensor(s, s, e, ALU.mult))
            then(dve.tensor_tensor(s2, s, s, ALU.mult))
            then(dve.tensor_scalar(acc, s2, 1.0 / 19, 1.0 / 17, ALU.mult, ALU.add))
            for m in (15, 13, 11, 9, 7, 5, 3, 1):
                then(dve.tensor_tensor(acc, acc, s2, ALU.mult))
                then(dve.tensor_scalar(acc, acc, 1.0 / m, None, ALU.add))
            then(dve.tensor_tensor(acc, acc, s, ALU.mult))
            then(dve.tensor_scalar(s, fb[:, :], 0.0, None, ALU.max))
            then(dve.scalar_tensor_tensor(out=acc, in0=acc, scalar=2.0, in1=s, op0=ALU.mult, op1=ALU.add))
            then(dve.tensor_scalar(small["decay"][:, :], acc, -4.0, None, ALU.mult))
            then(dve.tensor_scalar(small["hbg"][:, :], small["bg"][:, :], 0.5, None, ALU.mult))
            then(dve.memset(small["one_eps"][:, :], 1.0 + 1e-6))


def recurrence(nc, sb, ps, sem, c, w, dram, small):
    ident = c["ident"]
    SLOT = 2 * GRP
    X, R, XN = (sb(n, [P, TT, D], F32) for n in ("X", "R", "XN"))
    XTh, XTl = sb("XTh", [P, DC, TB], F32R), sb("XTl", [P, DC, TB], F32R)
    HALO = TAPS - 1
    UR = sb("UR", [P, HC, TB + HALO], F32)
    U = sb("U", [P, HC, TB], F32)
    Uh, Ul = sb("Uh", [P, HC, TB], F32R), sb("Ul", [P, HC, TB], F32R)
    G, GH = sb("G", [P, HC, TB], F32), sb("GH", [P, HC, TB], F32)
    H = sb("H", [P, GRP, TB], F32)
    TI, AL, BE = (sb(n, [P, SLOT, TB], F32) for n in ("TI", "AL", "BE"))
    carry = sb("carry", [P, HC], F32)
    stats, mv = sb("stats", [P, TT, 6], F32), sb("mv", [P, TT, 2], F32)
    rstd = sb("rstd", [P, TT], F32)
    pT = ps("pT", [P, DC, TB])
    pM = ps("pM", [P, RING, 512])
    pO = ps("pO", [P, TT, 512])

    x_landed, r_landed, x1_stored = sem("x_landed"), sem("r_landed"), sem("x1_stored")
    ln_step, ln_pow, ln_done = sem("ln_step"), sem("ln_pow"), sem("ln_done")
    xT_done, xhi_done, xlo_done = sem("xT_done"), sem("xhi_done"), sem("xlo_done")
    mm_done, mm_free = sem("mm_done"), sem("mm_free")
    conv_step, u_done, halo_done = sem("conv_step"), sem("u_done"), sem("halo_done")
    act_gate, gate_step, h_done = sem("act_gate"), sem("gate_step"), sem("h_done")
    gh_done, wo_done, resid_done = sem("gh_done"), sem("wo_done"), sem("resid_done")
    reset, passed = sem("reset"), sem("passed")

    x_v = dram["x"].rearrange("(n t p) d -> n p t d", t=TT, p=P)
    x1_v = dram["x1"].rearrange("(n t p) d -> n p t d", t=TT, p=P)
    CW, CB, DEC, HBG = small["conv_w"], small["conv_b"], small["decay"], small["hbg"]
    NG = HC // GRP
    AG = 5 * GRP

    def segments(eng, body):
        body(0, True, False)
        with eng.Fori(1, BLK_SEQ) as i:
            body(i, False, False)
        for b in range(1, BATCH):
            if b > 1:
                with eng.Fori(b * BLK_SEQ, (b + 1) * BLK_SEQ - (b == BATCH - 1)) as i:
                    body(i, False, False)
        with eng.Fori(BLK_SEQ, NBLK - 1) as i:
            body(i, False, False)
        body(NBLK - 1, False, True)

    with nc.Block() as block:
        @block.sync
        def _(sp):
            sp.dma_start(X[:, :, :], x_v[0]).then_inc(x_landed, 16)

            def body(i, first, last):
                if not last:
                    sp.wait_ge(ln_done, i + 1)
                    sp.dma_start(X[:, :, :], x_v[bass.ds(i + 1, 1)].rearrange("o p t d -> p (o t) d")
                                 if not isinstance(i, int) else x_v[i + 1]).then_inc(x_landed, 16)
                if not first:
                    sp.wait_ge(resid_done, i)
                    sp.dma_start(x1_v[bass.ds(i - 1, 1)].rearrange("o p t d -> p (o t) d")
                                 if not isinstance(i, int) else x1_v[i - 1], R[:, :, :]).then_inc(x1_stored, 16)
                    sp.wait_ge(x1_stored, 16 * i)
                sp.dma_start(R[:, :, :], x_v[bass.ds(i, 1)].rearrange("o p t d -> p (o t) d")
                             if not isinstance(i, int) else x_v[i]).then_inc(r_landed, 16)

            segments(sp, body)
            sp.wait_ge(resid_done, NBLK)
            sp.dma_start(x1_v[NBLK - 1], R[:, :, :]).then_inc(x1_stored, 16)
            sp.wait_ge(x1_stored, 16 * NBLK)

        @block.gpsimd
        def _(pool):
            def inverse_deviation(i):
                pool.wait_ge(ln_step, 6 * i + 5)
                pool.tensor_tensor(rstd[:, :], mv[:, :, 1], c["mhalf"][:, :], ALU.pow).then_inc(ln_pow, 1)

            def body(i, first, last):
                if not last:
                    inverse_deviation(i + 1)
                for k in range(HC):
                    pool.wait_ge(h_done, HC * i + k + 1)
                    if k == 0 and not first:
                        pool.wait_ge(wo_done, i)
                    pool.tensor_tensor(GH[:, k, :], G[:, k, :], H[:, k % GRP, :], ALU.mult).then_inc(gh_done, 1)

            inverse_deviation(0)
            segments(pool, body)

        @block.scalar
        def _(act):
            def x_hi(i):
                act.wait_ge(xT_done, i + 1)
                act.activation(XTh[:, 0:2, :], pT[:, 0:2, :], ACT.Copy).then_inc(xhi_done, 1)
                act.activation(XTh[:, 2:4, :], pT[:, 2:4, :], ACT.Copy).then_inc(xhi_done, 1)

            def body(i, first, last):
                use = 0
                if not first:
                    act.wait_ge(halo_done, i)
                for k in range(HC):
                    act.wait_ge(mm_done, USES * i + use + 1)
                    act.activation(UR[:, k, HALO:], pM[:, use % RING, 0:TB], ACT.Copy).then_inc(mm_free, 1)
                    use += 1
                if not first:
                    act.wait_ge(gh_done, HC * i)
                for k in range(HC):
                    act.wait_ge(mm_done, USES * i + use + 1)
                    act.activation(G[:, k, :], pM[:, use % RING, 0:TB], ACT.Gelu).then_inc(mm_free, 1)
                    use += 1
                if not last:
                    x_hi(i + 1)
                for g in range(NG):
                    for k in range(g * GRP, (g + 1) * GRP):
                        if k >= SLOT:
                            act.wait_ge(h_done, HC * i + k - SLOT + 1)
                        elif k == 0 and not first:
                            act.wait_ge(h_done, HC * i)
                        act.wait_ge(mm_done, USES * i + use + 1)
                        act.activation(AL[:, k % SLOT, :], pM[:, use % RING, 0:TB], ACT.Tanh, bias=HBG[:, k:k + 1],
                                       scale=0.5).then_inc(mm_free, 1)
                        use += 1
                        act.wait_ge(mm_done, USES * i + use + 1)
                        act.activation(TI[:, k % SLOT, :], pM[:, use % RING, 0:TB], ACT.Tanh, bias=HBG[:, HC + k:HC + k + 1],
                                       scale=0.5).then_inc(mm_free, 1)
                        use += 1
                    for k in range(g * GRP, (g + 1) * GRP):
                        act.wait_ge(mm_free, USES * i + use - 1 - 2 * ((g + 1) * GRP - 1 - k))
                        act.activation(AL[:, k % SLOT, :], AL[:, k % SLOT, :], ACT.Exp, bias=DEC[:, k:k + 1],
                                       scale=DEC[:, k:k + 1]).then_inc(act_gate, 1)
                    for k in range(GRP):
                        act.wait_ge(act_gate, 3 * HC * i + 3 * GRP * g + k + 1)
                        act.activation(BE[:, (g * GRP + k) % SLOT, :], AL[:, (g * GRP + k) % SLOT, :], ACT.Square).then_inc(act_gate, 1)
                    for k in range(GRP):
                        act.wait_ge(act_gate, 3 * HC * i + 3 * GRP * g + GRP + k + 1)
                        act.activation(BE[:, (g * GRP + k) % SLOT, :], BE[:, (g * GRP + k) % SLOT, :], ACT.Sqrt,
                                       bias=small["one_eps"][:, 0:1], scale=-1.0).then_inc(act_gate, 1)

            x_hi(0)
            segments(act, body)

        @block.vector
        def _(dve):
            def norm(i):
                dve.wait_ge(x_landed, 16 * i + 16)
                for t in range(TT):
                    dve.bn_stats(stats[:, t, :], X[:, t, :]).then_inc(ln_step, 1)
                for t in range(TT):
                    wait_apart(dve, ln_step, 6 * i + t + 1, passed)
                    dve.bn_aggr(mv[:, t, :], stats[:, t, :]).then_inc(ln_step, 1)
                dve.wait_ge(ln_step, 6 * i + 2 * TT)
                dve.tensor_scalar(mv[:, :, 1], mv[:, :, 1], EPS, None, ALU.add).then_inc(ln_step, 2)
                dve.wait_ge(ln_pow, i + 1)
                if not (isinstance(i, int) and i == 0):
                    dve.wait_ge(xT_done, i)
                for t in range(TT):
                    ins = dve.tensor_scalar(XN[:, t, :], X[:, t, :], mv[:, t, 0:1], rstd[:, t:t + 1],
                                            ALU.subtract, ALU.mult)
                ins.then_inc(ln_done, 1)

            def x_lo(i):
                for b in range(2):
                    dve.wait_ge(xhi_done, 2 * i + b + 1)
                    dve.tensor_tensor(XTl[:, 2 * b:2 * b + 2, :], pT[:, 2 * b:2 * b + 2, :],
                                      XTh[:, 2 * b:2 * b + 2, :].bitcast(F32), ALU.subtract).then_inc(xlo_done, 1)

            def convolve(i):
                PAIR = 2 * (TAPS + 1)
                for k in range(0, HC, 2):
                    base = HC * (TAPS + 1) * i + PAIR * (k // 2)
                    for m in (k, k + 1):
                        dve.wait_ge(mm_free, USES * i + m + 1)
                        dve.tensor_scalar(U[:, m, :], UR[:, m, 0:TB], CW[:, TAPS * m:TAPS * m + 1], CB[:, m:m + 1],
                                          ALU.mult, ALU.add).then_inc(conv_step, 1)
                    for j in range(1, TAPS):
                        for m in (k, k + 1):
                            dve.wait_ge(conv_step, base + 2 * j + m - k - 1)
                            dve.scalar_tensor_tensor(out=U[:, m, :], in0=UR[:, m, j:j + TB],
                                                     scalar=CW[:, TAPS * m + j:TAPS * m + j + 1], in1=U[:, m, :],
                                                     op0=ALU.mult, op1=ALU.add).then_inc(conv_step, 1)
                    for m in (k, k + 1):
                        dve.wait_ge(conv_step, base + 2 * TAPS + m - k - 1)
                        dve.tensor_copy(Uh[:, m, :], U[:, m, :]).then_inc(conv_step, 1)
                    for m in (k, k + 1):
                        dve.wait_ge(conv_step, base + 2 * TAPS + m - k + 1)
                        dve.tensor_tensor(Ul[:, m, :], U[:, m, :], Uh[:, m, :].bitcast(F32),
                                          ALU.subtract).then_inc(u_done, 1)
                dve.tensor_copy(UR[:, :, 0:HALO], UR[:, :, TB:TB + HALO]).then_inc(halo_done, 1)

            def gates(i):
                for k in range(HC):
                    g, r, q = k // GRP, k % GRP, k % SLOT
                    dve.wait_ge(act_gate, 3 * HC * i + 3 * GRP * g + 2 * GRP + r + 1)
                    base = 4 * HC * i + 4 * k
                    dve.scalar_tensor_tensor(out=TI[:, q, :], in0=TI[:, q, :], scalar=1.0, in1=U[:, k, :],
                                             op0=ALU.add, op1=ALU.mult).then_inc(gate_step, 1)
                    dve.wait_ge(gate_step, base + 1)
                    dve.scalar_tensor_tensor(out=TI[:, q, :], in0=TI[:, q, :], scalar=0.5, in1=BE[:, q, :],
                                             op0=ALU.mult, op1=ALU.mult).then_inc(gate_step, 1)
                    dve.wait_ge(gate_step, base + 2)
                    if k >= GRP:
                        dve.wait_ge(gh_done, HC * i + k - GRP + 1)
                    elif not (isinstance(i, int) and i == 0):
                        dve.wait_ge(gh_done, HC * i)
                    dve.tensor_tensor_scan(H[:, r, :], AL[:, q, :], TI[:, q, :], carry[:, k:k + 1],
                                           ALU.mult, ALU.add).then_inc(h_done, 1)
                    dve.wait_ge(h_done, HC * i + k + 1)
                    dve.tensor_copy(carry[:, k:k + 1], H[:, r, TB - 1:TB]).then_inc(gate_step, 2)

            def residual(i):
                dve.wait_ge(wo_done, i + 1)
                dve.wait_ge(r_landed, 16 * i + 16)
                for t in range(TT):
                    ins = dve.tensor_tensor(R[:, t, :], pO[:, t, :], R[:, t, :], ALU.add)
                ins.then_inc(resid_done, 1)

            def fresh_sequence(n):
                dve.memset(UR[:, :, 0:HALO], 0.0).then_inc(reset, 1)
                dve.memset(carry[:, :], 0.0).then_inc(reset, 1)
                dve.wait_ge(reset, 2 * n)

            def body(i, first, last):
                if not last:
                    norm(i + 1)
                convolve(i)
                if not first:
                    residual(i - 1)
                if not last:
                    x_lo(i + 1)
                gates(i)

            fresh_sequence(1)
            norm(0)
            x_lo(0)
            body(0, True, False)
            with dve.Fori(1, BLK_SEQ) as i:
                body(i, False, False)
            dve.wait_ge(halo_done, BLK_SEQ)
            dve.wait_ge(gate_step, 4 * HC * BLK_SEQ)
            fresh_sequence(2)
            with dve.Fori(BLK_SEQ, NBLK - 1) as i:
                body(i, False, False)
            body(NBLK - 1, False, True)
            residual(NBLK - 1)

        @block.tensor
        def _(pe):
            def transposes(i):
                pe.wait_ge(ln_done, i + 1)
                if not (isinstance(i, int) and i == 0):
                    pe.wait_ge(xlo_done, 2 * i)
                for k in range(DC):
                    for t in range(TT):
                        mm = pe.transpose(pT[:, k, t * P:(t + 1) * P], XN[:, t, k * P:(k + 1) * P], ident[:, :])
                mm.then_inc(xT_done, 1)

            def product(out_use, i, pairs, offset=0, skip_free=False):
                if not skip_free:
                    pe.wait_ge(mm_free, USES * i + out_use + offset - RING + 1)
                split(pe.matmul, pM[:, out_use % RING, 0:TB], pairs).then_inc(mm_done, 1)

            def in_product(i, chunk, use, **kw):
                s = slice(chunk * P, (chunk + 1) * P)
                product(use, i, [((w["Wih"][:, k, s], w["Wil"][:, k, s]), (XTh[:, k, :], XTl[:, k, :]))
                                 for k in range(DC)], **kw)

            def u_products(i, first=False, offset=0):
                pe.wait_ge(xlo_done, 2 * (i + (1 if offset else 0)) + 2)
                for k in range(HC):
                    in_product(i, HC + k, k, offset=offset, skip_free=first and k < RING)

            def body(i, first, last):
                for k in range(HC):
                    in_product(i, k, HC + k)
                if not last:
                    transposes(i + 1)
                pe.wait_ge(u_done, HC * (i + 1))
                for k in range(HC):
                    for half in range(2):
                        s = slice((half * HC + k) * P, (half * HC + k + 1) * P)
                        product(2 * HC + 2 * k + half, i, [((w["Wgh"][:, m, s], w["Wgl"][:, m, s]),
                                                            (Uh[:, m, :], Ul[:, m, :])) for m in range(HC)])
                if not last:
                    u_products(i, offset=USES)
                pe.wait_ge(gh_done, HC * (i + 1))
                if not first:
                    pe.wait_ge(resid_done, i)
                for t in range(TT):
                    for k in range(HC):
                        mm = pe.matmul(pO[:, t, :], GH[:, k, t * P:(t + 1) * P], w["Wo"][:, k, :],
                                       start=(k == 0), stop=(k == HC - 1))
                mm.then_inc(wo_done, 1)

            transposes(0)
            u_products(0, first=True)
            segments(pe, body)


GT = 4
LOOP = (2, NTILE // GT - 1)


def attention(nc, sb, ps, sem, c, dram):
    ident = c["ident"]
    WKh, WKl = (sb(n, [P, BATCH, DC, SC], F32R) for n in ("WKh", "WKl"))
    VWh, VWl = (sb(n, [P, BATCH, SCC, D], F32R) for n in ("VWh", "VWl"))
    stage = sb("stage", [P, 2 * BATCH, SCC * D], F32)
    pieces = [(n, b) for b in range(BATCH) for n in ("wk", "vw")]
    XA, XN, R = (sb(n, [P, 2, D], F32) for n in ("XA", "XN1", "R1"))
    XTh, XTl = (sb(n, [P, 2, DC, P], F32R) for n in ("X1Th", "X1Tl"))
    X2, X3 = sb("X2", [P, 2, D], F32), sb("X3", [P, 2, D], F32)
    X3T = sb("X3T", [P, DC, P], F32)
    E = sb("E", [P, 2, SCP], F32)
    PTh, PTl = (sb(n, [P, SCC, P], F32R) for n in ("PTh", "PTl"))
    mx, den = sb("mx", [P, HEADS], F32), sb("den", [P, HEADS], F32)
    st1, mv1, rs1, nm1 = (sb(n, [P, k], F32) for n, k in (("st1", 6), ("mv1", 2), ("rs1", 1), ("nm1", 1)))
    st3, mv3, rs3, nm3 = (sb(n, [P, k], F32) for n, k in (("st3", 6), ("mv3", 2), ("rs3", 1), ("nm3", 1)))
    Wg, bg = sb("Wgate", [P, DC, NE], F32), sb("bgate", [P, NE], F32)
    lg, sco, eq, prod = (sb(n, [P, GT, NE], F32) for n in ("lg", "sco", "eq", "prod"))
    oh, seen, ohs = sb("oh", [P, GT, NE], BF16), sb("seen", [P, NE], BF16), sb("ohs", [P, NE], F32)
    lmax, rden, first, pos, keep, place, away, spill = (
        sb(n, [P, GT], F32) for n in ("lmax", "rden", "first", "pos", "keep", "place", "away", "spill"))
    pair = sb("pair", [P, GT, 2], F32)
    SI = sb("SI", [P, GT], U32)
    pT, pS = ps("pT1", [P, DC, P]), ps("pS", [P, 2, 512])
    pP, pY = ps("pP", [P, 2, 4, P]), ps("pY", [P, D])
    pT3, pL = ps("pT3", [P, DC, P]), ps("pL", [P, 512])
    pLog = pL[:, 0:GT * NE].rearrange("p (t e) -> p t e", t=GT)
    pCnt = pL[:, GT * NE:2 * GT * NE].rearrange("p (t e) -> p t e", t=GT)

    piece_landed = [sem(f"piece_landed{n}") for n in range(2 * BATCH)]
    whi_done, wlo_done, g_landed, init = sem("whi_done"), sem("wlo_done"), sem("g_landed"), sem("init")
    xa_landed, r_landed = ([sem(f"{n}{k}") for k in range(2)] for n in ("xa_landed", "r1_landed"))
    x2_stored, x3_stored = ([sem(f"{n}{k}") for k in range(2)] for n in ("x2_stored", "x3_stored"))
    ln1_step, ln1_pow, ln1_done = sem("ln1_step"), sem("ln1_pow"), sem("ln1_done")
    ln3_step, ln3_pow, ln3_done = sem("ln3_step"), sem("ln3_pow"), sem("ln3_done")
    xT_done, xhi_done, xlo_done, score_done = (sem(n) for n in ("x1T_done", "x1hi_done", "x1lo_done", "score_done"))
    max_done, sub_done, exp_done, soft_step, prob_done = (
        sem(n) for n in ("max_done", "sub_done", "exp_done", "soft_step", "prob_done"))
    pt_done, phi_done, plo_done, y_done, x2_done = (sem(n) for n in ("pt_done", "phi_done", "plo_done", "y_done", "x2_done"))
    x3T_done, x3T_copied, logit_done = sem("x3T_done"), sem("x3T_copied"), sem("logit_done")
    route_dve, route_pool, route_exp, count_done = (sem(n) for n in ("route_dve", "route_pool", "route_exp", "count_done"))
    scattered, passed, pool_passed = sem("scattered"), sem("passed"), sem("pool_passed")
    RD, RP = 12, 13

    tiles = {n: dram[n].rearrange("(n p) d -> n p d", p=P) for n in ("x1", "x2", "x3", "out")}

    def num(t):
        return GT * t[0] + t[1]

    def uses(t, ring):
        return GT // ring * t[0] + t[1] // ring + 1

    def real(t):
        return not isinstance(t[0], int) or 0 <= num(t) < NTILE

    def group_real(g):
        return not isinstance(g, int) or 0 <= g < NTILE // GT

    def rows(name, t):
        n = num(t)
        return tiles[name][n] if isinstance(n, int) else tiles[name][bass.ds(n, 1)].rearrange("o p d -> p (o d)")

    def wait(eng, s, value):
        if not isinstance(value, int) or value > 0:
            eng.wait_ge(s, value)

    def pipeline(eng, step, end):
        for j in range(1, GT):
            step(-1, j)
        for g in range(0, LOOP[0]):
            for j in range(GT):
                step(g, j)
        with eng.Fori(*LOOP) as g:
            for j in range(GT):
                step(g, j)
        for n in range(GT * LOOP[1], NTILE + end):
            step(n // GT, n % GT)

    with nc.Block() as block:
        @block.sync
        def _(sp):
            for n, (name, b) in enumerate(pieces):
                src = dram["wk"][:, b, :, :] if name == "wk" else dram["vw"][b].rearrange("(c p) d -> p c d", p=P)
                k, m = (DC, SC) if name == "wk" else (SCC, D)
                sp.dma_start(stage[:, n, 0:k * m].rearrange("p (k m) -> p k m", k=k), src).then_inc(piece_landed[n], 16)
                if n == 0:
                    for t in ((0, 0), (0, 1)):
                        sp.dma_start(XA[:, t[1], :], rows("x1", t)).then_inc(xa_landed[t[1]], 16)
                    sp.dma_start(Wg[:, :, :], dram["Wgate"]).then_inc(g_landed, 16)
                    sp.dma_start(bg[:, :], dram["bgate"].partition_broadcast(P)).then_inc(g_landed, 16)

            def step(g, j):
                t = (g, j - 3)
                if real(t):
                    sp.wait_ge(ln3_done, num(t) + 1)
                    q = t[1] % 2
                    sp.dma_start(rows("x2", t), X2[:, q, :]).then_inc(x2_stored[q], 16)
                    sp.dma_start(rows("out", t), X2[:, q, :]).then_inc(x2_stored[q], 16)
                    sp.dma_start(rows("x3", t), X3[:, q, :]).then_inc(x3_stored[q], 16)
                t = (g, j + 4)
                if real(t) and not (isinstance(g, int) and num(t) < 2):
                    sp.wait_ge(ln1_done, num(t) - 1)
                    sp.dma_start(XA[:, t[1] % 2, :], rows("x1", t)).then_inc(xa_landed[t[1] % 2], 16)
                t = (g, j)
                if real(t):
                    wait(sp, x2_done, num(t) - 1)
                    sp.dma_start(R[:, t[1] % 2, :], rows("x1", t)).then_inc(r_landed[t[1] % 2], 16)

            pipeline(sp, step, 3)
            for q in range(2):
                sp.wait_ge(x2_stored[q], 32 * NTILE // 2)
                sp.wait_ge(x3_stored[q], 16 * NTILE // 2)

        @block.gpsimd
        def _(pool):
            half = c["mhalf"][:, 0:1]

            def deviation(t, step, done, mv, rs, nm, power):
                n = num(t)
                wait(pool, done, n)
                pool.wait_ge(step, 3 * n + 3)
                pool.tensor_tensor(rs[:, :], mv[:, 1:2], half, ALU.pow).then_inc(power, 1)
                wait_apart(pool, power, 2 * n + 1, pool_passed)
                pool.tensor_scalar(nm[:, :], mv[:, 0:1], rs[:, 0:1], -1.0, ALU.mult, ALU.mult).then_inc(power, 1)

            def probabilities(t):
                e = E[:, t[1] % 2, 0:SC].rearrange("p (h j) -> p h j", h=HEADS)
                pool.wait_ge(soft_step, 2 * num(t) + 2)
                pool.tensor_tensor(e, e, den[:, :].unsqueeze(2).to_broadcast([P, HEADS, NKV]), ALU.mult).then_inc(prob_done, 1)

            def over_experts(v):
                return v.unsqueeze(2).to_broadcast([P, GT, NE])

            def route_1(g):
                pool.wait_ge(route_dve, RD * g + 2)
                pool.tensor_tensor(lg[:, :, :], lg[:, :, :], over_experts(lmax[:, :]), ALU.subtract).then_inc(route_pool, 1)

            def route_2(g):
                pool.wait_ge(route_dve, RD * g + 4)
                pool.tensor_tensor(sco[:, :, :], sco[:, :, :], over_experts(rden[:, :]), ALU.mult).then_inc(route_pool, 1)

            def route_3(g):
                pool.wait_ge(route_dve, RD * g + 6)
                pool.tensor_tensor(eq[:, :, :], eq[:, :, :], c["iota16"][:, :].unsqueeze(1).to_broadcast([P, GT, NE]),
                                   ALU.mult).then_inc(route_pool, 1)

            def route_4(g):
                def step(k, ins):
                    ins.then_inc(route_pool, 1)
                    wait_apart(pool, route_pool, RP * g + k, pool_passed)
                wait_apart(pool, route_dve, RD * g + RD, pool_passed)
                step(4, pool.tensor_scalar(keep[:, :], pos[:, :], float(CAP), None, ALU.is_lt))
                step(5, pool.tensor_scalar(place[:, :], first[:, :], float(CAP), float(NE * CAP), ALU.mult, ALU.add))
                step(6, pool.tensor_tensor(place[:, :], place[:, :], pos[:, :], ALU.add))
                step(7, pool.tensor_tensor(away[:, :], place[:, :], spill[:, :], ALU.subtract))
                step(8, pool.tensor_tensor(away[:, :], away[:, :], keep[:, :], ALU.mult))
                step(9, pool.tensor_tensor(away[:, :], away[:, :], spill[:, :], ALU.add))
                if not (isinstance(g, int) and g == 0):
                    wait_apart(pool, scattered, 16 * GT * g, pool_passed)
                step(10, pool.tensor_copy(SI[:, :], away[:, :]))
                step(11, pool.tensor_scalar(pair[:, :, 0], spill[:, :], 1.0, -float(SLOTS + 1), ALU.mult, ALU.add))
                step(12, pool.tensor_copy(pair[:, :, 1], lmax[:, :]))
                step(13, pool.tensor_scalar(spill[:, :], spill[:, :], 1.0, float(GT * P), ALU.mult, ALU.add))
                for n in range(GT):
                    pool.indirect_dma_start(out=dram["slotmap"], out_offset=bass.IndirectOffsetOnAxis(SI[:, n:n + 1], 0),
                                            in_=pair[:, n, :], in_offset=None).then_inc(scattered, 16)

            def step(g, j):
                if j == 0 and group_real(g - 2):
                    route_2(g - 2)
                if real((g, j + 3)):
                    deviation((g, j + 3), ln1_step, ln1_done, mv1, rs1, nm1, ln1_pow)
                if j == 0 and group_real(g - 2):
                    route_3(g - 2)
                if real((g, j)):
                    probabilities((g, j))
                if real((g, j - 2)):
                    deviation((g, j - 2), ln3_step, ln3_done, mv3, rs3, nm3, ln3_pow)
                if j == 3 and group_real(g - 1):
                    route_1(g - 1)
                if j == 2 and group_real(g - 2):
                    route_4(g - 2)

            pool.memset(seen[:, :], 0.0).then_inc(init, 1)
            pool.memset(E[:, :, SC:SC + 1], 1.0).then_inc(init, 1)
            pool.memset(E[:, :, SC + 1:SCP], 0.0).then_inc(init, 1)
            for n in range(GT):
                pool.tensor_scalar(spill[:, n:n + 1], c["iotap"][:, :], 1.0, float(SLOTS + 1 + P * n), ALU.mult, ALU.add)\
                    .then_inc(init, 1)
            pool.wait_ge(init, 3 + GT)
            pipeline(pool, step, 2 * GT)
            pool.wait_ge(scattered, 16 * NTILE)

        @block.scalar
        def _(act):
            def step(g, j):
                t = (g, j - 1)
                if real(t):
                    n = num(t)
                    act.wait_ge(pt_done, n + 1)
                    wait(act, y_done, n)
                    act.activation(PTh[:, 0:4, :], pP[:, 0, :, :], ACT.Copy).then_inc(phi_done, 1)
                    act.activation(PTh[:, 4:SCC, :], pP[:, 1, 0:SCC - 4, :], ACT.Copy).then_inc(phi_done, 1)
                t = (g, j)
                if real(t):
                    e = E[:, t[1] % 2, 0:SC]
                    act.wait_ge(sub_done, num(t) + 1)
                    act.activation(e, e, ACT.Exp, scale=SCALE).then_inc(exp_done, 1)
                t = (g, j - 3)
                if real(t):
                    act.wait_ge(x3T_done, num(t) + 1)
                    wait(act, logit_done, num(t))
                    act.activation(X3T[:, :, :], pT3[:, :, :], ACT.Copy).then_inc(x3T_copied, 1)
                t = (g, j + 3)
                if real(t):
                    n = num(t)
                    act.wait_ge(ln1_pow, 2 * n + 2)
                    wait(act, xT_done, n - 1)
                    act.activation(XN[:, t[1] % 2, :], XA[:, t[1] % 2, :], ACT.Identity, bias=nm1[:, 0:1],
                                   scale=rs1[:, 0:1]).then_inc(ln1_done, 1)
                t = (g, j + 2)
                if real(t):
                    n = num(t)
                    act.wait_ge(xT_done, n + 1)
                    wait(act, score_done, n - 1)
                    act.activation(XTh[:, t[1] % 2, :, :], pT[:, :, :], ACT.Copy).then_inc(xhi_done, 1)
                t = (g, j - 2)
                if real(t):
                    n = num(t)
                    act.wait_ge(ln3_pow, 2 * n + 2)
                    wait(act, x3T_done, n - 1)
                    if n_uses(t) is not None:
                        act.wait_ge(x3_stored[t[1] % 2], 16 * n_uses(t))
                    act.activation(X3[:, t[1] % 2, :], X2[:, t[1] % 2, :], ACT.Identity, bias=nm3[:, 0:1],
                                   scale=rs3[:, 0:1]).then_inc(ln3_done, 1)
                if j == 3 and group_real(g - 1):
                    act.wait_ge(route_pool, RP * (g - 1) + 1)
                    act.activation(sco[:, :, :], lg[:, :, :], ACT.Exp).then_inc(route_exp, 1)

            def n_uses(t):
                n = uses(t, 2) - 1
                return None if isinstance(n, int) and n <= 0 else n

            for n, (name, b) in enumerate(pieces):
                act.wait_ge(piece_landed[n], 16)
                hi = (WKh[:, b, :, :] if name == "wk" else VWh[:, b, :, :])
                k, m = (DC, SC) if name == "wk" else (SCC, D)
                act.activation(hi, stage[:, n, 0:k * m].rearrange("p (k m) -> p k m", k=k), ACT.Copy).then_inc(whi_done, 1)
            pipeline(act, step, 3 + GT - 3)

        @block.vector
        def _(dve):
            mx_v = mx[:, :].rearrange("p (g h) -> p g h", g=2)
            s_v = pS[:, :, 0:HG * NKV].rearrange("p g (h j) -> p g h j", h=HG)

            def stats(src, ready, value, st, mv, step, n):
                dve.wait_ge(ready, value)
                dve.bn_stats(st[:, :], src).then_inc(step, 1)

            def aggregate(st, mv, step, power, n):
                wait(dve, power, 2 * n)
                wait_apart(dve, step, 3 * n + 1, passed)
                dve.bn_aggr(mv[:, :], st[:, :]).then_inc(step, 1)

            def add_eps(mv, step, n):
                dve.wait_ge(step, 3 * n + 2)
                dve.tensor_scalar(mv[:, 1:2], mv[:, 1:2], EPS, None, ALU.add).then_inc(step, 1)

            def over_experts(v):
                return v.unsqueeze(2).to_broadcast([P, GT, NE])

            def route_1(g):
                dve.wait_ge(logit_done, GT * g + GT)
                dve.tensor_tensor(lg[:, :, :], pLog, bg[:, :].unsqueeze(1).to_broadcast([P, GT, NE]), ALU.add).then_inc(route_dve, 1)
                dve.wait_ge(route_dve, RD * g + 1)
                if not (isinstance(g, int) and g == 0):
                    dve.wait_ge(route_pool, RP * g)
                dve.tensor_reduce(lmax[:, :], lg[:, :, :], AX.X, ALU.max).then_inc(route_dve, 1)

            def route_2(g):
                dve.wait_ge(route_exp, g + 1)
                dve.tensor_reduce(rden[:, :], sco[:, :, :], AX.X, ALU.add).then_inc(route_dve, 1)
                dve.wait_ge(route_dve, RD * g + 3)
                dve.reciprocal(rden[:, :], rden[:, :]).then_inc(route_dve, 1)

            def route_3(g):
                dve.wait_ge(route_pool, RP * g + 2)
                dve.tensor_reduce(lmax[:, :], sco[:, :, :], AX.X, ALU.max).then_inc(route_dve, 1)
                dve.wait_ge(route_dve, RD * g + 5)
                dve.tensor_tensor(eq[:, :, :], sco[:, :, :], over_experts(lmax[:, :]), ALU.is_equal).then_inc(route_dve, 1)

            def route_4(g):
                dve.wait_ge(route_pool, RP * g + 3)
                dve.tensor_reduce(first[:, :], eq[:, :, :], AX.X, ALU.min).then_inc(route_dve, 1)
                dve.wait_ge(route_dve, RD * g + 7)
                dve.tensor_tensor(oh[:, :, :], c["iota16"][:, :].unsqueeze(1).to_broadcast([P, GT, NE]),
                                  over_experts(first[:, :]), ALU.is_equal).then_inc(route_dve, 1)
                dve.wait_ge(route_dve, RD * g + 8)
                dve.tensor_reduce(ohs[:, :], oh[:, :, :].rearrange("p t e -> p e t"), AX.X, ALU.add).then_inc(route_dve, 1)

            def route_5(g):
                dve.wait_ge(count_done, g + 1)
                dve.tensor_tensor(prod[:, :, :], pCnt, oh[:, :, :], ALU.mult).then_inc(route_dve, 1)
                dve.tensor_tensor(seen[:, :], seen[:, :], ohs[:, :], ALU.add).then_inc(route_dve, 1)
                dve.wait_ge(route_dve, RD * g + 11)
                dve.tensor_reduce(pos[:, :], prod[:, :, :], AX.X, ALU.add).then_inc(route_dve, 1)

            def step(g, j):
                t = (g, j - 2)
                if real(t):
                    n, q = num(t), t[1] % 2
                    dve.wait_ge(y_done, n + 1)
                    dve.wait_ge(r_landed[q], 16 * uses(t, 2))
                    before = uses(t, 2) - 1
                    if not isinstance(before, int) or before > 0:
                        dve.wait_ge(x2_stored[q], 32 * before)
                    dve.tensor_tensor(X2[:, q, :], pY[:, :], R[:, q, :], ALU.add).then_inc(x2_done, 1)
                if j == 0 and group_real(g - 2):
                    route_3(g - 2)
                t = (g, j)
                if real(t):
                    n, q = num(t), t[1] % 2
                    dve.wait_ge(score_done, n + 1)
                    dve.tensor_reduce(mx_v, s_v, AX.X, ALU.max).then_inc(max_done, 1)
                if real((g, j + 3)):
                    m = (g, j + 3)
                    stats(XA[:, m[1] % 2, :], xa_landed[m[1] % 2], 16 * uses(m, 2), st1, mv1, ln1_step, num(m))
                if real(t):
                    dve.wait_ge(max_done, n + 1)
                    wait(dve, pt_done, n - 1)
                    dve.tensor_tensor(E[:, q, 0:SC].rearrange("p (g h j) -> p g h j", g=2, h=HG), s_v,
                                      mx_v.unsqueeze(3).to_broadcast([P, 2, HG, NKV]), ALU.subtract).then_inc(sub_done, 1)
                if real((g, j + 3)):
                    aggregate(st1, mv1, ln1_step, ln1_pow, num((g, j + 3)))
                t = (g, j - 2)
                if real(t):
                    stats(X2[:, t[1] % 2, :], x2_done, num(t) + 1, st3, mv3, ln3_step, num(t))
                if real((g, j + 3)):
                    add_eps(mv1, ln1_step, num((g, j + 3)))
                if real(t):
                    aggregate(st3, mv3, ln3_step, ln3_pow, num(t))
                if j == 3 and group_real(g - 1):
                    route_1(g - 1)
                t = (g, j - 1)
                if real(t):
                    n = num(t)
                    dve.wait_ge(phi_done, 2 * n + 2)
                    dve.tensor_tensor(PTl[:, 0:4, :], pP[:, 0, :, :], PTh[:, 0:4, :].bitcast(F32), ALU.subtract).then_inc(plo_done, 1)
                    dve.tensor_tensor(PTl[:, 4:SCC, :], pP[:, 1, 0:SCC - 4, :], PTh[:, 4:SCC, :].bitcast(F32),
                                      ALU.subtract).then_inc(plo_done, 1)
                if real((g, j - 2)):
                    add_eps(mv3, ln3_step, num((g, j - 2)))
                t = (g, j)
                if real(t):
                    n, q = num(t), t[1] % 2
                    dve.wait_ge(exp_done, n + 1)
                    wait(dve, prob_done, n)
                    dve.tensor_reduce(den[:, :], E[:, q, 0:SC].rearrange("p (h j) -> p h j", h=HEADS), AX.X,
                                      ALU.add).then_inc(soft_step, 1)
                    dve.wait_ge(soft_step, 2 * n + 1)
                    dve.reciprocal(den[:, :], den[:, :]).then_inc(soft_step, 1)
                if j == 0 and group_real(g - 2):
                    route_4(g - 2)
                if j == 1 and group_real(g - 2):
                    route_5(g - 2)
                t = (g, j + 2)
                if real(t):
                    n, q = num(t), t[1] % 2
                    dve.wait_ge(xhi_done, n + 1)
                    dve.tensor_tensor(XTl[:, q, :, :], pT[:, :, :], XTh[:, q, :, :].bitcast(F32), ALU.subtract).then_inc(xlo_done, 1)
                if j == 3 and group_real(g - 1):
                    route_2(g - 1)

            dve.wait_ge(init, 3 + GT)
            dve.wait_ge(g_landed, 32)
            for n, (name, b) in enumerate(pieces):
                dve.wait_ge(whi_done, n + 1)
                hi, lo = ((WKh, WKl) if name == "wk" else (VWh, VWl))
                k, m = (DC, SC) if name == "wk" else (SCC, D)
                dve.tensor_tensor(lo[:, b, :, :], stage[:, n, 0:k * m].rearrange("p (k m) -> p k m", k=k),
                                  hi[:, b, :, :].bitcast(F32), ALU.subtract).then_inc(wlo_done, 1)
            pipeline(dve, step, 2 + GT)

        @block.tensor
        def _(pe):
            def batch(t):
                n = num(t)
                return n // TILE_SEQ if isinstance(n, int) else pe.snap(n // TILE_SEQ)

            def of(v, b, k, s):
                return v[:, b, k, s] if isinstance(b, int) else v[:, bass.ds(b, 1), k, s].rearrange("p o n -> p (o n)")

            def step(g, j):
                t = (g, j - 1)
                if real(t):
                    n = num(t)
                    pe.wait_ge(prob_done, n + 1)
                    wait(pe, plo_done, 2 * n)
                    for k in range(SCC):
                        mm = pe.transpose(pP[:, k // 4, k % 4, :], E[:, t[1] % 2, k * P:(k + 1) * P], ident[:, :])
                    mm.then_inc(pt_done, 1)
                t = (g, j + 2)
                if real(t):
                    n = num(t)
                    pe.wait_ge(ln1_done, n + 1)
                    wait(pe, xlo_done, n)
                    for k in range(DC):
                        mm = pe.transpose(pT[:, k, :], XN[:, t[1] % 2, k * P:(k + 1) * P], ident[:, :])
                    mm.then_inc(xT_done, 1)
                t = (g, j - 3)
                if real(t):
                    n = num(t)
                    pe.wait_ge(ln3_done, n + 1)
                    wait(pe, x3T_copied, n)
                    for k in range(DC):
                        mm = pe.transpose(pT3[:, k, :], X3[:, t[1] % 2, k * P:(k + 1) * P], ident[:, :])
                    mm.then_inc(x3T_done, 1)
                t = (g, j + 1)
                if real(t):
                    n, q, b = num(t), t[1] % 2, batch(t)
                    pe.wait_ge(xlo_done, n + 1)
                    wait(pe, sub_done, n)
                    for h in range(2):
                        s = slice(h * HG * NKV, (h + 1) * HG * NKV)
                        mm = split(pe.matmul, pS[:, h, 0:HG * NKV],
                                   [((XTh[:, q, k, :], XTl[:, q, k, :]), (of(WKh, b, k, s), of(WKl, b, k, s)))
                                    for k in range(DC)])
                    mm.then_inc(score_done, 1)
                t = (g, j - 3)
                if real(t):
                    n = num(t)
                    pe.wait_ge(x3T_copied, n + 1)
                    if t[1] % GT == 0:
                        grp = g + (t[1] - t[1] % GT) // GT
                        wait(pe, route_dve, RD * (grp - 1) + 1)
                    if j == 2 and group_real(g - 2):
                        pe.wait_ge(route_dve, RD * (g - 2) + 10)
                    for k in range(DC):
                        mm = pe.matmul(pL[:, t[1] % GT * NE:(t[1] % GT + 1) * NE], X3T[:, k, :], Wg[:, k, :],
                                       start=(k == 0), stop=(k == DC - 1))
                    mm.then_inc(logit_done, 1)
                t = (g, j - 1)
                if real(t):
                    n, b = num(t), batch(t)
                    pe.wait_ge(plo_done, 2 * n + 2)
                    wait(pe, x2_done, n)
                    split(pe.matmul, pY[:, :], [((PTh[:, k, :], PTl[:, k, :]), (of(VWh, b, k, slice(0, D)), of(VWl, b, k, slice(0, D))))
                                                for k in range(SCC)]).then_inc(y_done, 1)
                if j == 1 and group_real(g - 2):
                    pe.wait_ge(route_dve, RD * (g - 2) + 9)
                    pe.matmul(pCnt, c["tri"][:, :], oh[:, :, :], start=True, stop=False)
                    pe.matmul(pCnt, c["ones"][:, :], seen[:, :].unsqueeze(1).to_broadcast([P, GT, NE]), start=False, stop=False)
                    for m in range(GT - 1):
                        mm = pe.matmul(pCnt[:, m + 1:GT, :], c["ones"][:, :],
                                       oh[:, m, :].unsqueeze(1).to_broadcast([P, GT - 1 - m, NE]), start=False, stop=(m == GT - 2))
                    mm.then_inc(count_done, 1)

            pe.wait_ge(wlo_done, 2 * BATCH)
            pipeline(pe, step, 2 + GT)


def experts(nc, sb, ps, sem, c, dram):
    ident = c["ident"]
    raw1, raw2 = (sb(n, [P, 2, 4, 512], F32) for n in ("raw1", "raw2"))
    W1h, W1l, W2h, W2l = (sb(n, [P, 2, 4, 512], F32R) for n in ("W1h", "W1l", "W2h", "W2l"))
    XE, X2E = (sb(n, [P, 2, ST, D], F32) for n in ("XE", "X2E"))
    XTh, XTl = (sb(n, [P, DC, CAP], F32R) for n in ("XEh", "XEl"))
    HR = sb("HR", [P, QC, CAP], F32)
    Hh, Hl = (sb(n, [P, 2, QC, CAP], F32R) for n in ("Hh", "Hl"))
    B1, B2 = sb("B1", [P, 2, HE // P], F32), sb("B2", [P, 2, D], F32)
    Y = sb("Y", [P, ST, D], F32)
    MP = sb("MP", [P, 2, ST, 2], F32)
    near = sb("near", [P, 2, ST], F32)
    GI, OI = sb("GI", [P, 2, ST], U32), sb("OI", [P, 2, ST], U32)
    pX = ps("pX", [P, DC, CAP])
    pH = ps("pH", [P, 2, QC, CAP])
    pY = ps("pYE", [P, ST, D])

    w1_landed, w2_landed, b_landed, mp_landed = ([sem(f"{n}{k}") for k in range(2)] for n in
                                                 ("w1_landed", "w2_landed", "b_landed", "mp_landed"))
    x_landed, x2_landed = ([sem(f"{n}{k}") for k in range(2)] for n in ("xe_landed", "x2e_landed"))
    idx_step, scattered, passed = sem("idx_step"), sem("y_scattered"), sem("passed")
    sp_passed = sem("sp_passed")
    w1hi, w1lo, w2hi, w2lo = (sem(n) for n in ("w1hi", "w1lo", "w2hi", "w2lo"))
    xT_done, xhi, xlo = sem("xeT_done"), sem("xehi"), sem("xelo")
    h_done, relu, hhi, hlo = sem("h_done"), sem("relu_done"), sem("hhi"), sem("hlo")
    w2_done, y_step, y_done = sem("w2_done"), sem("y_step"), sem("ye_done")

    w1_v = dram["W1"].rearrange("e (k p) (q h) -> e q p k h", p=P, q=NQ)
    w2_v = dram["W2"].rearrange("e (q k p) d -> e q p k d", p=P, q=NQ)
    map_v = dram["slotmap"][0:SLOTS, :].rearrange("(e t p) c -> e p t c", t=ST, p=P)
    IS = 3

    def wait(eng, s, value):
        if not isinstance(value, int) or value > 0:
            eng.wait_ge(s, value)

    def quarter(v, e, q):
        return v[e, q] if isinstance(e, int) else v[bass.ds(e, 1), q].rearrange("o p k h -> p (o k) h")

    def pairs(eng, body):
        for r in range(2):
            body(r, r, 0, False)
        with eng.Fori(1, NE // 2 - 1) as g:
            for r in range(2):
                body(2 * g + r, r, g, False)
        for r in range(2):
            body(NE - 2 + r, r, NE // 2 - 1, r == 1)

    with nc.Block() as block:
        @block.sync
        def _(sp):
            def load1(e, q):
                wait(sp, w1lo, NQ * e + q - 1)
                sp.dma_start(raw1[:, q % 2, :, :], quarter(w1_v, e, q)).then_inc(w1_landed[q % 2], 16)

            def load2(e, q):
                if isinstance(e, int):
                    wait(sp, w2lo, NQ * e + q - 1)
                else:
                    wait_apart(sp, w2lo, NQ * e + q - 1, sp_passed)
                sp.dma_start(raw2[:, q % 2, :, :], quarter(w2_v, e, q)).then_inc(w2_landed[q % 2], 16)

            def body(e, r, u, last):
                for q in range(NQ):
                    if q + 1 < NQ:
                        load1(e, q + 1)
                    elif not last:
                        load1(e + 1, 0)
                    load2(e, q)

            load1(0, 0)
            pairs(sp, body)

        @block.gpsimd
        def _(pool):
            def prepare(e, r, u):
                src = map_v[e] if isinstance(e, int) else map_v[bass.ds(e, 1)].rearrange("o p t c -> p (o t) c")
                wait(pool, y_done, e - 1)
                pool.dma_start(MP[:, r, :, :], src).then_inc(mp_landed[r], 16)
                pool.dma_start(B1[:, r, :], dram["b1"][e] if isinstance(e, int) else
                               dram["b1"][bass.ds(e, 1)].rearrange("o p k -> p (o k)")).then_inc(b_landed[r], 16)
                row = dram["b2"][e:e + 1, :] if isinstance(e, int) else dram["b2"][bass.ds(e, 1), :]
                pool.dma_start(B2[:, r, :], row.to_broadcast([P, D])).then_inc(b_landed[r], 16)
                wait(pool, scattered, 16 * ST * (e - 1))
                wait_apart(pool, mp_landed[r], 16 * u + 16, passed)
                pool.tensor_copy(OI[:, r, :], MP[:, r, :, 0]).then_inc(idx_step, 1)
                pool.tensor_scalar(near[:, r, :], MP[:, r, :, 0], float(TOK - 1), None, ALU.min).then_inc(idx_step, 1)
                wait_apart(pool, idx_step, IS * e + 2, passed)
                pool.tensor_copy(GI[:, r, :], near[:, r, :]).then_inc(idx_step, 1)
                wait(pool, xT_done, e - 1)
                wait_apart(pool, idx_step, IS * e + 3, passed)
                for src, dst, landed in (("x3", XE, x_landed), ("x2", X2E, x2_landed)):
                    for t in range(ST):
                        pool.indirect_dma_start(out=dst[:, r, t, :], out_offset=None, in_=dram[src],
                                                in_offset=bass.IndirectOffsetOnAxis(GI[:, r, t:t + 1], 0)).then_inc(landed[r], 16)

            def write(e, r):
                wait_apart(pool, y_done, e + 1, passed)
                for t in range(ST):
                    pool.indirect_dma_start(out=dram["out"], out_offset=bass.IndirectOffsetOnAxis(OI[:, r, t:t + 1], 0),
                                            in_=Y[:, t, :], in_offset=None, bounds_check=TOK - 1,
                                            oob_is_err=False).then_inc(scattered, 16)

            def body(e, r, u, last):
                if not last:
                    prepare(e + 1, 1 - r, u + r)
                write(e, r)

            prepare(0, 0, 0)
            pairs(pool, body)
            pool.wait_ge(scattered, 16 * ST * NE)

        @block.scalar
        def _(act):
            def w1_hi(e, q, u):
                act.wait_ge(w1_landed[q % 2], 16 * (NQ // 2 * e + q // 2 + 1))
                wait(act, h_done, NQ * e + q - 1)
                act.activation(W1h[:, q % 2, :, :], raw1[:, q % 2, :, :], ACT.Copy).then_inc(w1hi, 1)

            def w2_hi(e, q):
                act.wait_ge(w2_landed[q % 2], 16 * (NQ // 2 * e + q // 2 + 1))
                wait(act, w2_done, NQ * e + q - 1)
                act.activation(W2h[:, q % 2, :, :], raw2[:, q % 2, :, :], ACT.Copy).then_inc(w2hi, 1)

            def x_hi(e):
                act.wait_ge(xT_done, e + 1)
                wait(act, h_done, NQ * e)
                for b in range(2):
                    act.activation(XTh[:, 2 * b:2 * b + 2, :], pX[:, 2 * b:2 * b + 2, :], ACT.Copy).then_inc(xhi, 1)

            def body(e, r, u, last):
                for q in range(NQ):
                    if q + 1 < NQ:
                        w1_hi(e, q + 1, u)
                    elif not last:
                        w1_hi(e + 1, 0, u)
                    act.wait_ge(h_done, NQ * e + q + 1)
                    act.wait_ge(b_landed[r], 32 * u + 32)
                    wait(act, hlo, NQ * e + q)
                    for k in range(QC):
                        act.activation(HR[:, k, :], pH[:, q % 2, k, :], ACT.Relu,
                                       bias=B1[:, r, q * QC + k:q * QC + k + 1]).then_inc(relu, 1)
                    act.wait_ge(relu, QC * (NQ * e + q + 1))
                    wait(act, w2_done, NQ * e + q - 1)
                    act.activation(Hh[:, q % 2, :, :], HR[:, :, :], ACT.Copy).then_inc(hhi, 1)
                    w2_hi(e, q)
                if not last:
                    x_hi(e + 1)

            x_hi(0)
            w1_hi(0, 0, 0)
            pairs(act, body)

        @block.vector
        def _(dve):
            def w1_lo(e, q):
                dve.wait_ge(w1hi, NQ * e + q + 1)
                dve.tensor_tensor(W1l[:, q % 2, :, :], raw1[:, q % 2, :, :], W1h[:, q % 2, :, :].bitcast(F32),
                                  ALU.subtract).then_inc(w1lo, 1)

            def x_lo(e):
                for b in range(2):
                    dve.wait_ge(xhi, 2 * e + b + 1)
                    dve.tensor_tensor(XTl[:, 2 * b:2 * b + 2, :], pX[:, 2 * b:2 * b + 2, :],
                                      XTh[:, 2 * b:2 * b + 2, :].bitcast(F32), ALU.subtract).then_inc(xlo, 1)

            def finish(e, r, u):
                dve.wait_ge(w2_done, NQ * e + NQ)
                dve.wait_ge(b_landed[r], 32 * u + 32)
                wait(dve, scattered, 16 * ST * e)
                for t in range(ST):
                    dve.tensor_tensor(Y[:, t, :], pY[:, t, :], B2[:, r, :], ALU.add).then_inc(y_step, 1)
                dve.wait_ge(x2_landed[r], 16 * ST * (u + 1))
                dve.wait_ge(mp_landed[r], 16 * u + 16)
                for t in range(ST):
                    dve.wait_ge(y_step, ST * e + t + 1)
                    ins = dve.scalar_tensor_tensor(out=Y[:, t, :], in0=Y[:, t, :], scalar=MP[:, r, t, 1:2],
                                                   in1=X2E[:, r, t, :], op0=ALU.mult, op1=ALU.add)
                ins.then_inc(y_done, 1)

            def body(e, r, u, last):
                for q in range(NQ):
                    if q + 1 < NQ:
                        w1_lo(e, q + 1)
                    elif not last:
                        w1_lo(e + 1, 0)
                    if q == 0 and not (isinstance(e, int) and e == 0):
                        finish(e - 1, 1 - r, u - 1 + r)
                    dve.wait_ge(hhi, NQ * e + q + 1)
                    dve.tensor_tensor(Hl[:, q % 2, :, :], HR[:, :, :], Hh[:, q % 2, :, :].bitcast(F32),
                                      ALU.subtract).then_inc(hlo, 1)
                    dve.wait_ge(w2hi, NQ * e + q + 1)
                    dve.tensor_tensor(W2l[:, q % 2, :, :], raw2[:, q % 2, :, :], W2h[:, q % 2, :, :].bitcast(F32),
                                      ALU.subtract).then_inc(w2lo, 1)
                if not last:
                    x_lo(e + 1)

            x_lo(0)
            w1_lo(0, 0)
            pairs(dve, body)
            finish(NE - 1, 1, NE // 2 - 1)

        @block.tensor
        def _(pe):
            def transposes(e, r, u):
                pe.wait_ge(x_landed[r], 16 * ST * (u + 1))
                wait(pe, xlo, 2 * e)
                for k in range(DC):
                    for t in range(ST):
                        mm = pe.transpose(pX[:, k, t * P:(t + 1) * P], XE[:, r, t, k * P:(k + 1) * P], ident[:, :])
                mm.then_inc(xT_done, 1)

            def first_product(e, q):
                pe.wait_ge(w1lo, NQ * e + q + 1)
                if q == 0:
                    pe.wait_ge(xlo, 2 * e + 2)
                wait(pe, relu, QC * (NQ * e + q - 1))
                for m in range(QC):
                    s = slice(m * P, (m + 1) * P)
                    mm = split(pe.matmul, pH[:, q % 2, m, :], [((W1h[:, q % 2, k, s], W1l[:, q % 2, k, s]), (XTh[:, k, :], XTl[:, k, :]))
                                                               for k in range(DC)])
                mm.then_inc(h_done, 1)

            def second_product(e, q):
                pe.wait_ge(hlo, NQ * e + q + 1)
                pe.wait_ge(w2lo, NQ * e + q + 1)
                if q == 0:
                    wait(pe, y_step, ST * e)
                for t in range(ST):
                    s = slice(t * P, (t + 1) * P)
                    mm = split(pe.matmul, pY[:, t, :], [((Hh[:, q % 2, k, s], Hl[:, q % 2, k, s]), (W2h[:, q % 2, k, :], W2l[:, q % 2, k, :]))
                                                        for k in range(QC)], start=(q == 0), stop=(q == NQ - 1))
                mm.then_inc(w2_done, 1)

            def body(e, r, u, last):
                for q in range(NQ):
                    first_product(e, q)
                    if q:
                        second_product(e, q - 1)
                if not last:
                    transposes(e + 1, 1 - r, u + r)
                second_product(e, NQ - 1)

            transposes(0, 0, 0)
            pairs(pe, body)


def build(nc, dram):
    with ExitStack() as top:
        def alloc(stack):
            def sb(name, shape, dt):
                return stack.enter_context(nc.sbuf_tensor(name, shape, dt))

            def ps(name, shape, dt=F32):
                return stack.enter_context(nc.psum_tensor(name, shape, dt))

            def sem(name):
                return stack.enter_context(nc.semaphore(name))
            return sb, ps, sem

        sb, _, sem = alloc(top)
        c = constants(nc, sb, sem)
        with ExitStack() as part:
            sb, ps, sem = alloc(part)
            w = {n: sb(n, [P, k, 2 * HID], F32R) for n, k in (("Wih", DC), ("Wil", DC), ("Wgh", HC), ("Wgl", HC))}
            w["Wo"] = sb("Wo_sb", [P, HC, D], F32)
            small = {"fb": sb("fb", [P, HC], F32), "conv_w": sb("conv_w", [P, HC * TAPS], F32),
                     "conv_b": sb("conv_b", [P, HC], F32), "bg": sb("bg", [P, 2 * HC], F32),
                     "hbg": sb("hbg", [P, 2 * HC], F32), "decay": sb("decay", [P, HC], F32),
                     "one_eps": sb("one_eps", [P, 1], F32), "work": sb("work", [P, 5, HC], F32)}
            with ExitStack() as staging:
                prepare(nc, *alloc(staging), w, dram, small)
            recurrence(nc, sb, ps, sem, c, w, dram, small)
        with ExitStack() as part:
            attention(nc, *alloc(part), c, dram)
        with ExitStack() as part:
            experts(nc, *alloc(part), c, dram)


SCRATCH = {"x1": [TOK, D], "x2": [TOK, D], "x3": [TOK, D],
           "wk": [P, BATCH, DC, SC], "vw": [BATCH, SCP, D],
           "slotmap": [SLOTS + 1 + TOK, 2]}


def layout(i):
    import numpy as np

    def chunks(a):
        return np.ascontiguousarray(a.reshape(a.shape[0] // P, P, a.shape[1]).transpose(1, 0, 2))

    def columns(a):
        return np.ascontiguousarray(a.reshape(-1, P).T)

    return {
        "x": i["x"].reshape(TOK, D),
        "Wi": chunks(i["L0_attn_Wi"].T), "Wg": chunks(i["L0_attn_Wg"].T), "Wo": chunks(i["L0_attn_Wo"].T),
        "conv_w": np.ascontiguousarray(i["L0_attn_conv_w"].reshape(HC, P, TAPS).transpose(1, 0, 2).reshape(P, HC * TAPS)),
        "conv_b": columns(i["L0_attn_conv_b"]), "bg": columns(i["L0_attn_bg"]), "fb": columns(i["L0_attn_forget_base"]),
        "ctxT": np.ascontiguousarray(i["ctx_768"].reshape(BATCH * NKV, CC, P).transpose(2, 1, 0)),
        "Wk": chunks(i["L0_xattn_Wk"]), "Wv": chunks(i["L0_xattn_Wv"]),
        "WqT": chunks(i["L0_xattn_Wq"].T), "xWo": chunks(i["L0_xattn_Wo"]),
        "bo": i["L0_xattn_bo"].reshape(1, D),
        "Wgate": chunks(i["L0_ffn_Wg"]), "bgate": i["L0_ffn_bg"],
        "W1": i["L0_ffn_W1"], "W2": i["L0_ffn_W2"],
        "b1": np.ascontiguousarray(i["L0_ffn_b1"].reshape(NE, HE // P, P).transpose(0, 2, 1)), "b2": i["L0_ffn_b2"],
    }


def kernel(**inputs):
    import numpy as _np
    import concourse.bacc as _bacc
    from concourse import mybir as _mybir
    from concourse.bass_utils import run_bass_kernel_spmd as _run

    nc = _bacc.Bacc("TRN2", target_bir_lowering=False, num_devices=1)
    arrays, dram = {}, {}
    for name, a in layout({k: _np.asarray(v) for k, v in inputs.items()}).items():
        a = _np.ascontiguousarray(a)
        arrays[f"in_{name}"] = a
        dram[name] = nc.dram_tensor(f"in_{name}", a.shape, _mybir.dt.from_np(a.dtype), kind="ExternalInput").ap()
    for name, shape in SCRATCH.items():
        dram[name] = nc.dram_tensor(name, shape, F32, kind="Internal").ap()
    dram["out"] = nc.dram_tensor("out_dram", (TOK, D), F32, kind="ExternalOutput").ap()
    build(nc, dram)
    r = _run(nc, [arrays], core_ids=[0])
    return r.results[0]["out_dram"].reshape(BATCH, SEQ, D)
```

```python
from contextlib import ExitStack

import concourse.bass as bass
from concourse import mybir

F32 = mybir.dt.float32
F32R = mybir.dt.float32r
BF16 = mybir.dt.bfloat16
I32 = mybir.dt.int32
U32 = mybir.dt.uint32
ALU = mybir.AluOpType
ACT = mybir.ActivationFunctionType
AX = mybir.AxisListType

P = 128
BATCH, SEQ, D = 2, 2048, 512
TOK = BATCH * SEQ
HID, TAPS = 768, 4
DC, HC = D // P, HID // P
EPS = 1e-5

TB = 256
NBLK = TOK // TB
BLK_SEQ = SEQ // TB
TT = TB // P
RING = 4
USES = 4 * HC
WS = 3
GRP = 2

HEADS, DH, CTX, NKV = 8, 64, 384, 77
CC = CTX // P
HG = HEADS // 2
SC = HEADS * NKV
SCC = -(-(SC + 1) // P)
SCP = SCC * P
NTILE = TOK // P
TILE_SEQ = SEQ // P
SCALE = DH ** -0.5

NE, HE = 16, 2048
CAP = -(-TOK // NE)
SLOTS = NE * CAP
NQ = 4
QC = HE // NQ // P
ST = CAP // P


def split(mm, out, pairs, start=True, stop=True):
    n = len(pairs)
    for k, ((ah, al), (bh, bl)) in enumerate(pairs):
        mm(out, ah, bh, start=start and k == 0, stop=False)
        mm(out, ah, bl, start=False, stop=False)
        last = mm(out, al, bh, start=False, stop=stop and k == n - 1)
    return last


def wait_apart(eng, sem, value, passed):
    eng.wait_ge(sem, value)
    eng.sem_inc(passed, 1)


def constants(nc, sb, sem):
    c = {
        "ident": sb("ident", [P, P], F32), "tri": sb("tri", [P, P], BF16), "ones": sb("ones", [P, P], BF16),
        "iota16": sb("iota16", [P, NE], F32), "iotap": sb("iotap", [P, 1], F32),
        "mhalf": sb("mhalf", [P, TT], F32),
    }
    made = sem("constants_made")
    with nc.Block() as block:
        @block.gpsimd
        def _(pool):
            pool.memset(c["ident"][:, :], 0.0).then_inc(made, 1)
            pool.memset(c["tri"][:, :], 1.0).then_inc(made, 1)
            pool.memset(c["ones"][:, :], 1.0).then_inc(made, 1)
            pool.memset(c["mhalf"][:, :], -0.5).then_inc(made, 1)
            pool.wait_ge(made, 4)
            pool.affine_select(out=c["ident"][:, :], in_=c["ident"][:, :], compare_op=ALU.not_equal, fill=1.0,
                               base=0, pattern=[[-1, P]], channel_multiplier=1).then_inc(made, 1)
            pool.affine_select(out=c["tri"][:, :], in_=c["tri"][:, :], compare_op=ALU.is_gt, fill=0.0,
                               base=0, pattern=[[1, P]], channel_multiplier=-1).then_inc(made, 1)
            pool.iota(c["iota16"][:, :], pattern=[[1, NE]], base=-NE, channel_multiplier=0,
                      allow_small_or_imprecise_dtypes=True).then_inc(made, 1)
            pool.iota(c["iotap"][:, :], pattern=[[0, 1]], base=0, channel_multiplier=1,
                      allow_small_or_imprecise_dtypes=True).then_inc(made, 1)
            pool.wait_ge(made, 8)
    return c


def prepare(nc, sb, ps, sem, w, dram, small, X, x_landed):
    stage = sb("w_stage", [P, 2, 2 * HID], F32)
    landed = [sem("w_landed0"), sem("w_landed1")]
    hi_done, lo_done, small_landed, wo_landed = (sem(n) for n in ("w_hi_done", "w_lo_done", "small_landed", "wo_landed"))
    sp_step, sp_exp = sem("softplus_step"), sem("softplus_exp")
    jobs = [(dram["Wi"], w["Wih"], w["Wil"], k) for k in range(DC)] + \
           [(dram["Wg"], w["Wgh"], w["Wgl"], k) for k in range(HC)] + \
           [(dram["Wo"][:, 0:WS, :].rearrange("p (o k) d -> p o (k d)", o=1), w["Woh"], w["Wol"], 0)]
    fb, cw = small["fb"], small["work"]

    NJ = BATCH * NKV
    NP = HEADS // 2
    ctxT, Wkv = sb("ctxT", [P, CC, NJ], F32), sb("Wkv", [P, 2 * CC, D], F32)
    Wk, Wv = Wkv[:, 0:CC, :], Wkv[:, CC:2 * CC, :]
    WqT, Wo = sb("WqT", [P, NP, D], F32), sb("Wo2", [P, NP, D], F32)
    KT, VT = sb("KT", [P, HEADS, NJ], F32), sb("VT", [P, HEADS, NJ], F32)
    WKs = sb("WKs", [P, 2, BATCH, SC], F32)
    VWs = Wkv[0:NKV, :, :]
    zero = sb("zero", [SCP - SC - 1, D], F32)
    none = sb("none", [P, 2 * SLOTS // P], F32)
    pR = ps("pR", [P, 4, 512])
    in_landed = {n: sem(f"{n}_in") for n in ("ctxT", "Wk", "Wv", "WqT", "xWo")}
    zeroed, pads_stored, map_cleared = (sem(n) for n in ("zeroed", "pads_stored", "map_cleared"))
    halves_zeroed = sem("halves_zeroed")
    pe_done, evac, wk_evac, vw_evac = sem("pe_done"), sem("evac"), sem("wk_evac"), sem("vw_evac")
    wk_stored, vw_stored = ([sem(f"{n}_stored{b}") for b in range(k)] for n, k in (("wk", 2), ("vw", CC)))
    NK, NS, NV = 2 * NP, DC * HEADS, BATCH * HEADS
    vw = dram["vw"]

    with nc.Block() as block:
        @block.sync
        def _(sp):
            for t, n in ((ctxT, "ctxT"), (Wk, "Wk"), (Wv, "Wv")):
                sp.dma_start(t[:, :, :], dram[n]).then_inc(in_landed[n], 16)
            for n, (src, hi, lo, k) in enumerate(jobs):
                if n >= 2:
                    sp.wait_ge(lo_done, n - 1)
                m = src.shape[2]
                sp.dma_start(stage[:, n % 2, 0:m], src[:, k, :]).then_inc(landed[n % 2], 16)
                if n == 0:
                    for name in ("fb", "conv_w", "conv_b", "bg"):
                        sp.dma_start(small[name][:, :], dram[name]).then_inc(small_landed, 16)
                    for t, nm in ((WqT, "WqT"), (Wo, "xWo")):
                        sp.dma_start(t[:, :, :], dram[nm]).then_inc(in_landed[nm], 16)
            sp.dma_start(X[:, :, :], dram["x"][0:TB, :].rearrange("(t p) d -> p t d", p=P)).then_inc(x_landed, 16)
            sp.dma_start(w["Wo"][:, :, :], dram["Wo"][:, WS:HC, :]).then_inc(wo_landed, 16)
            sp.wait_ge(wo_landed, 16)

        @block.gpsimd
        def _(pool):
            pool.memset(zero[:, :], 0.0).then_inc(zeroed, 1)
            pool.memset(none[:, :], 2.0 * TOK).then_inc(zeroed, 1)
            pool.wait_ge(zeroed, 2)
            pool.dma_start(dram["slotmap"][0:SLOTS, :].rearrange("(p r) c -> p (r c)", p=P), none[:, :]).then_inc(map_cleared, 16)
            for b in range(BATCH):
                pool.dma_start(vw[b, SC + 1:SCP, :], zero[:, :]).then_inc(pads_stored, 16)
                pool.dma_start(vw[b, SC:SC + 1, :], dram["bo"]).then_inc(pads_stored, 16)
            for k in range(DC):
                pool.wait_ge(wk_evac, HEADS * (k + 1))
                pool.dma_start(dram["wk"][:, :, k, :], WKs[:, k % 2, :, :]).then_inc(wk_stored[k % 2], 16)
            for n in range(NV // 2):
                b, h = 2 * n // HEADS, 2 * n % HEADS
                pool.wait_ge(vw_evac, 2 * (n + 1))
                pool.dma_start(vw[b, h * NKV:(h + 2) * NKV, :].rearrange("(h j) d -> j h d", h=2),
                               VWs[:, 2 * (n % CC):2 * (n % CC) + 2, :]).then_inc(vw_stored[n % CC], 16)
            pool.wait_ge(map_cleared, 16)
            pool.wait_ge(pads_stored, 32 * BATCH)
            for r in range(2):
                pool.wait_ge(wk_stored[r], 16 * DC // 2)
            for r in range(CC):
                pool.wait_ge(vw_stored[r], 16 * ((NV // 2 - r + CC - 1) // CC))

        @block.tensor
        def _(pe):
            use = 0

            def begin():
                if use - 3 > NK + NS:
                    pe.wait_ge(vw_evac, use - 3 - NK - NS)
                elif use - 3 > NK:
                    pe.wait_ge(wk_evac, use - 3 - NK)
                elif use >= 4:
                    pe.wait_ge(evac, use - 3)

            pe.wait_ge(in_landed["ctxT"], 16)
            for src, name in ((Wk, "Wk"), (Wv, "Wv")):
                pe.wait_ge(in_landed[name], 16)
                for h in range(NP):
                    begin()
                    for k in range(CC):
                        mm = pe.matmul(pR[:, use % 4, 0:NJ], src[:, k, h * P:(h + 1) * P], ctxT[:, k, :],
                                       start=(k == 0), stop=(k == CC - 1))
                    mm.then_inc(pe_done, 1)
                    use += 1
            pe.wait_ge(in_landed["WqT"], 16)
            pe.wait_ge(evac, NK)
            pe.wait_ge(halves_zeroed, 4)
            for k in range(DC):
                for h in range(HEADS):
                    begin()
                    pe.matmul(pR[:, use % 4, 0:NJ], WqT[:, h // 2, k * P:(k + 1) * P], KT[:, h, :],
                              start=True, stop=True).then_inc(pe_done, 1)
                    use += 1
            pe.wait_ge(in_landed["xWo"], 16)
            for b in range(BATCH):
                for h in range(HEADS):
                    begin()
                    pe.matmul(pR[0:NKV, use % 4, :], VT[:, h, b * NKV:(b + 1) * NKV], Wo[:, h // 2, :],
                              start=True, stop=True).then_inc(pe_done, 1)
                    use += 1

        @block.scalar
        def _(act):
            act.wait_ge(small_landed, 64)
            act.activation(cw[:, 0, :], fb[:, :], ACT.Abs).then_inc(sp_exp, 1)
            act.wait_ge(sp_exp, 1)
            act.activation(cw[:, 1, :], cw[:, 0, :], ACT.Exp, scale=-1.0).then_inc(sp_exp, 1)
            def wk(k):
                for h in range(HEADS):
                    n = HEADS * k + h
                    act.wait_ge(pe_done, NK + n + 1)
                    if h == 0 and k >= 2:
                        act.wait_ge(wk_stored[k % 2], 16 * (k // 2))
                    act.activation(WKs[:, k % 2, :, h * NKV:(h + 1) * NKV],
                                   pR[:, (NK + n) % 4, 0:NJ].rearrange("p (b j) -> p b j", b=BATCH), ACT.Copy)\
                        .then_inc(wk_evac, 1)

            def vwo(n):
                u = n // 2
                act.wait_ge(pe_done, NK + NS + n + 1)
                if n % 2 == 0 and u >= CC:
                    act.wait_ge(vw_stored[u % CC], 16 * (u // CC))
                act.activation(VWs[:, 2 * (u % CC) + n % 2, :], pR[0:NKV, (NK + NS + n) % 4, :], ACT.Copy).then_inc(vw_evac, 1)

            chunk_behind = {2: 0, 3: 1, 4: 2, 5: 3}
            for n, (src, hi, lo, k) in enumerate(jobs):
                act.wait_ge(landed[n % 2], 16 * (n // 2 + 1))
                act.activation(hi[:, k, :], stage[:, n % 2, 0:src.shape[2]], ACT.Copy).then_inc(hi_done, 1)
                if n in chunk_behind:
                    wk(chunk_behind[n])
                if n >= len(jobs) - 3:
                    vwo(2 * (n - len(jobs) + 3))
                    vwo(2 * (n - len(jobs) + 3) + 1)
            for m in range(6, NV):
                vwo(m)

        @block.vector
        def _(dve):
            def projections():
                for n in range(NK):
                    dve.wait_ge(pe_done, n + 1)
                    dst = KT if n < NP else VT
                    for half in range(2):
                        rows = slice(half * DH, (half + 1) * DH)
                        ins = dve.tensor_copy(dst[rows, 2 * (n % NP) + half, :], pR[rows, n % 4, 0:NJ])
                    ins.then_inc(evac, 1)

            def softplus():
                step = [0]

                def then(ins):
                    step[0] += 1
                    ins.then_inc(sp_step, 1)
                    dve.wait_ge(sp_step, step[0])

                dve.wait_ge(sp_exp, 2)
                dve.wait_ge(small_landed, 64)
                e, s, s2, acc = cw[:, 1, :], cw[:, 2, :], cw[:, 3, :], cw[:, 4, :]
                then(dve.tensor_scalar(s, e, 2.0, None, ALU.add))
                then(dve.reciprocal(s, s))
                then(dve.tensor_tensor(s, s, e, ALU.mult))
                then(dve.tensor_tensor(s2, s, s, ALU.mult))
                then(dve.tensor_scalar(acc, s2, 1.0 / 19, 1.0 / 17, ALU.mult, ALU.add))
                for m in (15, 13, 11, 9, 7, 5, 3, 1):
                    then(dve.tensor_tensor(acc, acc, s2, ALU.mult))
                    then(dve.tensor_scalar(acc, acc, 1.0 / m, None, ALU.add))
                then(dve.tensor_tensor(acc, acc, s, ALU.mult))
                then(dve.tensor_scalar(s, fb[:, :], 0.0, None, ALU.max))
                then(dve.scalar_tensor_tensor(out=acc, in0=acc, scalar=2.0, in1=s, op0=ALU.mult, op1=ALU.add))
                then(dve.tensor_scalar(small["decay"][:, :], acc, -4.0, None, ALU.mult))
                then(dve.tensor_scalar(small["hbg"][:, :], small["bg"][:, :], 0.5, None, ALU.mult))
                then(dve.memset(small["one_eps"][:, :], 1.0 + 1e-6))

            for t in (KT, VT):
                v = t[:, :, :].rearrange("p (n two) j -> p n two j", two=2)
                dve.memset(v[0:DH, :, 1, :], 0.0).then_inc(halves_zeroed, 1)
                dve.memset(v[DH:P, :, 0, :], 0.0).then_inc(halves_zeroed, 1)
            between = {0: projections, 10: softplus}
            for n, (src, hi, lo, k) in enumerate(jobs):
                dve.wait_ge(hi_done, n + 1)
                dve.tensor_tensor(lo[:, k, :], stage[:, n % 2, 0:src.shape[2]], hi[:, k, :].bitcast(F32),
                                  ALU.subtract).then_inc(lo_done, 1)
                if n in between:
                    between[n]()


def recurrence(nc, sb, ps, sem, c, w, dram, small, X, x_landed):
    ident = c["ident"]
    SLOT = 2 * GRP
    R, XN = sb("R", [P, TT, D], F32), X
    XTh, XTl = sb("XTh", [P, DC, TB], F32R), sb("XTl", [P, DC, TB], F32R)
    HALO = TAPS - 1
    UR = sb("UR", [P, HC, TB + HALO], F32)
    U = sb("U", [P, HC, TB], F32)
    Uh, Ul = sb("Uh", [P, HC, TB], F32R), sb("Ul", [P, HC, TB], F32R)
    G, GH = sb("G", [P, HC, TB], F32), sb("GH", [P, HC - WS, TB], F32)
    GHh, GHl = sb("GHh", [P, WS, TB], F32R), sb("GHl", [P, WS, TB], F32R)
    H = sb("H", [P, GRP, TB], F32)
    TI, AL = (sb(n, [P, SLOT, TB], F32) for n in ("TI", "AL"))
    BE = sb("BE", [P, GRP + 1, TB], F32)
    carry = sb("carry", [P, HC], F32)
    stats, mv = sb("stats", [P, TT, 6], F32), sb("mv", [P, TT, 2], F32)
    rstd = sb("rstd", [P, TT], F32)
    pT = ps("pT", [P, DC, TB])
    pM = ps("pM", [P, RING, 512])
    pO = ps("pO", [P, TT, 512])

    r_landed, x1_stored = sem("r_landed"), sem("x1_stored")
    ln_step, ln_pow, ln_done = sem("ln_step"), sem("ln_pow"), sem("ln_done")
    xT_done, xhi_done, xlo_done = sem("xT_done"), sem("xhi_done"), sem("xlo_done")
    mm_done, mm_free = sem("mm_done"), sem("mm_free")
    conv_step, u_done, halo_done = sem("conv_step"), sem("u_done"), sem("halo_done")
    act_gate, gate_step, h_done = sem("act_gate"), sem("gate_step"), sem("h_done")
    gh_step, pool_passed = sem("gh_step"), sem("pool_passed")
    gh_done, wo_done, resid_done = sem("gh_done"), sem("wo_done"), sem("resid_done")
    reset, passed = sem("reset"), sem("passed")

    x_v = dram["x"].rearrange("(n t p) d -> n p t d", t=TT, p=P)
    x1_v = dram["x1"].rearrange("(n t p) d -> n p t d", t=TT, p=P)
    CW, CB, DEC, HBG = small["conv_w"], small["conv_b"], small["decay"], small["hbg"]
    NG = HC // GRP
    AG = 5 * GRP

    def segments(eng, body):
        body(0, True, False)
        with eng.Fori(1, BLK_SEQ) as i:
            body(i, False, False)
        for b in range(1, BATCH):
            if b > 1:
                with eng.Fori(b * BLK_SEQ, (b + 1) * BLK_SEQ - (b == BATCH - 1)) as i:
                    body(i, False, False)
        with eng.Fori(BLK_SEQ, NBLK - 1) as i:
            body(i, False, False)
        body(NBLK - 1, False, True)

    with nc.Block() as block:
        @block.sync
        def _(sp):
            def body(i, first, last):
                if not last:
                    sp.wait_ge(xT_done, i + 1)
                    sp.dma_start(X[:, :, :], x_v[bass.ds(i + 1, 1)].rearrange("o p t d -> p (o t) d")
                                 if not isinstance(i, int) else x_v[i + 1]).then_inc(x_landed, 16)
                if not first:
                    sp.wait_ge(resid_done, i)
                    sp.dma_start(x1_v[bass.ds(i - 1, 1)].rearrange("o p t d -> p (o t) d")
                                 if not isinstance(i, int) else x1_v[i - 1], R[:, :, :]).then_inc(x1_stored, 16)
                    sp.wait_ge(x1_stored, 16 * i)
                sp.dma_start(R[:, :, :], x_v[bass.ds(i, 1)].rearrange("o p t d -> p (o t) d")
                             if not isinstance(i, int) else x_v[i]).then_inc(r_landed, 16)

            segments(sp, body)
            sp.wait_ge(resid_done, NBLK)
            sp.dma_start(x1_v[NBLK - 1], R[:, :, :]).then_inc(x1_stored, 16)
            sp.wait_ge(x1_stored, 16 * NBLK)

        @block.gpsimd
        def _(pool):
            def inverse_deviation(i):
                pool.wait_ge(ln_step, 6 * i + 5)
                pool.tensor_tensor(rstd[:, :], mv[:, :, 1], c["mhalf"][:, :], ALU.pow).then_inc(ln_pow, 1)

            def body(i, first, last):
                if not last:
                    inverse_deviation(i + 1)
                for k in range(HC):
                    pool.wait_ge(h_done, HC * i + k + 1)
                    if k == 0 and not first:
                        pool.wait_ge(wo_done, i)
                    if k >= WS:
                        pool.tensor_tensor(GH[:, k - WS, :], G[:, k, :], H[:, k % GRP, :], ALU.mult).then_inc(gh_done, 1)
                    else:
                        step = 2 * (WS * i + k)
                        pool.tensor_tensor(G[:, k, :], G[:, k, :], H[:, k % GRP, :], ALU.mult).then_inc(gh_step, 1)
                        wait_apart(pool, gh_step, step + 1, pool_passed)
                        pool.tensor_copy(GHh[:, k, :], G[:, k, :]).then_inc(gh_step, 1)
                        wait_apart(pool, gh_step, step + 2, pool_passed)
                        pool.tensor_tensor(GHl[:, k, :], G[:, k, :], GHh[:, k, :].bitcast(F32), ALU.subtract).then_inc(gh_done, 1)

            inverse_deviation(0)
            segments(pool, body)

        @block.scalar
        def _(act):
            def x_hi(i):
                act.wait_ge(xT_done, i + 1)
                act.activation(XTh[:, 0:2, :], pT[:, 0:2, :], ACT.Copy).then_inc(xhi_done, 1)
                act.activation(XTh[:, 2:4, :], pT[:, 2:4, :], ACT.Copy).then_inc(xhi_done, 1)

            def body(i, first, last):
                use = 0
                if not first:
                    act.wait_ge(halo_done, i)
                for k in range(HC):
                    act.wait_ge(mm_done, USES * i + use + 1)
                    act.activation(UR[:, k, HALO:], pM[:, use % RING, 0:TB], ACT.Copy).then_inc(mm_free, 1)
                    use += 1
                if not first:
                    act.wait_ge(gh_done, HC * i)
                for k in range(HC):
                    act.wait_ge(mm_done, USES * i + use + 1)
                    act.activation(G[:, k, :], pM[:, use % RING, 0:TB], ACT.Gelu).then_inc(mm_free, 1)
                    use += 1
                if not last:
                    x_hi(i + 1)
                for g in range(NG):
                    for k in range(g * GRP, (g + 1) * GRP):
                        if k >= SLOT:
                            act.wait_ge(h_done, HC * i + k - SLOT + 1)
                        elif k == 0 and not first:
                            act.wait_ge(h_done, HC * i)
                        act.wait_ge(mm_done, USES * i + use + 1)
                        act.activation(AL[:, k % SLOT, :], pM[:, use % RING, 0:TB], ACT.Tanh, bias=HBG[:, k:k + 1],
                                       scale=0.5).then_inc(mm_free, 1)
                        use += 1
                        act.wait_ge(mm_done, USES * i + use + 1)
                        act.activation(TI[:, k % SLOT, :], pM[:, use % RING, 0:TB], ACT.Tanh, bias=HBG[:, HC + k:HC + k + 1],
                                       scale=0.5).then_inc(mm_free, 1)
                        use += 1
                    for k in range(g * GRP, (g + 1) * GRP):
                        act.wait_ge(mm_free, USES * i + use - 1 - 2 * ((g + 1) * GRP - 1 - k))
                        act.activation(AL[:, k % SLOT, :], AL[:, k % SLOT, :], ACT.Exp, bias=DEC[:, k:k + 1],
                                       scale=DEC[:, k:k + 1]).then_inc(act_gate, 1)
                    for k in range(GRP):
                        act.wait_ge(act_gate, 3 * HC * i + 3 * GRP * g + k + 1)
                        used = HC * i + g * GRP + k - GRP
                        if not isinstance(used, int) or used > 0:
                            act.wait_ge(h_done, used)
                        act.activation(BE[:, (g * GRP + k) % (GRP + 1), :], AL[:, (g * GRP + k) % SLOT, :], ACT.Square).then_inc(act_gate, 1)
                    for k in range(GRP):
                        act.wait_ge(act_gate, 3 * HC * i + 3 * GRP * g + GRP + k + 1)
                        act.activation(BE[:, (g * GRP + k) % (GRP + 1), :], BE[:, (g * GRP + k) % (GRP + 1), :], ACT.Sqrt,
                                       bias=small["one_eps"][:, 0:1], scale=-1.0).then_inc(act_gate, 1)

            x_hi(0)
            segments(act, body)

        @block.vector
        def _(dve):
            def norm(i):
                dve.wait_ge(x_landed, 16 * i + 16)
                for t in range(TT):
                    dve.bn_stats(stats[:, t, :], X[:, t, :]).then_inc(ln_step, 1)
                for t in range(TT):
                    wait_apart(dve, ln_step, 6 * i + t + 1, passed)
                    dve.bn_aggr(mv[:, t, :], stats[:, t, :]).then_inc(ln_step, 1)
                dve.wait_ge(ln_step, 6 * i + 2 * TT)
                dve.tensor_scalar(mv[:, :, 1], mv[:, :, 1], EPS, None, ALU.add).then_inc(ln_step, 2)
                dve.wait_ge(ln_pow, i + 1)
                for t in range(TT):
                    ins = dve.tensor_scalar(XN[:, t, :], X[:, t, :], mv[:, t, 0:1], rstd[:, t:t + 1],
                                            ALU.subtract, ALU.mult)
                ins.then_inc(ln_done, 1)

            def x_lo(i):
                for b in range(2):
                    dve.wait_ge(xhi_done, 2 * i + b + 1)
                    dve.tensor_tensor(XTl[:, 2 * b:2 * b + 2, :], pT[:, 2 * b:2 * b + 2, :],
                                      XTh[:, 2 * b:2 * b + 2, :].bitcast(F32), ALU.subtract).then_inc(xlo_done, 1)

            def convolve(i):
                PAIR = 2 * (TAPS + 1)
                for k in range(0, HC, 2):
                    base = HC * (TAPS + 1) * i + PAIR * (k // 2)
                    for m in (k, k + 1):
                        dve.wait_ge(mm_free, USES * i + m + 1)
                        dve.tensor_scalar(U[:, m, :], UR[:, m, 0:TB], CW[:, TAPS * m:TAPS * m + 1], CB[:, m:m + 1],
                                          ALU.mult, ALU.add).then_inc(conv_step, 1)
                    for j in range(1, TAPS):
                        for m in (k, k + 1):
                            dve.wait_ge(conv_step, base + 2 * j + m - k - 1)
                            dve.scalar_tensor_tensor(out=U[:, m, :], in0=UR[:, m, j:j + TB],
                                                     scalar=CW[:, TAPS * m + j:TAPS * m + j + 1], in1=U[:, m, :],
                                                     op0=ALU.mult, op1=ALU.add).then_inc(conv_step, 1)
                    for m in (k, k + 1):
                        dve.wait_ge(conv_step, base + 2 * TAPS + m - k - 1)
                        dve.tensor_copy(Uh[:, m, :], U[:, m, :]).then_inc(conv_step, 1)
                    for m in (k, k + 1):
                        dve.wait_ge(conv_step, base + 2 * TAPS + m - k + 1)
                        dve.tensor_tensor(Ul[:, m, :], U[:, m, :], Uh[:, m, :].bitcast(F32),
                                          ALU.subtract).then_inc(u_done, 1)
                dve.tensor_copy(UR[:, :, 0:HALO], UR[:, :, TB:TB + HALO]).then_inc(halo_done, 1)

            def gates(i):
                for k in range(HC):
                    g, r, q = k // GRP, k % GRP, k % SLOT
                    dve.wait_ge(act_gate, 3 * HC * i + 3 * GRP * g + 2 * GRP + r + 1)
                    base = 4 * HC * i + 4 * k
                    dve.scalar_tensor_tensor(out=TI[:, q, :], in0=TI[:, q, :], scalar=1.0, in1=U[:, k, :],
                                             op0=ALU.add, op1=ALU.mult).then_inc(gate_step, 1)
                    dve.wait_ge(gate_step, base + 1)
                    dve.scalar_tensor_tensor(out=TI[:, q, :], in0=TI[:, q, :], scalar=0.5, in1=BE[:, k % (GRP + 1), :],
                                             op0=ALU.mult, op1=ALU.mult).then_inc(gate_step, 1)
                    dve.wait_ge(gate_step, base + 2)
                    if k >= GRP:
                        dve.wait_ge(gh_done, HC * i + k - GRP + 1)
                    elif not (isinstance(i, int) and i == 0):
                        dve.wait_ge(gh_done, HC * i)
                    dve.tensor_tensor_scan(H[:, r, :], AL[:, q, :], TI[:, q, :], carry[:, k:k + 1],
                                           ALU.mult, ALU.add).then_inc(h_done, 1)
                    dve.wait_ge(h_done, HC * i + k + 1)
                    dve.tensor_copy(carry[:, k:k + 1], H[:, r, TB - 1:TB]).then_inc(gate_step, 2)

            def residual(i):
                dve.wait_ge(wo_done, i + 1)
                dve.wait_ge(r_landed, 16 * i + 16)
                for t in range(TT):
                    ins = dve.tensor_tensor(R[:, t, :], pO[:, t, :], R[:, t, :], ALU.add)
                ins.then_inc(resid_done, 1)

            def fresh_sequence(n):
                dve.memset(UR[:, :, 0:HALO], 0.0).then_inc(reset, 1)
                dve.memset(carry[:, :], 0.0).then_inc(reset, 1)
                dve.wait_ge(reset, 2 * n)

            def body(i, first, last):
                if not last:
                    norm(i + 1)
                convolve(i)
                if not first:
                    residual(i - 1)
                if not last:
                    x_lo(i + 1)
                gates(i)

            fresh_sequence(1)
            norm(0)
            x_lo(0)
            body(0, True, False)
            with dve.Fori(1, BLK_SEQ) as i:
                body(i, False, False)
            dve.wait_ge(halo_done, BLK_SEQ)
            dve.wait_ge(gate_step, 4 * HC * BLK_SEQ)
            fresh_sequence(2)
            with dve.Fori(BLK_SEQ, NBLK - 1) as i:
                body(i, False, False)
            body(NBLK - 1, False, True)
            residual(NBLK - 1)

        @block.tensor
        def _(pe):
            def transposes(i):
                pe.wait_ge(ln_done, i + 1)
                if not (isinstance(i, int) and i == 0):
                    pe.wait_ge(xlo_done, 2 * i)
                for k in range(DC):
                    for t in range(TT):
                        mm = pe.transpose(pT[:, k, t * P:(t + 1) * P], XN[:, t, k * P:(k + 1) * P], ident[:, :])
                mm.then_inc(xT_done, 1)

            def product(out_use, i, pairs, offset=0, skip_free=False):
                if not skip_free:
                    pe.wait_ge(mm_free, USES * i + out_use + offset - RING + 1)
                split(pe.matmul, pM[:, out_use % RING, 0:TB], pairs).then_inc(mm_done, 1)

            def in_product(i, chunk, use, **kw):
                s = slice(chunk * P, (chunk + 1) * P)
                product(use, i, [((w["Wih"][:, k, s], w["Wil"][:, k, s]), (XTh[:, k, :], XTl[:, k, :]))
                                 for k in range(DC)], **kw)

            def u_products(i, first=False, offset=0):
                pe.wait_ge(xlo_done, 2 * (i + (1 if offset else 0)) + 2)
                for k in range(HC):
                    in_product(i, HC + k, k, offset=offset, skip_free=first and k < RING)

            def body(i, first, last):
                for k in range(HC):
                    in_product(i, k, HC + k)
                if not last:
                    transposes(i + 1)
                pe.wait_ge(u_done, HC * (i + 1))
                for k in range(HC):
                    for half in range(2):
                        s = slice((half * HC + k) * P, (half * HC + k + 1) * P)
                        product(2 * HC + 2 * k + half, i, [((w["Wgh"][:, m, s], w["Wgl"][:, m, s]),
                                                            (Uh[:, m, :], Ul[:, m, :])) for m in range(HC)])
                if not last:
                    u_products(i, offset=USES)
                pe.wait_ge(gh_done, HC * (i + 1))
                if not first:
                    pe.wait_ge(resid_done, i)
                for t in range(TT):
                    s = slice(t * P, (t + 1) * P)
                    split(pe.matmul, pO[:, t, :], [((GHh[:, k, s], GHl[:, k, s]),
                                                    (w["Woh"][:, 0, k * D:(k + 1) * D], w["Wol"][:, 0, k * D:(k + 1) * D]))
                                                   for k in range(WS)], stop=False)
                    for k in range(WS, HC):
                        mm = pe.matmul(pO[:, t, :], GH[:, k - WS, s], w["Wo"][:, k - WS, :], start=False, stop=(k == HC - 1))
                mm.then_inc(wo_done, 1)

            transposes(0)
            u_products(0, first=True)
            segments(pe, body)


GT = 4
LOOP = (3, NTILE // GT - 1)


def attention(nc, sb, ps, sem, c, dram):
    ident = c["ident"]
    WKh, WKl = (sb(n, [P, BATCH, DC, SC], F32R) for n in ("WKh", "WKl"))
    VWh, VWl = (sb(n, [P, BATCH, SCC, D], F32R) for n in ("VWh", "VWl"))
    stage = sb("stage", [P, 2 * BATCH, SCC * D], F32)
    pieces = [(n, b) for b in range(BATCH) for n in ("wk", "vw")]
    split_behind = {(-1, 2): 0, (-1, 3): 1}
    split_in = {divmod(GT * LOOP[0] - 2 * (2 * BATCH - n) + 1, GT): n for n in range(2, 2 * BATCH)}
    XA = sb("XA", [P, GT, D], F32)
    XN, R = (sb(n, [P, 2, D], F32) for n in ("XN1", "R1"))
    XTh, XTl = (sb(n, [P, 2, DC, P], F32R) for n in ("X1Th", "X1Tl"))
    X2, X3 = sb("X2", [P, 2, D], F32), sb("X3", [P, 2, D], F32)
    X3T = sb("X3T", [P, DC, P], F32)
    E = sb("E", [P, 2, SCP], F32)
    PTh, PTl = (sb(n, [P, SCC, P], F32R) for n in ("PTh", "PTl"))
    mx, den = sb("mx", [P, HEADS], F32), sb("den", [P, HEADS], F32)
    st1, mv1, rs1, nm1 = (sb(n, [P, k], F32) for n, k in (("st1", 6), ("mv1", 2), ("rs1", 1), ("nm1", 1)))
    st3, mv3, rs3, nm3 = (sb(n, [P, k], F32) for n, k in (("st3", 6), ("mv3", 2), ("rs3", 1), ("nm3", 1)))
    Wg, bg = sb("Wgate", [P, DC, NE], F32), sb("bgate", [P, NE], F32)
    lg, sco, eq, prod = (sb(n, [P, GT, NE], F32) for n in ("lg", "sco", "eq", "prod"))
    oh, seen, ohs = sb("oh", [P, GT, NE], BF16), sb("seen", [P, NE], BF16), sb("ohs", [P, NE], F32)
    lmax, rden, gate, first, pos, keep, place, away, spill = (
        sb(n, [P, GT], F32) for n in ("lmax", "rden", "gate", "first", "pos", "keep", "place", "away", "spill"))
    pair = sb("pair", [P, GT, 2], F32)
    SI = sb("SI", [P, GT], U32)
    pT, pS = ps("pT1", [P, DC, P]), ps("pS", [P, 2, 512])
    pP, pY = ps("pP", [P, 2, 4, P]), ps("pY", [P, D])
    pT3, pL = ps("pT3", [P, DC, P]), ps("pL", [P, 512])
    pLog = pL[:, 0:GT * NE].rearrange("p (t e) -> p t e", t=GT)
    pCnt = pL[:, GT * NE:2 * GT * NE].rearrange("p (t e) -> p t e", t=GT)

    piece_landed = [sem(f"piece_landed{n}") for n in range(2 * BATCH)]
    whi_done, wlo_done, g_landed, init = sem("whi_done"), sem("wlo_done"), sem("g_landed"), sem("init")
    xa_landed, r_landed = ([sem(f"{n}{k}") for k in range(r)] for n, r in (("xa_landed", GT), ("r1_landed", 2)))
    x2_stored, x3_stored = ([sem(f"{n}{k}") for k in range(2)] for n in ("x2_stored", "x3_stored"))
    ln1_step, ln1_pow, ln1_done = sem("ln1_step"), sem("ln1_pow"), sem("ln1_done")
    ln3_step, ln3_pow, ln3_done = sem("ln3_step"), sem("ln3_pow"), sem("ln3_done")
    xT_done, xhi_done, xlo_done, score_done = (sem(n) for n in ("x1T_done", "x1hi_done", "x1lo_done", "score_done"))
    max_done, sub_done, exp_done, soft_step, prob_done = (
        sem(n) for n in ("max_done", "sub_done", "exp_done", "soft_step", "prob_done"))
    pt_done, phi_done, plo_done, y_done, x2_done = (sem(n) for n in ("pt_done", "phi_done", "plo_done", "y_done", "x2_done"))
    x3T_done, x3T_copied, logit_done = sem("x3T_done"), sem("x3T_copied"), sem("logit_done")
    route_dve, route_pool, route_slot, route_exp, count_done = (
        sem(n) for n in ("route_dve", "route_pool", "route_slot", "route_exp", "count_done"))
    scattered, passed, pool_passed = sem("scattered"), sem("passed"), sem("pool_passed")
    RD, RP, RS = 12, 3, 10

    tiles = {n: dram[n].rearrange("(n p) d -> n p d", p=P) for n in ("x1", "x2", "x3", "out")}

    def num(t):
        return GT * t[0] + t[1]

    def uses(t, ring):
        return GT // ring * t[0] + t[1] // ring + 1

    def real(t):
        return not isinstance(t[0], int) or 0 <= num(t) < NTILE

    def group_real(g):
        return not isinstance(g, int) or 0 <= g < NTILE // GT

    def rows(name, t):
        n = num(t)
        return tiles[name][n] if isinstance(n, int) else tiles[name][bass.ds(n, 1)].rearrange("o p d -> p (o d)")

    def wait(eng, s, value):
        if not isinstance(value, int) or value > 0:
            eng.wait_ge(s, value)

    def pipeline(eng, step, end):
        for j in range(1, GT):
            step(-1, j)
        for g in range(0, LOOP[0]):
            for j in range(GT):
                step(g, j)
        with eng.Fori(*LOOP) as g:
            for j in range(GT):
                step(g, j)
        for n in range(GT * LOOP[1], NTILE + end):
            step(n // GT, n % GT)

    with nc.Block() as block:
        @block.sync
        def _(sp):
            for t in ((0, m) for m in range(GT)):
                sp.dma_start(XA[:, t[1], :], rows("x1", t)).then_inc(xa_landed[t[1]], 16)
            for n, (name, b) in enumerate(pieces):
                src = dram["wk"][:, b, :, :] if name == "wk" else dram["vw"][b].rearrange("(c p) d -> p c d", p=P)
                k, m = (DC, SC) if name == "wk" else (SCC, D)
                sp.dma_start(stage[:, n, 0:k * m].rearrange("p (k m) -> p k m", k=k), src).then_inc(piece_landed[n], 16)
                if n == 1:
                    sp.dma_start(Wg[:, :, :], dram["Wgate"]).then_inc(g_landed, 16)
                    sp.dma_start(bg[:, :], dram["bgate"].partition_broadcast(P)).then_inc(g_landed, 16)

            def step(g, j):
                t = (g, j - 3)
                if real(t):
                    sp.wait_ge(ln3_done, num(t) + 1)
                    q = t[1] % 2
                    sp.dma_start(rows("x2", t), X2[:, q, :]).then_inc(x2_stored[q], 16)
                    sp.dma_start(rows("out", t), X2[:, q, :]).then_inc(x2_stored[q], 16)
                    sp.dma_start(rows("x3", t), X3[:, q, :]).then_inc(x3_stored[q], 16)
                t = (g, j + 4)
                if real(t) and not (isinstance(g, int) and num(t) < GT):
                    wait(sp, ln1_done, num(t) - GT + 1)
                    sp.dma_start(XA[:, t[1] % GT, :], rows("x1", t)).then_inc(xa_landed[t[1] % GT], 16)
                t = (g, j)
                if real(t):
                    wait(sp, x2_done, num(t) - 1)
                    sp.dma_start(R[:, t[1] % 2, :], rows("x1", t)).then_inc(r_landed[t[1] % 2], 16)

            pipeline(sp, step, 3)
            for q in range(2):
                sp.wait_ge(x2_stored[q], 32 * NTILE // 2)
                sp.wait_ge(x3_stored[q], 16 * NTILE // 2)

        @block.gpsimd
        def _(pool):
            half = c["mhalf"][:, 0:1]

            def deviation(t, step, done, mv, rs, nm, power):
                n = num(t)
                wait(pool, done, n)
                pool.wait_ge(step, 3 * n + 3)
                pool.tensor_tensor(rs[:, :], mv[:, 1:2], half, ALU.pow).then_inc(power, 1)
                wait_apart(pool, power, 2 * n + 1, pool_passed)
                pool.tensor_scalar(nm[:, :], mv[:, 0:1], rs[:, 0:1], -1.0, ALU.mult, ALU.mult).then_inc(power, 1)

            def probabilities(t):
                e = E[:, t[1] % 2, 0:SC].rearrange("p (h j) -> p h j", h=HEADS)
                pool.wait_ge(soft_step, 2 * num(t) + 2)
                pool.tensor_tensor(e, e, den[:, :].unsqueeze(2).to_broadcast([P, HEADS, NKV]), ALU.mult).then_inc(prob_done, 1)

            def over_experts(v):
                return v.unsqueeze(2).to_broadcast([P, GT, NE])

            def route_1(g):
                pool.wait_ge(route_dve, RD * g + 2)
                pool.tensor_tensor(lg[:, :, :], lg[:, :, :], over_experts(lmax[:, :]), ALU.subtract).then_inc(route_pool, 1)

            def route_2(g):
                pool.wait_ge(route_dve, RD * g + 4)
                pool.tensor_tensor(sco[:, :, :], sco[:, :, :], over_experts(rden[:, :]), ALU.mult).then_inc(route_pool, 1)

            def route_3(g):
                pool.wait_ge(route_dve, RD * g + 6)
                pool.tensor_tensor(eq[:, :, :], eq[:, :, :], c["iota16"][:, :].unsqueeze(1).to_broadcast([P, GT, NE]),
                                   ALU.mult).then_inc(route_pool, 1)

            def route_4(g):
                def step(k, ins):
                    ins.then_inc(route_slot, 1)
                    wait_apart(pool, route_slot, RS * g + k, pool_passed)
                wait_apart(pool, route_dve, RD * g + RD, pool_passed)
                step(1, pool.tensor_scalar(keep[:, :], pos[:, :], float(CAP), None, ALU.is_lt))
                step(2, pool.tensor_scalar(place[:, :], first[:, :], float(CAP), float(NE * CAP), ALU.mult, ALU.add))
                step(3, pool.tensor_tensor(place[:, :], place[:, :], pos[:, :], ALU.add))
                step(4, pool.tensor_tensor(away[:, :], place[:, :], spill[:, :], ALU.subtract))
                step(5, pool.tensor_tensor(away[:, :], away[:, :], keep[:, :], ALU.mult))
                step(6, pool.tensor_tensor(away[:, :], away[:, :], spill[:, :], ALU.add))
                if not (isinstance(g, int) and g == 0):
                    wait_apart(pool, scattered, 16 * GT * g, pool_passed)
                step(7, pool.tensor_copy(SI[:, :], away[:, :]))
                step(8, pool.tensor_scalar(pair[:, :, 0], spill[:, :], 1.0, -float(SLOTS + 1), ALU.mult, ALU.add))
                step(9, pool.tensor_copy(pair[:, :, 1], gate[:, :]))
                step(10, pool.tensor_scalar(spill[:, :], spill[:, :], 1.0, float(GT * P), ALU.mult, ALU.add))

            def scatter(g, m):
                for n in (m, m + 1):
                    pool.indirect_dma_start(out=dram["slotmap"], out_offset=bass.IndirectOffsetOnAxis(SI[:, n:n + 1], 0),
                                            in_=pair[:, n, :], in_offset=None).then_inc(scattered, 16)

            def step(g, j):
                if real((g, j + 3)):
                    deviation((g, j + 3), ln1_step, ln1_done, mv1, rs1, nm1, ln1_pow)
                if j == 0 and group_real(g - 2):
                    route_2(g - 2)
                if j == 1 and group_real(g - 2):
                    route_3(g - 2)
                if real((g, j)):
                    probabilities((g, j))
                if real((g, j - 2)):
                    deviation((g, j - 2), ln3_step, ln3_done, mv3, rs3, nm3, ln3_pow)
                if j == 3 and group_real(g - 1):
                    route_1(g - 1)
                if j == 3 and group_real(g - 2):
                    route_4(g - 2)
                if group_real(g - 3):
                    if not isinstance(g, int) or g < NTILE // GT + 1:
                        if j < 2:
                            scatter(g - 3, 2 * j)
                    elif j == int(group_real(g - 2)):
                        scatter(g - 3, 0)
                        scatter(g - 3, 2)

            pool.memset(seen[:, :], 0.0).then_inc(init, 1)
            pool.memset(E[:, :, SC:SC + 1], 1.0).then_inc(init, 1)
            pool.memset(E[:, :, SC + 1:SCP], 0.0).then_inc(init, 1)
            for n in range(GT):
                pool.tensor_scalar(spill[:, n:n + 1], c["iotap"][:, :], 1.0, float(SLOTS + 1 + P * n), ALU.mult, ALU.add)\
                    .then_inc(init, 1)
            pool.wait_ge(init, 3 + GT)
            pipeline(pool, step, 2 * GT + 2)
            pool.wait_ge(scattered, 16 * NTILE)

        @block.scalar
        def _(act):
            def step(g, j):
                if isinstance(g, int) and (g, j) in split_in:
                    w_hi(split_in[g, j])
                t = (g, j - 1)
                if real(t):
                    n = num(t)
                    act.wait_ge(pt_done, n + 1)
                    wait(act, y_done, n)
                    act.activation(PTh[:, 0:4, :], pP[:, 0, :, :], ACT.Copy).then_inc(phi_done, 1)
                    act.activation(PTh[:, 4:SCC, :], pP[:, 1, 0:SCC - 4, :], ACT.Copy).then_inc(phi_done, 1)
                t = (g, j)
                if real(t):
                    e = E[:, t[1] % 2, 0:SC]
                    act.wait_ge(sub_done, num(t) + 1)
                    act.activation(e, e, ACT.Exp, scale=SCALE).then_inc(exp_done, 1)
                t = (g, j - 3)
                if real(t):
                    act.wait_ge(x3T_done, num(t) + 1)
                    wait(act, logit_done, num(t))
                    act.activation(X3T[:, :, :], pT3[:, :, :], ACT.Copy).then_inc(x3T_copied, 1)
                t = (g, j + 3)
                if real(t):
                    n = num(t)
                    act.wait_ge(ln1_pow, 2 * n + 2)
                    wait(act, xT_done, n - 1)
                    act.activation(XN[:, t[1] % 2, :], XA[:, t[1] % GT, :], ACT.Identity, bias=nm1[:, 0:1],
                                   scale=rs1[:, 0:1]).then_inc(ln1_done, 1)
                t = (g, j + 2)
                if real(t):
                    n = num(t)
                    act.wait_ge(xT_done, n + 1)
                    wait(act, score_done, n - 1)
                    act.activation(XTh[:, t[1] % 2, :, :], pT[:, :, :], ACT.Copy).then_inc(xhi_done, 1)
                t = (g, j - 2)
                if real(t):
                    n = num(t)
                    act.wait_ge(ln3_pow, 2 * n + 2)
                    wait(act, x3T_done, n - 1)
                    if n_uses(t) is not None:
                        act.wait_ge(x3_stored[t[1] % 2], 16 * n_uses(t))
                    act.activation(X3[:, t[1] % 2, :], X2[:, t[1] % 2, :], ACT.Identity, bias=nm3[:, 0:1],
                                   scale=rs3[:, 0:1]).then_inc(ln3_done, 1)
                if j == 3 and group_real(g - 1):
                    act.wait_ge(route_pool, RP * (g - 1) + 1)
                    act.activation(sco[:, :, :], lg[:, :, :], ACT.Exp).then_inc(route_exp, 1)
                if isinstance(g, int) and (g, j) in split_behind:
                    w_hi(split_behind[g, j])

            def w_hi(n):
                name, b = pieces[n]
                act.wait_ge(piece_landed[n], 16)
                hi = (WKh[:, b, :, :] if name == "wk" else VWh[:, b, :, :])
                k, m = (DC, SC) if name == "wk" else (SCC, D)
                act.activation(hi, stage[:, n, 0:k * m].rearrange("p (k m) -> p k m", k=k), ACT.Copy).then_inc(whi_done, 1)

            def n_uses(t):
                n = uses(t, 2) - 1
                return None if isinstance(n, int) and n <= 0 else n

            pipeline(act, step, 3 + GT - 3)

        @block.vector
        def _(dve):
            mx_v = mx[:, :].rearrange("p (g h) -> p g h", g=2)
            s_v = pS[:, :, 0:HG * NKV].rearrange("p g (h j) -> p g h j", h=HG)

            def stats(src, ready, value, st, mv, step, n):
                dve.wait_ge(ready, value)
                dve.bn_stats(st[:, :], src).then_inc(step, 1)

            def aggregate(st, mv, step, power, n):
                wait(dve, power, 2 * n)
                wait_apart(dve, step, 3 * n + 1, passed)
                dve.bn_aggr(mv[:, :], st[:, :]).then_inc(step, 1)

            def add_eps(mv, step, n):
                dve.wait_ge(step, 3 * n + 2)
                dve.tensor_scalar(mv[:, 1:2], mv[:, 1:2], EPS, None, ALU.add).then_inc(step, 1)

            def over_experts(v):
                return v.unsqueeze(2).to_broadcast([P, GT, NE])

            def route_1(g):
                if isinstance(g, int) and g == 0:
                    dve.wait_ge(g_landed, 32)
                dve.wait_ge(logit_done, GT * g + GT)
                dve.tensor_tensor(lg[:, :, :], pLog, bg[:, :].unsqueeze(1).to_broadcast([P, GT, NE]), ALU.add).then_inc(route_dve, 1)
                dve.wait_ge(route_dve, RD * g + 1)
                dve.tensor_reduce(lmax[:, :], lg[:, :, :], AX.X, ALU.max).then_inc(route_dve, 1)

            def route_2(g):
                dve.wait_ge(route_exp, g + 1)
                dve.tensor_reduce(rden[:, :], sco[:, :, :], AX.X, ALU.add).then_inc(route_dve, 1)
                dve.wait_ge(route_dve, RD * g + 3)
                dve.reciprocal(rden[:, :], rden[:, :]).then_inc(route_dve, 1)

            def route_3(g):
                dve.wait_ge(route_pool, RP * g + 2)
                if not (isinstance(g, int) and g == 0):
                    dve.wait_ge(route_slot, RS * g)
                dve.tensor_reduce(gate[:, :], sco[:, :, :], AX.X, ALU.max).then_inc(route_dve, 1)
                dve.wait_ge(route_dve, RD * g + 5)
                dve.tensor_tensor(eq[:, :, :], sco[:, :, :], over_experts(gate[:, :]), ALU.is_equal).then_inc(route_dve, 1)

            def route_4(g):
                dve.wait_ge(route_pool, RP * g + 3)
                dve.tensor_reduce(first[:, :], eq[:, :, :], AX.X, ALU.min).then_inc(route_dve, 1)
                dve.wait_ge(route_dve, RD * g + 7)
                dve.tensor_tensor(oh[:, :, :], c["iota16"][:, :].unsqueeze(1).to_broadcast([P, GT, NE]),
                                  over_experts(first[:, :]), ALU.is_equal).then_inc(route_dve, 1)
                dve.wait_ge(route_dve, RD * g + 8)
                dve.tensor_reduce(ohs[:, :], oh[:, :, :].rearrange("p t e -> p e t"), AX.X, ALU.add).then_inc(route_dve, 1)

            def route_5(g):
                dve.wait_ge(count_done, g + 1)
                later = GT * (g + 2)
                dve.wait_ge(logit_done, min(later, NTILE) if isinstance(later, int) else later)
                dve.tensor_tensor(prod[:, :, :], pCnt, oh[:, :, :], ALU.mult).then_inc(route_dve, 1)
                dve.tensor_tensor(seen[:, :], seen[:, :], ohs[:, :], ALU.add).then_inc(route_dve, 1)
                dve.wait_ge(route_dve, RD * g + 11)
                dve.tensor_reduce(pos[:, :], prod[:, :, :], AX.X, ALU.add).then_inc(route_dve, 1)

            def w_lo(n):
                name, b = pieces[n]
                dve.wait_ge(whi_done, n + 1)
                hi, lo = ((WKh, WKl) if name == "wk" else (VWh, VWl))
                k, m = (DC, SC) if name == "wk" else (SCC, D)
                dve.tensor_tensor(lo[:, b, :, :], stage[:, n, 0:k * m].rearrange("p (k m) -> p k m", k=k),
                                  hi[:, b, :, :].bitcast(F32), ALU.subtract).then_inc(wlo_done, 1)

            def step(g, j):
                if isinstance(g, int) and (g, j) in split_in:
                    w_lo(split_in[g, j])
                t = (g, j)
                if real(t):
                    n, q = num(t), t[1] % 2
                    dve.wait_ge(score_done, n + 1)
                    dve.tensor_reduce(mx_v, s_v, AX.X, ALU.max).then_inc(max_done, 1)
                if real((g, j + 3)):
                    m = (g, j + 3)
                    stats(XA[:, m[1] % GT, :], xa_landed[m[1] % GT], 16 * uses(m, GT), st1, mv1, ln1_step, num(m))
                if real(t):
                    dve.wait_ge(max_done, n + 1)
                    wait(dve, pt_done, n - 1)
                    dve.tensor_tensor(E[:, q, 0:SC].rearrange("p (g h j) -> p g h j", g=2, h=HG), s_v,
                                      mx_v.unsqueeze(3).to_broadcast([P, 2, HG, NKV]), ALU.subtract).then_inc(sub_done, 1)
                if real((g, j + 3)):
                    aggregate(st1, mv1, ln1_step, ln1_pow, num((g, j + 3)))
                t = (g, j - 2)
                if real(t):
                    n, q = num(t), t[1] % 2
                    dve.wait_ge(y_done, n + 1)
                    dve.wait_ge(r_landed[q], 16 * uses(t, 2))
                    before = uses(t, 2) - 1
                    if not isinstance(before, int) or before > 0:
                        dve.wait_ge(x2_stored[q], 32 * before)
                    dve.tensor_tensor(X2[:, q, :], pY[:, :], R[:, q, :], ALU.add).then_inc(x2_done, 1)
                if real((g, j + 3)):
                    add_eps(mv1, ln1_step, num((g, j + 3)))
                if j == 0 and group_real(g - 2):
                    route_2(g - 2)
                if j == 1 and group_real(g - 2):
                    route_3(g - 2)
                if real(t):
                    stats(X2[:, t[1] % 2, :], x2_done, num(t) + 1, st3, mv3, ln3_step, num(t))
                if real(t):
                    aggregate(st3, mv3, ln3_step, ln3_pow, num(t))
                if j == 3 and group_real(g - 1):
                    route_1(g - 1)
                t = (g, j - 1)
                if real(t):
                    n = num(t)
                    dve.wait_ge(phi_done, 2 * n + 2)
                    dve.tensor_tensor(PTl[:, 0:4, :], pP[:, 0, :, :], PTh[:, 0:4, :].bitcast(F32), ALU.subtract).then_inc(plo_done, 1)
                    dve.tensor_tensor(PTl[:, 4:SCC, :], pP[:, 1, 0:SCC - 4, :], PTh[:, 4:SCC, :].bitcast(F32),
                                      ALU.subtract).then_inc(plo_done, 1)
                if real((g, j - 2)):
                    add_eps(mv3, ln3_step, num((g, j - 2)))
                t = (g, j)
                if real(t):
                    n, q = num(t), t[1] % 2
                    dve.wait_ge(exp_done, n + 1)
                    wait(dve, prob_done, n)
                    dve.tensor_reduce(den[:, :], E[:, q, 0:SC].rearrange("p (h j) -> p h j", h=HEADS), AX.X,
                                      ALU.add).then_inc(soft_step, 1)
                    dve.wait_ge(soft_step, 2 * n + 1)
                    dve.reciprocal(den[:, :], den[:, :]).then_inc(soft_step, 1)
                if j == 1 and group_real(g - 2):
                    route_4(g - 2)
                if j == 2 and group_real(g - 2):
                    route_5(g - 2)
                t = (g, j + 2)
                if real(t):
                    n, q = num(t), t[1] % 2
                    dve.wait_ge(xhi_done, n + 1)
                    dve.tensor_tensor(XTl[:, q, :, :], pT[:, :, :], XTh[:, q, :, :].bitcast(F32), ALU.subtract).then_inc(xlo_done, 1)
                if isinstance(g, int) and (g, j) in split_behind:
                    w_lo(split_behind[g, j])

            dve.wait_ge(init, 3 + GT)
            pipeline(dve, step, 3 + GT)

        @block.tensor
        def _(pe):
            def batch(t):
                n = num(t)
                return n // TILE_SEQ if isinstance(n, int) else pe.snap(n // TILE_SEQ)

            def of(v, b, k, s):
                return v[:, b, k, s] if isinstance(b, int) else v[:, bass.ds(b, 1), k, s].rearrange("p o n -> p (o n)")

            def step(g, j):
                t = (g, j - 1)
                if real(t):
                    n = num(t)
                    pe.wait_ge(prob_done, n + 1)
                    wait(pe, plo_done, 2 * n)
                    for k in range(SCC):
                        mm = pe.transpose(pP[:, k // 4, k % 4, :], E[:, t[1] % 2, k * P:(k + 1) * P], ident[:, :])
                    mm.then_inc(pt_done, 1)
                t = (g, j + 2)
                if real(t):
                    n = num(t)
                    pe.wait_ge(ln1_done, n + 1)
                    wait(pe, xlo_done, n)
                    for k in range(DC):
                        mm = pe.transpose(pT[:, k, :], XN[:, t[1] % 2, k * P:(k + 1) * P], ident[:, :])
                    mm.then_inc(xT_done, 1)
                t = (g, j - 3)
                if real(t):
                    n = num(t)
                    pe.wait_ge(ln3_done, n + 1)
                    wait(pe, x3T_copied, n)
                    for k in range(DC):
                        mm = pe.transpose(pT3[:, k, :], X3[:, t[1] % 2, k * P:(k + 1) * P], ident[:, :])
                    mm.then_inc(x3T_done, 1)
                if j == 2 and group_real(g - 2):
                    pe.wait_ge(route_dve, RD * (g - 2) + 9)
                    pe.matmul(pCnt, c["tri"][:, :], oh[:, :, :], start=True, stop=False)
                    pe.matmul(pCnt, c["ones"][:, :], seen[:, :].unsqueeze(1).to_broadcast([P, GT, NE]), start=False, stop=False)
                    for m in range(GT - 1):
                        mm = pe.matmul(pCnt[:, m + 1:GT, :], c["ones"][:, :],
                                       oh[:, m, :].unsqueeze(1).to_broadcast([P, GT - 1 - m, NE]), start=False, stop=(m == GT - 2))
                    mm.then_inc(count_done, 1)
                t = (g, j + 1)
                if real(t):
                    n, q, b = num(t), t[1] % 2, batch(t)
                    if isinstance(n, int) and n in (0, GT * LOOP[0]):
                        pe.wait_ge(wlo_done, 1 if n == 0 else 2 * BATCH)
                    pe.wait_ge(xlo_done, n + 1)
                    wait(pe, sub_done, n)
                    for h in range(2):
                        s = slice(h * HG * NKV, (h + 1) * HG * NKV)
                        mm = split(pe.matmul, pS[:, h, 0:HG * NKV],
                                   [((XTh[:, q, k, :], XTl[:, q, k, :]), (of(WKh, b, k, s), of(WKl, b, k, s)))
                                    for k in range(DC)])
                    mm.then_inc(score_done, 1)
                t = (g, j - 3)
                if real(t):
                    n = num(t)
                    if isinstance(n, int) and n == 0:
                        pe.wait_ge(g_landed, 32)
                    pe.wait_ge(x3T_copied, n + 1)
                    if t[1] % GT == 0:
                        grp = g + (t[1] - t[1] % GT) // GT
                        wait(pe, route_dve, RD * (grp - 1) + 1)
                    if j == 3 and group_real(g - 2):
                        pe.wait_ge(route_dve, RD * (g - 2) + 10)
                    for k in range(DC):
                        mm = pe.matmul(pL[:, t[1] % GT * NE:(t[1] % GT + 1) * NE], X3T[:, k, :], Wg[:, k, :],
                                       start=(k == 0), stop=(k == DC - 1))
                    mm.then_inc(logit_done, 1)
                t = (g, j - 1)
                if real(t):
                    n, b = num(t), batch(t)
                    if isinstance(n, int) and n == 0:
                        pe.wait_ge(wlo_done, 2)
                    pe.wait_ge(plo_done, 2 * n + 2)
                    wait(pe, x2_done, n)
                    split(pe.matmul, pY[:, :], [((PTh[:, k, :], PTl[:, k, :]), (of(VWh, b, k, slice(0, D)), of(VWl, b, k, slice(0, D))))
                                                for k in range(SCC)]).then_inc(y_done, 1)

            pipeline(pe, step, 3 + GT)


def experts(nc, sb, ps, sem, c, dram):
    ident = c["ident"]
    NT = NE * ST
    raw1, raw2 = (sb(n, [P, NQ, 4, 512], F32) for n in ("raw1", "raw2"))
    W1h, W1l, W2h, W2l = (sb(n, [P, 2, 4, 512], F32R) for n in ("W1h", "W1l", "W2h", "W2l"))
    XE, X2E = (sb(n, [P, 2, ST, D], F32) for n in ("XE", "X2E"))
    XTh, XTl = (sb(n, [P, DC, CAP], F32R) for n in ("XEh", "XEl"))
    HR = sb("HR", [P, QC, CAP], F32)
    Hh, Hl = (sb(n, [P, 2, QC, CAP], F32R) for n in ("Hh", "Hl"))
    B1, B2 = sb("B1", [P, 2, HE // P], F32), sb("B2", [P, 2, D], F32)
    Y = sb("Y", [P, ST, D], F32)
    MR = sb("MR", [NT, P, 2], F32)
    token, near, gate = (sb(n, [P, NT], F32) for n in ("token_e", "near_e", "gate_e"))
    whole = sb("whole_token", [P, NT], I32)
    GI, OI = sb("GI", [P, 2, ST], U32), sb("OI", [P, ST], U32)
    pX = ps("pX", [P, DC, CAP])
    pH = ps("pH", [P, 2, QC, CAP])
    pY = ps("pYE", [P, ST, D])

    w1_landed, w2_landed = ([sem(f"{n}{k}") for k in range(NQ)] for n in ("w1_landed", "w2_landed"))
    b_landed, x_landed, x2_landed = ([sem(f"{n}{k}") for k in range(2)] for n in ("b_landed", "xe_landed", "x2e_landed"))
    map_landed, map_turned, map_step, map_done = (sem(n) for n in ("map_landed", "map_turned", "map_step", "map_done"))
    gi_done, oi_done, scattered = sem("gi_done"), sem("oi_done"), sem("y_scattered")
    passed, sp_passed = sem("passed"), sem("sp_passed")
    w1hi, w1lo, w2hi, w2lo = (sem(n) for n in ("w1hi", "w1lo", "w2hi", "w2lo"))
    xT_done, xhi, xlo = sem("xeT_done"), sem("xehi"), sem("xelo")
    h_done, relu, hhi, hlo = sem("h_done"), sem("relu_done"), sem("hhi"), sem("hlo")
    w2_done, y_step, y_done = sem("w2_done"), sem("y_step"), sem("ye_done")

    w1_v = dram["W1"].rearrange("e (k p) (q h) -> e q p k h", p=P, q=NQ)
    w2_v = dram["W2"].rearrange("e (q k p) d -> e q p k d", p=P, q=NQ)
    map_v = dram["slotmap"][0:SLOTS, :].rearrange("(t p) c -> t p c", p=P)

    def wait(eng, s, value):
        if not isinstance(value, int) or value > 0:
            eng.wait_ge(s, value)

    def quarter(v, e, q):
        return v[e, q] if isinstance(e, int) else v[bass.ds(e, 1), q].rearrange("o p k h -> p (o k) h")

    def columns(v, e, t, n):
        return v[:, ST * e + t:ST * e + t + n] if isinstance(e, int) else v[:, bass.ds(ST * e + t, n)]

    def pairs(eng, body):
        for r in range(2):
            body(r, r, 0, r == 0, False)
        with eng.Fori(1, NE // 2 - 1) as g:
            for r in range(2):
                body(2 * g + r, r, g, False, False)
        for r in range(2):
            body(NE - 2 + r, r, NE // 2 - 1, False, r == 1)

    with nc.Block() as block:
        @block.sync
        def _(sp):
            def load1(e, q):
                wait(sp, w1lo, NQ * (e - 1) + q + 1)
                sp.dma_start(raw1[:, q, :, :], quarter(w1_v, e, q)).then_inc(w1_landed[q], 16)

            def load2(e, q):
                if isinstance(e, int):
                    wait(sp, w2lo, NQ * (e - 1) + q + 1)
                else:
                    wait_apart(sp, w2lo, NQ * (e - 1) + q + 1, sp_passed)
                sp.dma_start(raw2[:, q, :, :], quarter(w2_v, e, q)).then_inc(w2_landed[q], 16)

            def biases(e, r):
                if isinstance(e, int):
                    wait(sp, y_done, e - 1)
                    b1, b2 = dram["b1"][e], dram["b2"][e:e + 1, :]
                else:
                    wait_apart(sp, y_done, e - 1, sp_passed)
                    b1, b2 = dram["b1"][bass.ds(e, 1)].rearrange("o p k -> p (o k)"), dram["b2"][bass.ds(e, 1), :]
                sp.dma_start(B1[:, r, :], b1).then_inc(b_landed[r], 16)
                sp.dma_start(B2[:, r, :], b2.to_broadcast([P, D])).then_inc(b_landed[r], 16)

            def body(e, r, u, first, last):
                for q in range(NQ):
                    if q + 1 < NQ:
                        load1(e, q + 1)
                    elif not last:
                        load1(e + 1, 0)
                    if q == 0:
                        biases(e, r)
                        if first:
                            sp.wait_ge(x_landed[0], 16 * ST)
                    load2(e, q)

            sp.dma_start(MR[:, :, :], map_v).then_inc(map_landed, 16)
            load1(0, 0)
            pairs(sp, body)

        @block.gpsimd
        def _(pool):
            def gather_x3(e, r, u):
                if not (isinstance(u, int) and u == 0):
                    wait_apart(pool, xT_done, e - 1, passed)
                    wait_apart(pool, x2_landed[r], 16 * ST * u, passed)
                pool.tensor_copy(GI[:, r, :], columns(near, e, 0, ST)).then_inc(gi_done, 1)
                wait_apart(pool, gi_done, e + 1, passed)
                for t in range(ST):
                    pool.indirect_dma_start(out=XE[:, r, t, :], out_offset=None, in_=dram["x3"],
                                            in_offset=bass.IndirectOffsetOnAxis(GI[:, r, t:t + 1], 0)).then_inc(x_landed[r], 16)

            def gather_x2(e, r):
                for t in range(ST):
                    pool.indirect_dma_start(out=X2E[:, r, t, :], out_offset=None, in_=dram["x2"],
                                            in_offset=bass.IndirectOffsetOnAxis(GI[:, r, t:t + 1], 0)).then_inc(x2_landed[r], 16)

            def write(e, r):
                if not (isinstance(e, int) and e == 0):
                    wait_apart(pool, scattered, 16 * ST * e, passed)
                wait_apart(pool, y_done, e + 1, passed)
                pool.tensor_copy(OI[:, :], columns(token, e, 0, ST)).then_inc(oi_done, 1)
                wait_apart(pool, oi_done, e + 1, passed)
                for t in range(ST):
                    pool.indirect_dma_start(out=dram["out"], out_offset=bass.IndirectOffsetOnAxis(OI[:, t:t + 1], 0),
                                            in_=Y[:, t, :], in_offset=None, bounds_check=TOK - 1,
                                            oob_is_err=False).then_inc(scattered, 16)

            def body(e, r, u, first, last):
                if not last:
                    gather_x3(e + 1, 1 - r, u + r)
                if not first:
                    write(e - 1, 1 - r)
                if not last:
                    gather_x2(e + 1, 1 - r)

            pool.wait_ge(map_done, 1)
            gather_x3(0, 0, 0)
            gather_x2(0, 0)
            pairs(pool, body)
            write(NE - 1, 1)
            pool.wait_ge(scattered, 16 * ST * NE)

        @block.scalar
        def _(act):
            def w1_hi(e, q):
                act.wait_ge(w1_landed[q], 16 * (e + 1))
                wait(act, h_done, NQ * e + q - 1)
                act.activation(W1h[:, q % 2, :, :], raw1[:, q, :, :], ACT.Copy).then_inc(w1hi, 1)

            def w2_hi(e, q):
                act.wait_ge(w2_landed[q], 16 * (e + 1))
                wait(act, w2_done, NQ * e + q - 1)
                act.activation(W2h[:, q % 2, :, :], raw2[:, q, :, :], ACT.Copy).then_inc(w2hi, 1)

            def x_hi(e):
                act.wait_ge(xT_done, e + 1)
                for b in range(2):
                    act.activation(XTh[:, 2 * b:2 * b + 2, :], pX[:, 2 * b:2 * b + 2, :], ACT.Copy).then_inc(xhi, 1)

            def body(e, r, u, first, last):
                for q in range(NQ):
                    if q + 1 < NQ:
                        w1_hi(e, q + 1)
                    elif not last:
                        w1_hi(e + 1, 0)
                        x_hi(e + 1)
                    act.wait_ge(h_done, NQ * e + q + 1)
                    act.wait_ge(b_landed[r], 32 * u + 32)
                    wait(act, hlo, NQ * e + q)
                    for k in range(QC):
                        act.activation(HR[:, k, :], pH[:, q % 2, k, :], ACT.Relu,
                                       bias=B1[:, r, q * QC + k:q * QC + k + 1]).then_inc(relu, 1)
                    act.wait_ge(relu, QC * (NQ * e + q + 1))
                    wait(act, w2_done, NQ * e + q - 1)
                    act.activation(Hh[:, q % 2, :, :], HR[:, :, :], ACT.Copy).then_inc(hhi, 1)
                    w2_hi(e, q)

            w1_hi(0, 0)
            x_hi(0)
            pairs(act, body)

        @block.vector
        def _(dve):
            def w1_lo(e, q):
                dve.wait_ge(w1hi, NQ * e + q + 1)
                dve.tensor_tensor(W1l[:, q % 2, :, :], raw1[:, q, :, :], W1h[:, q % 2, :, :].bitcast(F32),
                                  ALU.subtract).then_inc(w1lo, 1)

            def x_lo(e):
                for b in range(2):
                    dve.wait_ge(xhi, 2 * e + b + 1)
                    dve.tensor_tensor(XTl[:, 2 * b:2 * b + 2, :], pX[:, 2 * b:2 * b + 2, :],
                                      XTh[:, 2 * b:2 * b + 2, :].bitcast(F32), ALU.subtract).then_inc(xlo, 1)

            def finish(e, r, u):
                dve.wait_ge(w2_done, NQ * e + NQ)
                dve.wait_ge(b_landed[r], 32 * u + 32)
                wait(dve, scattered, 16 * ST * e)
                for t in range(ST):
                    dve.tensor_tensor(Y[:, t, :], pY[:, t, :], B2[:, r, :], ALU.add).then_inc(y_step, 1)
                dve.wait_ge(x2_landed[r], 16 * ST * (u + 1))
                for t in range(ST):
                    dve.wait_ge(y_step, ST * e + t + 1)
                    ins = dve.scalar_tensor_tensor(out=Y[:, t, :], in0=Y[:, t, :], scalar=columns(gate, e, t, 1),
                                                   in1=X2E[:, r, t, :], op0=ALU.mult, op1=ALU.add)
                ins.then_inc(y_done, 1)

            def body(e, r, u, first, last):
                for q in range(NQ):
                    if q + 1 < NQ:
                        w1_lo(e, q + 1)
                    elif not last:
                        w1_lo(e + 1, 0)
                        x_lo(e + 1)
                    dve.wait_ge(hhi, NQ * e + q + 1)
                    dve.tensor_tensor(Hl[:, q % 2, :, :], HR[:, :, :], Hh[:, q % 2, :, :].bitcast(F32),
                                      ALU.subtract).then_inc(hlo, 1)
                    dve.wait_ge(w2hi, NQ * e + q + 1)
                    dve.tensor_tensor(W2l[:, q % 2, :, :], raw2[:, q, :, :], W2h[:, q % 2, :, :].bitcast(F32),
                                      ALU.subtract).then_inc(w2lo, 1)
                    if q == 0 and not first:
                        finish(e - 1, 1 - r, u - 1 + r)

            dve.wait_ge(map_turned, 1)
            dve.tensor_copy(token[:, :], pX[:, 0, 0:NT]).then_inc(map_step, 1)
            dve.wait_ge(map_step, 1)
            dve.tensor_scalar(near[:, :], token[:, :], float(TOK - 1), None, ALU.min).then_inc(map_done, 1)
            dve.tensor_copy(gate[:, :], pX[:, 1, 0:NT]).then_inc(map_step, 1)
            dve.tensor_copy(whole[:, :], token[:, :]).then_inc(map_step, 1)
            w1_lo(0, 0)
            x_lo(0)
            pairs(dve, body)
            finish(NE - 1, 1, NE // 2 - 1)

        @block.tensor
        def _(pe):
            def transposes(e, r, u):
                pe.wait_ge(x_landed[r], 16 * ST * (u + 1))
                wait(pe, xlo, 2 * e)
                for k in range(DC):
                    for t in range(ST):
                        mm = pe.transpose(pX[:, k, t * P:(t + 1) * P], XE[:, r, t, k * P:(k + 1) * P], ident[:, :])
                mm.then_inc(xT_done, 1)

            def first_product(e, q, tiles):
                pe.wait_ge(w1lo, NQ * e + q + 1)
                if q == 0:
                    pe.wait_ge(xlo, 2 * e + 2)
                wait(pe, relu, QC * (NQ * e + q - 1))
                n = slice(0, tiles * P)
                for m in range(QC):
                    s = slice(m * P, (m + 1) * P)
                    mm = split(pe.matmul, pH[:, q % 2, m, n], [((W1h[:, q % 2, k, s], W1l[:, q % 2, k, s]), (XTh[:, k, n], XTl[:, k, n]))
                                                               for k in range(DC)])
                mm.then_inc(h_done, 1)

            def second_product(e, q, tiles):
                pe.wait_ge(hlo, NQ * e + q + 1)
                pe.wait_ge(w2lo, NQ * e + q + 1)
                if q == 0:
                    wait(pe, y_step, ST * e)
                for t in range(tiles):
                    s = slice(t * P, (t + 1) * P)
                    mm = split(pe.matmul, pY[:, t, :], [((Hh[:, q % 2, k, s], Hl[:, q % 2, k, s]), (W2h[:, q % 2, k, :], W2l[:, q % 2, k, :]))
                                                        for k in range(QC)], start=(q == 0), stop=(q == NQ - 1))
                mm.then_inc(w2_done, 1)

            def middle(e, tiles):
                for q in range(1, NQ):
                    first_product(e, q, tiles)
                    if q + 1 < NQ:
                        second_product(e, q - 1, tiles)

            def by_load(e, work):
                if isinstance(e, int) and e == 0:
                    return work(ST)
                full = pe.value_load(whole[0:1, 1 + ST * e:2 + ST * e] if isinstance(e, int) else
                                     whole[0:1, bass.ds(ST * e + 1, 1)], min_val=0, max_val=2 * TOK)
                with pe.If(full < TOK):
                    work(ST)
                with pe.Else():
                    work(1)

            def body(e, r, u, first, last):
                by_load(e, lambda tiles: first_product(e, 0, tiles))
                if not first:
                    by_load(e - 1, lambda tiles: second_product(e - 1, NQ - 1, tiles))
                by_load(e, lambda tiles: middle(e, tiles))
                if not last:
                    transposes(e + 1, 1 - r, u + r)
                by_load(e, lambda tiles: second_product(e, NQ - 2, tiles))

            pe.wait_ge(map_landed, 16)
            for n in range(2):
                mm = pe.transpose(pX[:, n, 0:NT], MR[:, :, n], ident[0:NT, 0:NT])
            mm.then_inc(map_turned, 1)
            pe.wait_ge(map_step, 3)
            transposes(0, 0, 0)
            pairs(pe, body)
            by_load(NE - 1, lambda tiles: second_product(NE - 1, NQ - 1, tiles))


def build(nc, dram):
    with ExitStack() as top:
        def alloc(stack):
            def sb(name, shape, dt):
                return stack.enter_context(nc.sbuf_tensor(name, shape, dt))

            def ps(name, shape, dt=F32):
                return stack.enter_context(nc.psum_tensor(name, shape, dt))

            def sem(name):
                return stack.enter_context(nc.semaphore(name))
            return sb, ps, sem

        sb, _, sem = alloc(top)
        c = constants(nc, sb, sem)
        with ExitStack() as part:
            sb, ps, sem = alloc(part)
            w = {n: sb(n, [P, k, 2 * HID], F32R) for n, k in (("Wih", DC), ("Wil", DC), ("Wgh", HC), ("Wgl", HC))}
            w["Woh"], w["Wol"] = (sb(n, [P, 1, WS * D], F32R) for n in ("Woh", "Wol"))
            w["Wo"] = sb("Wo_sb", [P, HC - WS, D], F32)
            small = {"fb": sb("fb", [P, HC], F32), "conv_w": sb("conv_w", [P, HC * TAPS], F32),
                     "conv_b": sb("conv_b", [P, HC], F32), "bg": sb("bg", [P, 2 * HC], F32),
                     "hbg": sb("hbg", [P, 2 * HC], F32), "decay": sb("decay", [P, HC], F32),
                     "one_eps": sb("one_eps", [P, 1], F32), "work": sb("work", [P, 5, HC], F32)}
            X, x_landed = sb("X", [P, TT, D], F32), sem("x_landed")
            with ExitStack() as staging:
                prepare(nc, *alloc(staging), w, dram, small, X, x_landed)
            recurrence(nc, sb, ps, sem, c, w, dram, small, X, x_landed)
        with ExitStack() as part:
            attention(nc, *alloc(part), c, dram)
        with ExitStack() as part:
            experts(nc, *alloc(part), c, dram)


SCRATCH = {"x1": [TOK, D], "x2": [TOK, D], "x3": [TOK, D],
           "wk": [P, BATCH, DC, SC], "vw": [BATCH, SCP, D],
           "slotmap": [SLOTS + 1 + TOK, 2]}


def layout(i):
    import numpy as np

    def chunks(a):
        return np.ascontiguousarray(a.reshape(a.shape[0] // P, P, a.shape[1]).transpose(1, 0, 2))

    def columns(a):
        return np.ascontiguousarray(a.reshape(-1, P).T)

    return {
        "x": i["x"].reshape(TOK, D),
        "Wi": chunks(i["L0_attn_Wi"].T), "Wg": chunks(i["L0_attn_Wg"].T), "Wo": chunks(i["L0_attn_Wo"].T),
        "conv_w": np.ascontiguousarray(i["L0_attn_conv_w"].reshape(HC, P, TAPS).transpose(1, 0, 2).reshape(P, HC * TAPS)),
        "conv_b": columns(i["L0_attn_conv_b"]), "bg": columns(i["L0_attn_bg"]), "fb": columns(i["L0_attn_forget_base"]),
        "ctxT": np.ascontiguousarray(i["ctx_768"].reshape(BATCH * NKV, CC, P).transpose(2, 1, 0)),
        "Wk": chunks(i["L0_xattn_Wk"]), "Wv": chunks(i["L0_xattn_Wv"]),
        "WqT": chunks(i["L0_xattn_Wq"].T), "xWo": chunks(i["L0_xattn_Wo"]),
        "bo": i["L0_xattn_bo"].reshape(1, D),
        "Wgate": chunks(i["L0_ffn_Wg"]), "bgate": i["L0_ffn_bg"],
        "W1": i["L0_ffn_W1"], "W2": i["L0_ffn_W2"],
        "b1": np.ascontiguousarray(i["L0_ffn_b1"].reshape(NE, HE // P, P).transpose(0, 2, 1)), "b2": i["L0_ffn_b2"],
    }


def kernel(**inputs):
    import numpy as _np
    import concourse.bacc as _bacc
    from concourse import mybir as _mybir
    from concourse.bass_utils import run_bass_kernel_spmd as _run

    nc = _bacc.Bacc("TRN2", target_bir_lowering=False, num_devices=1)
    arrays, dram = {}, {}
    for name, a in layout({k: _np.asarray(v) for k, v in inputs.items()}).items():
        a = _np.ascontiguousarray(a)
        arrays[f"in_{name}"] = a
        dram[name] = nc.dram_tensor(f"in_{name}", a.shape, _mybir.dt.from_np(a.dtype), kind="ExternalInput").ap()
    for name, shape in SCRATCH.items():
        dram[name] = nc.dram_tensor(name, shape, F32, kind="Internal").ap()
    dram["out"] = nc.dram_tensor("out_dram", (TOK, D), F32, kind="ExternalOutput").ap()
    build(nc, dram)
    r = _run(nc, [arrays], core_ids=[0])
    return r.results[0]["out_dram"].reshape(BATCH, SEQ, D)
```
